# Optimizing a Trainium2 kernel written in Bass

```python
import numpy as np
import jax
import jax.numpy as jnp

def _softmax(x, axis=-1):
    return jax.nn.softmax(x, axis=axis)

def _gelu(x):
    return jax.nn.gelu(x, approximate=True)

def _silu(x):
    return jax.nn.silu(x)

def _sigmoid(x):
    return jax.nn.sigmoid(x)

def _layernorm(x, axis=-1, eps=1e-05):
    m = jnp.mean(x, axis=axis, keepdims=True)
    v = jnp.var(x, axis=axis, keepdims=True)
    return (x - m) / jnp.sqrt(v + eps)

def _scatter_add(tgt, idx, src, axis=0):
    return tgt.at[idx].add(src)

def _segment_sum(src, seg, n):
    return jax.ops.segment_sum(src, seg, n)
kernel_name = 'mk_adj_ffn_d2_adj_r2_c61b6f'

def setup_inputs(seed: int=0):
    np.random.seed(seed)
    _w = jnp.asarray

    def _rec_inputs():
        import jax
        import jax.numpy as jnp
        _gk = jax.random.key(seed)
        x = -0.0002928 + 1 * jax.random.normal(jax.random.fold_in(_gk, 1), (128, 64, 128), jnp.float32)
        _a = jax.random.bernoulli(jax.random.fold_in(_gk, 2), 0.125, (128, 64, 64))
        _a = jnp.logical_or(_a, jnp.swapaxes(_a, -1, -2))
        _a = jnp.logical_or(_a, jnp.eye(64, dtype=bool))
        _af = _a.astype(jnp.float32)
        _af = _af * jax.random.uniform(jax.random.fold_in(_gk, 3), (128, 64, 64), jnp.float32, 0.05, 1)
        adj = _af
        return (x, adj)
    x, adj = _rec_inputs()

    def _L0_gnn_setup():
        import jax, jax.numpy as jnp
        import numpy as np
        B, N, D, H = (8, 1024, 128, 512)
        RMS_EPS = 1e-06

        def _rmsnorm(h, w, eps=RMS_EPS):
            var = jnp.mean(jnp.square(h), axis=-1, keepdims=True)
            return h * jax.lax.rsqrt(var + eps) * w
        key = jax.random.key(seed)
        ks = jax.random.split(key, 5)
        x = jax.random.normal(ks[0], (B, N, D), dtype=jnp.float32)
        adjacency = jax.random.uniform(ks[1], (B, N, N), dtype=jnp.float32)
        epsilon = jnp.zeros((), dtype=jnp.float32)
        W1 = jax.random.normal(ks[2], (D, H), dtype=jnp.float32) * (1.0 / np.sqrt(D))
        b1 = jnp.zeros((H,), dtype=jnp.float32)
        rms_weight = jnp.ones((H,), dtype=jnp.float32)
        W2 = jax.random.normal(ks[3], (H, D), dtype=jnp.float32) * (1.0 / np.sqrt(H))
        b2 = jnp.zeros((D,), dtype=jnp.float32)
        return {'x': x, 'adjacency': adjacency, 'epsilon': epsilon, 'W1': W1, 'b1': b1, 'rms_weight': rms_weight, 'W2': W2, 'b2': b2}
    _L0_gnn_all = _L0_gnn_setup()
    _L0_gnn_in = {k: v for k, v in _L0_gnn_all.items() if k in ('epsilon', 'W1', 'b1', 'rms_weight', 'W2', 'b2')}
    del _L0_gnn_all

    def _L0_ffn_setup():
        import jax, jax.numpy as jnp
        import numpy as np
        C = 128
        HID = 512
        E = 8
        TEMP = 1.0
        key = jax.random.key(seed)
        ks = jax.random.split(key, 7)
        x = jax.random.normal(ks[0], (8, 8192, C), dtype=jnp.float32)
        W1 = jax.random.normal(ks[1], (C, HID), dtype=jnp.float32) * 0.02
        b1 = jnp.zeros((HID,), dtype=jnp.float32)
        Wg = jax.random.normal(ks[2], (HID, E), dtype=jnp.float32) * 0.02
        bg = jnp.zeros((E,), dtype=jnp.float32)
        Wd = jax.random.normal(ks[3], (E, HID, C), dtype=jnp.float32) * 0.02
        bd = jnp.zeros((E, C), dtype=jnp.float32)
        return {'x': x, 'W1': W1, 'b1': b1, 'Wg': Wg, 'bg': bg, 'Wd': Wd, 'bd': bd}
    _L0_ffn_all = _L0_ffn_setup()
    _L0_ffn_in = {k: v for k, v in _L0_ffn_all.items() if k in ('W1', 'b1', 'Wg', 'bg', 'Wd', 'bd')}
    del _L0_ffn_all

    def _L1_gnn_setup():
        import jax, jax.numpy as jnp
        import numpy as np
        key = jax.random.key(seed)
        k1, k2, k3, k4 = jax.random.split(key, 4)
        B, N, d_in, d_out = (8, 1024, 128, 128)
        x = jax.random.normal(k1, (B, N, d_in), dtype=jnp.float32)
        adj_hat = jax.random.uniform(k2, (B, N, N), dtype=jnp.float32)
        W = jax.random.normal(k3, (d_out, d_in), dtype=jnp.float32) * (1.0 / np.sqrt(d_in))
        b = jax.random.normal(k4, (d_out,), dtype=jnp.float32) * 0.01
        return {'x': x, 'adj_hat': adj_hat, 'W': W, 'b': b}
    _L1_gnn_all = _L1_gnn_setup()
    _L1_gnn_in = {k: v for k, v in _L1_gnn_all.items() if k in ('W', 'b')}
    del _L1_gnn_all

    def _L1_ffn_setup():
        import math
        import jax, jax.numpy as jnp
        import numpy as np
        CAPACITY_FACTOR = 1.25
        TOP_K = 2
        LN_EPS = 1e-05

        def _layer_norm(x, gamma, beta):
            mu = jnp.mean(x, axis=-1, keepdims=True)
            var = jnp.var(x, axis=-1, keepdims=True)
            return (x - mu) * jax.lax.rsqrt(var + LN_EPS) * gamma + beta
        key = jax.random.key(seed)
        ks = jax.random.split(key, 4)
        B, S, D, F, E = (8, 2048, 128, 256, 8)
        x = jax.random.normal(ks[0], (B, S, D), dtype=jnp.float32)
        Wr = jax.random.normal(ks[1], (D, E), dtype=jnp.float32) / np.sqrt(D)
        br = jnp.zeros((E,), jnp.float32)
        W1 = jax.random.normal(ks[2], (E, D, F), dtype=jnp.float32) / np.sqrt(D)
        b1 = jnp.zeros((E, F), jnp.float32)
        W2 = jax.random.normal(ks[3], (E, F, D), dtype=jnp.float32) / np.sqrt(F)
        b2 = jnp.zeros((E, D), jnp.float32)
        gamma = jnp.ones((D,), jnp.float32)
        beta = jnp.zeros((D,), jnp.float32)
        return {'x': x, 'Wr': Wr, 'br': br, 'W1': W1, 'b1': b1, 'W2': W2, 'b2': b2, 'gamma': gamma, 'beta': beta}
    _L1_ffn_all = _L1_ffn_setup()
    _L1_ffn_in = {k: v for k, v in _L1_ffn_all.items() if k in ('Wr', 'br', 'W1', 'b1', 'W2', 'b2', 'gamma', 'beta')}
    del _L1_ffn_all
    return {'x': x, 'adj': adj, 'L0_gnn_epsilon': _L0_gnn_in['epsilon'], 'L0_gnn_W1': _L0_gnn_in['W1'], 'L0_gnn_b1': _L0_gnn_in['b1'], 'L0_gnn_rms_weight': _L0_gnn_in['rms_weight'], 'L0_gnn_W2': _L0_gnn_in['W2'], 'L0_gnn_b2': _L0_gnn_in['b2'], 'L0_ffn_W1': _L0_ffn_in['W1'], 'L0_ffn_b1': _L0_ffn_in['b1'], 'L0_ffn_Wg': _L0_ffn_in['Wg'], 'L0_ffn_bg': _L0_ffn_in['bg'], 'L0_ffn_Wd': _L0_ffn_in['Wd'], 'L0_ffn_bd': _L0_ffn_in['bd'], 'L1_gnn_W': _L1_gnn_in['W'], 'L1_gnn_b': _L1_gnn_in['b'], 'L1_ffn_Wr': _L1_ffn_in['Wr'], 'L1_ffn_br': _L1_ffn_in['br'], 'L1_ffn_W1': _L1_ffn_in['W1'], 'L1_ffn_b1': _L1_ffn_in['b1'], 'L1_ffn_W2': _L1_ffn_in['W2'], 'L1_ffn_b2': _L1_ffn_in['b2'], 'L1_ffn_gamma': _L1_ffn_in['gamma'], 'L1_ffn_beta': _L1_ffn_in['beta']}

def reference(x, adj, L0_gnn_epsilon, L0_gnn_W1, L0_gnn_b1, L0_gnn_rms_weight, L0_gnn_W2, L0_gnn_b2, L0_ffn_W1, L0_ffn_b1, L0_ffn_Wg, L0_ffn_bg, L0_ffn_Wd, L0_ffn_bd, L1_gnn_W, L1_gnn_b, L1_ffn_Wr, L1_ffn_br, L1_ffn_W1, L1_ffn_b1, L1_ffn_W2, L1_ffn_b2, L1_ffn_gamma, L1_ffn_beta):
    import jax
    import jax.numpy as jnp

    def _L0_gnn_ref(x, adjacency, epsilon, W1, b1, rms_weight, W2, b2):
        import jax, jax.numpy as jnp
        import numpy as np
        B, N, D, H = (8, 1024, 128, 512)
        RMS_EPS = 1e-06

        def _rmsnorm(h, w, eps=RMS_EPS):
            var = jnp.mean(jnp.square(h), axis=-1, keepdims=True)
            return h * jax.lax.rsqrt(var + eps) * w
        neighbor_sum = jnp.einsum('bnm,bmd->bnd', adjacency, x)
        agg = epsilon * x + neighbor_sum
        h = jnp.einsum('bnd,dh->bnh', agg, W1) + b1
        h = jax.nn.silu(_rmsnorm(h, rms_weight))
        out = jnp.einsum('bnh,hd->bnd', h, W2) + b2
        return out

    def _L0_ffn_ref(x, W1, b1, Wg, bg, Wd, bd):
        import jax, jax.numpy as jnp
        import numpy as np
        C = 128
        HID = 512
        E = 8
        TEMP = 1.0
        orig_shape = x.shape
        xf = x.reshape(-1, orig_shape[-1])
        H = jax.nn.gelu(xf @ W1 + b1, approximate=False)
        probs = jax.nn.softmax((H @ Wg + bg) / TEMP, axis=-1)
        assign = jnp.argmax(probs, axis=-1)
        out = jnp.zeros_like(xf)
        for e in range(Wd.shape[0]):
            y = H @ Wd[e] + bd[e]
            sel = (assign == e)[:, None]
            out = out + jnp.where(sel, probs[:, e:e + 1] * y, 0.0)
        return out.reshape(orig_shape)

    def _L1_gnn_ref(x, adj_hat, W, b):
        import jax, jax.numpy as jnp
        import numpy as np
        N = adj_hat.shape[1]
        diag = jnp.diagonal(adj_hat, axis1=-2, axis2=-1)
        d = adj_hat.sum(axis=-1) - diag
        d_inv_sqrt = jnp.power(d, -0.5)
        dad = d_inv_sqrt[:, :, None] * adj_hat * d_inv_sqrt[:, None, :]
        h = jnp.einsum('bnd,od->bno', x, W) + b
        return jnp.einsum('bnm,bmo->bno', dad, h)

    def _L1_ffn_ref(x, Wr, br, W1, b1, W2, b2, gamma, beta):
        import math
        import jax, jax.numpy as jnp
        import numpy as np
        CAPACITY_FACTOR = 1.25
        TOP_K = 2
        LN_EPS = 1e-05

        def _layer_norm(x, gamma, beta):
            mu = jnp.mean(x, axis=-1, keepdims=True)
            var = jnp.var(x, axis=-1, keepdims=True)
            return (x - mu) * jax.lax.rsqrt(var + LN_EPS) * gamma + beta
        B, S, D = x.shape
        E = Wr.shape[1]
        N = B * S
        K = TOP_K
        logits = jnp.mean(x, axis=1) @ Wr + br
        routing_weights = jax.nn.softmax(logits, axis=-1)
        capacity = float(math.ceil(N * CAPACITY_FACTOR / E))
        expected_loads = routing_weights.sum(axis=0) * (N / B)
        scale = jnp.where(expected_loads > capacity, capacity / expected_loads, 1.0)
        routing_weights = jax.nn.softmax(routing_weights * scale, axis=-1)
        rw_tok = jnp.broadcast_to(routing_weights[:, None, :], (B, S, E)).reshape(N, E)
        top_w, top_i = jax.lax.top_k(rw_tok, K)
        top_w = jax.nn.softmax(top_w, axis=-1)
        xf = x.reshape(N, D)
        h = jax.nn.gelu(jnp.einsum('nd,edf->enf', xf, W1) + b1[:, None, :], approximate=False)
        y = jnp.einsum('enf,efd->end', h, W2) + b2[:, None, :]
        w_dense = jnp.zeros((N, E), x.dtype).at[jnp.arange(N)[:, None], top_i].add(top_w)
        out = jnp.einsum('ne,end->nd', w_dense, y).reshape(B, S, D)
        out = _layer_norm(out + x, gamma, beta)
        return out
    x = x + _L0_gnn_ref(_layernorm(x, axis=-1), adj, L0_gnn_epsilon, L0_gnn_W1, L0_gnn_b1, L0_gnn_rms_weight, L0_gnn_W2, L0_gnn_b2)
    x = x + _L0_ffn_ref(_layernorm(x, axis=-1), L0_ffn_W1, L0_ffn_b1, L0_ffn_Wg, L0_ffn_bg, L0_ffn_Wd, L0_ffn_bd)
    x = x + _L1_gnn_ref(_layernorm(x, axis=-1), adj, L1_gnn_W, L1_gnn_b)
    x = x + _L1_ffn_ref(_layernorm(x, axis=-1), L1_ffn_Wr, L1_ffn_br, L1_ffn_W1, L1_ffn_b1, L1_ffn_W2, L1_ffn_b2, L1_ffn_gamma, L1_ffn_beta)
    return x

_drawn_inputs = setup_inputs


def setup_inputs(seed=0):
    import zlib

    import numpy as np

    out = dict(_drawn_inputs(seed))
    spreads = {'L0_gnn_b1': (0.0, 0.1),
     'L0_gnn_rms_weight': (1.0, 0.2),
     'L0_gnn_b2': (0.0, 0.1),
     'L0_ffn_b1': (0.0, 0.8),
     'L0_ffn_bg': (0.0, 0.1),
     'L0_ffn_bd': (0.0, 0.1),
     'L1_ffn_br': (0.0, 0.1),
     'L1_ffn_b1': (0.0, 0.395),
     'L1_ffn_b2': (0.0, 0.271),
     'L1_ffn_gamma': (1.0, 0.2),
     'L1_ffn_beta': (0.0, 0.1)}
    factors = {'L0_ffn_Wg': 2.912, 'L0_ffn_Wd': 7.783}
    for name, (base, spread) in spreads.items():
        noise = np.random.default_rng([zlib.crc32(name.encode()), seed]).standard_normal(out[name].shape)
        drawn = base * np.exp(spread * noise) if base else spread * noise
        out[name] = jnp.asarray(drawn.astype(out[name].dtype))
    for name, factor in factors.items():
        out[name] = (out[name] * factor).astype(out[name].dtype)
    return out
```

```python
from contextlib import ExitStack

import concourse.bass as bass
from concourse import mybir

F32 = mybir.dt.float32
F16 = mybir.dt.float16
I32 = mybir.dt.int32
U32 = mybir.dt.uint32
ALU = mybir.AluOpType
ACT = mybir.ActivationFunctionType
AX = mybir.AxisListType

P = 128
GRAPHS, NODES, D = 128, 64, 128
HID = 512
EXPERTS = 8
FF = 256
TOKENS = GRAPHS * NODES
TILES = TOKENS // P
PER = 4
GROUPS = TILES // PER
WIDE = PER * P
CH = HID // P
FCH = FF // P
TOPK = 2
LO_ROW = 32
SCALE = 64.0
UNSCALE = 1.0 / SCALE
LN_EPS = 1e-5
RMS_EPS = 1e-6
CAPACITY = float(-(-TOKENS * 5 // (4 * EXPERTS)))


class Group:

    def __init__(self, i, off):
        self.i, self.off = i, off
        self.parity = off % 2
        self.half = i + off // 2
        self.n = i * 2 + off

    def plus(self, k):
        return Group(self.i, self.off + k)

    def live(self):
        return not isinstance(self.n, int) or 0 <= self.n < GROUPS

    def tile(self, t):
        return self.n * PER + t


def behind(g, t, k):
    return g.plus((t - k) // PER), (t - k) % PER


def reached(eng, sem, count):
    if not isinstance(count, int) or count > 0:
        eng.wait_ge(sem, count)


def over_groups(eng, body, lead, tail):
    pairs = (GROUPS - lead - 1) // 2
    for n in range(lead):
        body(Group(0, n))
    with eng.Fori(0, pairs) as i:
        body(Group(i, lead))
        body(Group(i, lead + 1))
    for n in range(lead + 2 * pairs, GROUPS + tail):
        body(Group(0, n))


def build(nc, x_in, adj_in, eps_in, gw1_in, gb1_in, rms_in, gw2_in, gb2_in, fw1_in, fb1_in, wg_in,
          bg_in, wd_in, bd_in, nw_in, nb_in, wr_in, br_in, ew1_in, eb1_in, ew2_in, eb2_in,
          gamma_in, beta_in, out, upto="D"):
    ctx = ExitStack()

    def sb(name, shape, dt=F32):
        return ctx.enter_context(nc.sbuf_tensor(name, shape, dt))

    def sem(name):
        return ctx.enter_context(nc.semaphore(name))

    class Carve:

        def __init__(self, tensor):
            self.tensor, self.at = tensor, 0

        def take(self, *shape, dt=F32):
            n = 1
            for s in shape:
                n *= s
            words = n if dt == F32 else n // 2
            v = self.tensor[:, self.at:self.at + words]
            self.at += words
            if dt == F16:
                v = v.bitcast(F16)
            if len(shape) == 2:
                v = v.rearrange("p (a b) -> p a b", b=shape[1])
            if len(shape) == 3:
                v = v.rearrange("p (a b c) -> p a b c", b=shape[1], c=shape[2])
            return v

    with ctx:
        X = sb("X", [P, TILES, D])
        XN3 = sb("XN3", [P, TILES, D])
        ADJH = sb("ADJH", [P, TILES, P], F16)
        ADJL = sb("ADJL", [P, TILES, P], F16)
        GW1 = [sb(f"GW1{s}", [P, HID], F16) for s in "HL"]
        GW2 = [sb(f"GW2{s}", [P, CH, D], F16) for s in "HL"]
        FW1 = [sb(f"FW1{s}", [P, HID], F16) for s in "HL"]
        WG = [sb(f"WG{s}", [P, CH, EXPERTS], F16) for s in "HL"]
        WD = [sb(f"WD{s}", [P, CH, EXPERTS * D], F16) for s in "HL"]
        NWT = [sb(f"NWT{s}", [P, D], F16) for s in "HL"]
        EXPERT = sb("EXPERT", [P, EXPERTS, 4 * FF], F16)
        W1_AT, W2_AT = (0, FF), (2 * FF, 3 * FF)
        EBIAS = sb("EBIAS", [P, FF + D], F16)
        CHOSEN = sb("CHOSEN", [P, TILES, 2 * TOPK], F16)
        ROWS = dict(gb1=HID, gb2=D, nb=D, bd=EXPERTS * D)
        row_at, n_rows = {}, 0
        for k, n in ROWS.items():
            row_at[k] = n_rows
            n_rows += n
        BROW = sb("BROW", [2, n_rows], F16)

        def brow(k, a, n):
            return BROW[0:2, row_at[k] + a:row_at[k] + a + n]

        IDENT = sb("IDENT", [P, P])
        NOTI = sb("NOTI", [P, P])
        ONES = sb("ONES", [P, P])
        ONE2 = sb("ONE2", [2, P], F16)
        SLOT3 = sb("SLOT3", [P, 2 * TOPK * 4 * FF], F16)
        IDX = sb("IDX", [P, TILES, 2 * TOPK], I32)
        WTOP = sb("WTOP", [P, TILES, 2 * TOPK])
        EPSH = sb("EPSH", [P, P], F16)
        EPSL = sb("EPSL", [P, P], F16)
        EPSC = sb("EPSC", [P, 1])
        NEGH = sb("NEGH", [P, P])
        RMSW = sb("RMSW", [P, HID])
        FB1 = sb("FB1", [P, CH])
        FB1R = sb("FB1R", [CH, P])
        BGB = sb("BGB", [P, EXPERTS])
        RIOTA = sb("RIOTA", [P, EXPERTS])
        DEG = sb("DEG", [P, TILES])
        DIS = sb("DIS", [P, TILES])
        MEANT = sb("MEANT", [P, GRAPHS])
        WR = sb("WR", [P, EXPERTS])
        BR = sb("BR", [P, EXPERTS])
        GAMMA = sb("GAMMA", [P, D])
        BETA = sb("BETA", [P, D])
        WORK = sb("WORK", [P, 11648])
        PS = ctx.enter_context(nc.psum_tensor("PS", [P, 8, 512], F32))

        far = Carve(XN3[:, :, :].rearrange("p a b -> p (a b)"))
        S_WD = far.take(CH, EXPERTS, D)
        S_EW1 = far.take(EXPERTS, FF)
        S_EW2 = far.take(EXPERTS, FF)
        near = Carve(X[:, :, :].rearrange("p a b -> p (a b)")[:, 3 * WIDE:])
        S_GW1 = near.take(HID)
        S_GW2 = near.take(CH, D)
        S_FW1 = near.take(HID)
        S_WG = near.take(CH, EXPERTS)
        S_NW = near.take(D)
        S_ROW = Carve(WORK[:, :]).take(n_rows)[0:2, :]
        rowp = Carve(WORK[:, n_rows:])
        R_HI = rowp.take(n_rows, dt=F16)[0:2, :]
        R_LO = rowp.take(n_rows, dt=F16)[0:2, :]
        EPSI = rowp.take(P)
        S_EB = rowp.take(FF + D)

        a = Carve(WORK[:, 9860:])
        A_ADJ = [a.take(PER, P) for _ in range(2)]
        A_OFF = a.take(PER, P)
        a2 = Carve(WORK[:, 0:9700])
        A_XN = [a2.take(PER, D) for _ in range(2)]
        A_XH = [a2.take(PER, D, dt=F16) for _ in range(2)]
        A_XL = [a2.take(PER, D, dt=F16) for _ in range(2)]
        A_GH = [a2.take(WIDE, dt=F16) for _ in range(2)]
        A_GL = [a2.take(WIDE, dt=F16) for _ in range(2)]
        A_H = [a2.take(HID) for _ in range(4)]
        A_HH = [a2.take(CH, P, dt=F16) for _ in range(2)]
        A_HL = [a2.take(CH, P, dt=F16) for _ in range(2)]
        A_JUNK = [a2.take(HID, dt=F16) for _ in range(2)]
        A_SS = [a2.take(1) for _ in range(2)]
        A_SE = [a2.take(1) for _ in range(2)]
        A_RS = [a2.take(1) for _ in range(2)]
        A_ST = [a2.take(PER, 6) for _ in range(2)]
        A_MV = [a2.take(PER, 2) for _ in range(2)]
        A_VE = [a2.take(PER) for _ in range(2)]
        A_RL = [a2.take(PER) for _ in range(2)]

        b = Carve(WORK[:, :])
        B_H = b.take(CH, WIDE)
        B_HH = [b.take(CH, WIDE, dt=F16) for _ in range(2)]
        B_HL = [b.take(CH, WIDE, dt=F16) for _ in range(2)]
        B_XN = b.take(PER, D)
        B_XH = b.take(WIDE, dt=F16)
        B_XL = b.take(WIDE, dt=F16)
        C_XN = b.take(PER, D)
        C_XH = b.take(WIDE, dt=F16)
        C_XL = b.take(WIDE, dt=F16)
        C_HH = b.take(PER, D, dt=F16)
        C_HL = b.take(PER, D, dt=F16)
        ACC = [b.take(2, D) for _ in range(2)]
        SM = {}
        for k in ("B", "C", "E"):
            SM[k] = dict(st=b.take(PER, 6), mv=b.take(PER, 2), ve=b.take(PER), rs=b.take(PER))
        C_DS = b.take(PER)
        E_XN = b.take(PER, D)
        LG = b.take(PER, EXPERTS)
        LZ = b.take(PER, EXPERTS)
        LT = b.take(PER, EXPERTS)
        LC = b.take(PER, EXPERTS)
        LN_ = b.take(PER, EXPERTS)
        LD = b.take(PER, EXPERTS)
        LR = b.take(PER, EXPERTS)
        LM = b.take(PER, 1)
        LX = b.take(PER, 1)
        LS = b.take(PER, 1)
        LP = b.take(PER, 1)
        GATE = [b.take(PER, EXPERTS) for _ in range(2)]

        r = Carve(WORK[:, :])
        R_L = r.take(EXPERTS); R_Z = r.take(EXPERTS); R_E = r.take(EXPERTS); R_W = r.take(EXPERTS)
        R_C = r.take(EXPERTS); R_S = r.take(EXPERTS); R_W2 = r.take(EXPERTS); R_Z2 = r.take(EXPERTS)
        R_E2 = r.take(EXPERTS); R_V = r.take(EXPERTS); R_M8 = r.take(EXPERTS); R_I8 = r.take(EXPERTS).bitcast(U32)
        R_1 = [r.take(1) for _ in range(8)]
        R_Q = r.take(4)
        R_D = r.take(4, P)
        R_OH = r.take(TOPK, P)

        SLOT = [v.rearrange("p (k w) -> p k w", k=2 * TOPK)
                for v in (WD[0][:].rearrange("p a b -> p (a b)"), WD[1][:].rearrange("p a b -> p (a b)"), WORK[:, 0:2048].bitcast(F16), SLOT3[:])]
        d = Carve(WORK[:, 2048:])
        D_G = [d.take(WIDE) for _ in range(2)]
        D_GH = [d.take(FCH, 2 * TOPK, NODES, dt=F16) for _ in range(4)]
        D_GL = [d.take(FCH, 2 * TOPK, NODES, dt=F16) for _ in range(4)]
        D_YW = [d.take(2, TOPK, NODES) for _ in range(2)]
        D_YS = [d.take(2, NODES) for _ in range(2)]
        D_R = d.take(PER, D)
        D_N = [d.take(PER, D) for _ in range(2)]
        D_XB = [d.take(PER, D) for _ in range(2)]
        D_O = [d.take(PER, D) for _ in range(2)]
        SM["D"] = dict(st=d.take(PER, 6), mv=d.take(PER, 2), ve=d.take(PER), rs=d.take(PER))

        w_near = sem("w_near"); w_far = sem("w_far"); w_small = sem("w_small")
        prep_hi = sem("prep_hi"); prep_done = sem("prep_done"); const_done = sem("const_done")
        pool_step = sem("pool_step"); adj_clear = sem("adj_clear")
        load = [sem("load_even"), sem("load_odd")]
        A = {k: sem("A_" + k) for k in (
            "stats", "mv", "veps", "rstd", "xn", "xn_hi", "xn_lo", "offd", "deg", "dis",
            "adjT", "adj_hi", "adj_lo", "agg", "agg_hi", "agg_lo",
            "h", "sq", "seps", "rs", "norm", "silu", "hT", "hT_hi", "hT_lo", "y", "x1")}
        B = {k: sem("B_" + k) for k in (
            "stats", "mv", "veps", "rstd", "xn", "xT", "xT_hi", "xT_lo", "h", "gelu", "h_hi", "h_lo",
            "logits", "lg", "lmax", "lz", "tanh", "step", "gate", "y", "acc", "comb")}
        C = {k: sem("C_" + k) for k in (
            "stats", "mv", "veps", "rstd", "xn", "xT", "xT_hi", "xT_lo", "h", "disS", "h_hi", "h_lo",
            "y", "x3")}
        E = {k: sem("E_" + k) for k in (
            "stats", "mv", "veps", "rstd", "xn", "xT", "xT_hi", "xT_lo", "kept")}
        R = {k: sem("R_" + k) for k in ("pe", "dve", "z", "exp", "step", "logits", "weights", "loads", "diagonal", "rows", "go")}
        stored = sem("stored")
        fetched = [sem(f"experts_fetched_{t}") for t in range(PER)]
        DD = {k: sem("D_" + k) for k in (
            "h", "gelu", "hi", "lo", "y", "yw", "ys", "yT", "r", "stats", "mv", "veps", "rstd", "norm",
            "xb", "gam", "out")}
        store = [sem("store_even"), sem("store_odd")]

        x_view = x_in.rearrange("(t two) n d -> (two n) t d", two=2)
        adj_view = adj_in.rearrange("(t two) n m -> two n t m", two=2)
        out_view = out.rearrange("(t two) n d -> (two n) t d", two=2)

        block = ctx.enter_context(nc.Block())

        @block.sync
        def _(sp):
            sp.wait_ge(adj_clear, 2)

            def a_load(g):
                reached(sp, load[g.parity], g.half * 48)
                reached(sp, A["adjT"], g.n - 1)
                reached(sp, A["offd"], g.n - 1)
                if isinstance(g.n, int) and g.n >= 2 and g.n < 5:
                    sp.wait_ge(prep_done, 1)
                if not isinstance(g.n, int):
                    pass
                sp.dma_start(X[:, bass.ds(g.n * PER, PER), :], x_view[:, bass.ds(g.n * PER, PER), :]).then_inc(load[g.parity], 16)
                for half in range(2):
                    s = slice(half * NODES, (half + 1) * NODES)
                    sp.dma_start(A_ADJ[g.parity][s, :, s], adj_view[half, :, bass.ds(g.n * PER, PER), :]).then_inc(load[g.parity], 16)

            over_groups(sp, a_load, 3, 0)

            if upto != "D":
                last = dict(A=(A["x1"], GROUPS), B=(B["comb"], TILES), C=(C["x3"], GROUPS), E=(E["xT_lo"], GROUPS))[upto]
                sp.wait_ge(*last)
                sp.dma_start(out_view, X[:, :, :] if upto != "E" else XN3[:, :, :]).then_inc(stored, 16)
                sp.wait_ge(stored, 16)
                return

            sp.wait_ge(R["go"], 1)

            def d_body(g):
                for t in range(PER):
                    if g.live():
                        n = g.tile(t)
                        experts = nc.values_load_multi_w_load_instructions(
                            IDX[0:1, bass.ds(n, 1), :].rearrange("p a b -> p (a b)"), engines=[mybir.EngineType.SP],
                            min_val=0, max_val=EXPERTS - 1, skip_runtime_bounds_check_because="stage R clamps them")[1]
                        reached(sp, DD["y"], n - 3)
                        for k, e in enumerate(experts):
                            sp.dma_start(SLOT[t][:, k], EXPERT[:, bass.ds(e, 1), :].rearrange("p a b -> p (a b)")).then_inc(fetched[t], 16)
                dn = g.plus(-3)
                if dn.live():
                    sp.wait_ge(DD["out"], dn.n + 1)
                    sp.dma_start(out_view[:, bass.ds(dn.n * PER, PER), :], D_O[dn.parity]).then_inc(store[dn.parity], 16)

            over_groups(sp, d_body, 4, 3)
            for j in range(2):
                sp.wait_ge(store[j], GROUPS // 2 * 16)

        @block.gpsimd
        def _(pool):
            for j in range(2):
                nc.gpsimd.memset(A_ADJ[j], 0.0).then_inc(adj_clear, 1)
            nc.gpsimd.memset(S_EB, 0.0).then_inc(adj_clear, 1)
            nc.gpsimd.memset(IDENT[:], 0.0).then_inc(pool_step, 1)
            nc.gpsimd.memset(NOTI[:], 1.0).then_inc(pool_step, 1)
            nc.gpsimd.memset(ONES[:], 1.0)
            nc.gpsimd.memset(ONE2[:], 1.0)
            nc.gpsimd.memset(NEGH[:], -0.5)
            pool.wait_ge(pool_step, 2)
            nc.gpsimd.affine_select(out=IDENT[:], in_=IDENT[:], compare_op=ALU.not_equal, fill=1.0, base=0,
                                    pattern=[[-1, P]], channel_multiplier=1)
            nc.gpsimd.affine_select(out=NOTI[:], in_=NOTI[:], compare_op=ALU.not_equal, fill=0.0, base=0,
                                    pattern=[[-1, P]], channel_multiplier=1)
            nc.gpsimd.iota(RIOTA[:], pattern=[[-1, EXPERTS]], base=EXPERTS, channel_multiplier=0,
                           allow_small_or_imprecise_dtypes=True).then_inc(const_done, 1)
            pool.wait_ge(const_done, 1)

            def power(dst, src, ready, at, s_out, k):
                pool.wait_ge(ready, at)
                nc.gpsimd.tensor_tensor(dst, src, NEGH[:, 0:k], ALU.pow).then_inc(s_out, 1)

            def a_prep(g):
                j = g.parity
                pool.wait_ge(load[j], g.half * 48 + 48)
                reached(pool, A["deg"], g.n)
                nc.gpsimd.tensor_tensor(A_OFF, A_ADJ[j], NOTI[:, :].unsqueeze(1).broadcast_to([P, PER, P]), ALU.mult).then_inc(A["offd"], 1)
                power(A_RL[j], A_VE[j], A["veps"], g.n + 1, A["rstd"], PER)

            def a_deg(g):
                pool.wait_ge(A["deg"], g.n + 1)
                nc.gpsimd.tensor_tensor(DIS[:, bass.ds(g.n * PER, PER)], DEG[:, bass.ds(g.n * PER, PER)], NEGH[:, 0:PER], ALU.pow).then_inc(A["dis"], 1)

            def a_body(g):
                for t in range(PER):
                    if t == 0 and g.plus(1).live():
                        a_prep(g.plus(1))
                    if g.live():
                        n = g.tile(t)
                        power(A_RS[t % 2], A_SE[t % 2], A["seps"], n + 1, A["rs"], 1)
                    if t == 3 and g.plus(1).live():
                        a_deg(g.plus(1))

            a_prep(Group(0, 0))
            a_deg(Group(0, 0))
            over_groups(pool, a_body, 2, 0)
            if upto == "A":
                return

            def ln_power(g, k, sems, j=0):
                power(SM[k]["rs"], SM[k]["ve"], sems["veps"], g.n + 1, sems["rstd"], PER)

            def bc_body(g):
                if g.plus(1).live():
                    ln_power(g.plus(1), "B", B)
                if g.plus(-1).live() and upto != "B":
                    ln_power(g.plus(-1), "C", C)
                if g.plus(-2).live() and upto not in "BC":
                    ln_power(g.plus(-2), "E", E)

            ln_power(Group(0, 0), "B", B)
            over_groups(pool, bc_body, 3, 2)
            if upto != "D":
                return

            pool.wait_ge(R["go"], 1)

            def d_body(g):
                dn = g.plus(-2)
                if dn.live():
                    j = dn.parity
                    reached(pool, DD["out"], dn.n - 1)
                    nc.gpsimd.tensor_tensor(D_XB[j], X[:, bass.ds(dn.n * PER, PER), :],
                                            BETA[:, :].unsqueeze(1).broadcast_to([P, PER, D]), ALU.add).then_inc(DD["xb"], 1)
                    ln_power(dn, "D", DD)
                    pool.wait_ge(DD["norm"], dn.n + 1)
                    nc.gpsimd.tensor_tensor(D_N[j], D_N[j], GAMMA[:, :].unsqueeze(1).broadcast_to([P, PER, D]), ALU.mult).then_inc(DD["gam"], 1)
                    pool.wait_ge(DD["gam"], dn.n + 1)
                    pool.wait_ge(DD["xb"], dn.n + 1)
                    reached(pool, store[j], (dn.half) * 16)
                    nc.gpsimd.tensor_tensor(D_O[j], D_N[j], D_XB[j], ALU.add).then_inc(DD["out"], 1)

            over_groups(pool, d_body, 4, 2)

        @block.scalar
        def _(act):
            act.dma_start(S_ROW[:, row_at["gb1"]:row_at["gb1"] + HID], gb1_in.partition_broadcast(2)).then_inc(w_small, 16)
            act.dma_start(S_ROW[:, row_at["gb2"]:row_at["gb2"] + D], gb2_in.partition_broadcast(2)).then_inc(w_small, 16)
            act.dma_start(S_ROW[:, row_at["nb"]:row_at["nb"] + D], nb_in.partition_broadcast(2)).then_inc(w_small, 16)
            act.dma_start(S_ROW[:, row_at["bd"]:row_at["bd"] + EXPERTS * D], bd_in.rearrange("e d -> (e d)").partition_broadcast(2)).then_inc(w_small, 16)
            act.dma_start(EPSC[:], eps_in.partition_broadcast(P)).then_inc(w_small, 16)
            act.dma_start(RMSW[:], rms_in.partition_broadcast(P)).then_inc(w_small, 16)
            act.dma_start(FB1R[:], fb1_in.rearrange("(c p) -> c p", p=P)).then_inc(w_small, 16)
            act.dma_start(BGB[:], bg_in.partition_broadcast(P)).then_inc(w_small, 16)
            act.dma_start(BR[:], br_in.partition_broadcast(P)).then_inc(w_small, 16)
            act.dma_start(GAMMA[:], gamma_in.partition_broadcast(P)).then_inc(w_small, 16)
            act.dma_start(BETA[:], beta_in.partition_broadcast(P)).then_inc(w_small, 16)
            act.dma_start(WR[:], wr_in).then_inc(w_small, 16)
            act.dma_start(S_GW1, gw1_in).then_inc(w_near, 16)
            act.dma_start(S_GW2, gw2_in.rearrange("(c p) d -> p c d", p=P)).then_inc(w_near, 16)
            act.dma_start(S_FW1, fw1_in).then_inc(w_near, 16)
            act.dma_start(S_WG, wg_in.rearrange("(c p) e -> p c e", p=P)).then_inc(w_near, 16)
            act.dma_start(S_NW, nw_in).then_inc(w_near, 16)
            for c in range(CH):
                act.dma_start(S_WD[:, c], wd_in.rearrange("e (c p) d -> c p e d", p=P)[c]).then_inc(w_far, 16)
            act.wait_ge(adj_clear, 3)
            for at in (0, LO_ROW):
                act.dma_start(S_EB[at:at + EXPERTS, 0:FF], eb1_in).then_inc(w_far, 16)
                act.dma_start(S_EB[at:at + EXPERTS, FF:FF + D], eb2_in).then_inc(w_far, 16)
            act.dma_start(S_EW1, ew1_in.rearrange("e d f -> d e f")).then_inc(w_far, 16)
            act.dma_start(S_EW2.rearrange("p e (c d) -> p (e c) d", d=D), ew2_in.rearrange("e (c p) d -> p (e c) d", p=P)).then_inc(w_far, 16)
            act.wait_ge(w_small, 12 * 16)
            nc.scalar.activation(R_HI, S_ROW, ACT.Copy, scale=SCALE).then_inc(prep_hi, 1)
            act.wait_ge(w_near, 5 * 16)
            for dst, src in ((GW1[0][:], S_GW1), (GW2[0][:], S_GW2), (FW1[0][:], S_FW1), (WG[0][:], S_WG)):
                nc.scalar.activation(dst, src, ACT.Copy, scale=SCALE).then_inc(prep_hi, 1)
            act.wait_ge(w_far, 10 * 16)
            for dst, src in ((EBIAS[:], S_EB), (WD[0][:].rearrange("p c (e d) -> p c e d", d=D), S_WD),
                             (EXPERT[:, :, W1_AT[0]:W1_AT[0] + FF], S_EW1), (EXPERT[:, :, W2_AT[0]:W2_AT[0] + FF], S_EW2)):
                nc.scalar.activation(dst, src, ACT.Copy, scale=SCALE).then_inc(prep_hi, 1)

            act.wait_ge(prep_done, 2)

            def adj_hi(g):
                act.wait_ge(A["adjT"], g.n + 1)
                nc.scalar.activation(ADJH[:, bass.ds(g.n * PER, PER), :], PS[:, 0, :].rearrange("p (a b) -> p a b", b=P), ACT.Copy).then_inc(A["adj_hi"], 1)

            def xn_hi(g):
                act.wait_ge(A["xn"], g.n + 1)
                reached(act, A["agg"], g.n - 1)
                nc.scalar.activation(A_XH[g.parity], A_XN[g.parity], ACT.Copy).then_inc(A["xn_hi"], 1)

            def agg_hi(g):
                act.wait_ge(A["agg"], g.n + 1)
                reached(act, A["h"], g.tile(-4))
                nc.scalar.activation(A_GH[g.parity], PS[:, 1, :], ACT.Copy).then_inc(A["agg_hi"], 1)

            def a_body(g):
                for t in range(PER):
                    if g.live():
                        n = g.tile(t)
                        act.wait_ge(A["h"], n + 1)
                        reached(act, A["rs"], n - 1)
                        reached(act, A["sq"], n - 1)
                        nc.scalar.activation(A_JUNK[t % 2], PS[:, 2 + t % 2, :], ACT.Square, scale=UNSCALE * HID ** -0.5,
                                             accum_out=A_SS[t % 2]).then_inc(A["sq"], 1)
                    if t == 0 and g.plus(1).live():
                        adj_hi(g.plus(1))
                    g1, t1 = behind(g, t, 1)
                    g2, t2 = behind(g, t, 2)
                    if g2.live():
                        n = g2.tile(t2)
                        act.wait_ge(A["hT"], n + 1)
                        reached(act, A["y"], n - 1)
                        nc.scalar.activation(A_HH[t2 % 2], PS[:, 4 + t2 % 2, :].rearrange("p (a b) -> p a b", b=P), ACT.Copy).then_inc(A["hT_hi"], 1)
                    if t == 1 and g.plus(1).live():
                        xn_hi(g.plus(1))
                    if t == 3 and g.plus(1).live():
                        agg_hi(g.plus(1))
                    if g1.live():
                        n = g1.tile(t1)
                        act.wait_ge(A["norm"], n + 1)
                        nc.scalar.activation(A_H[t1], A_H[t1], ACT.Silu).then_inc(A["silu"], 1)

            adj_hi(Group(0, 0))
            xn_hi(Group(0, 0))
            agg_hi(Group(0, 0))
            over_groups(act, a_body, 2, 1)
            if upto == "A":
                return

            act.wait_ge(A["x1"], GROUPS)

            def b_x_hi(g):
                act.wait_ge(B["xT"], g.n + 1)
                reached(act, B["h"], g.n * CH)
                nc.scalar.activation(B_XH, PS[:, 4, :], ACT.Copy).then_inc(B["xT_hi"], 1)

            def b_gelu(g, c):
                act.wait_ge(B["h"], g.n * CH + c + 1)
                reached(act, B["h_lo"], g.n * CH - CH + c + 1)
                nc.scalar.activation(B_H[:, c], PS[:, 5 + c % 2, :], ACT.Gelu, bias=FB1[:, c:c + 1], scale=UNSCALE).then_inc(B["gelu"], 1)
                act.wait_ge(B["gelu"], g.n * CH + c + 1)
                reached(act, B["y"], g.tile(-PER))
                nc.scalar.activation(B_HH[g.parity][:, c], B_H[:, c], ACT.Copy).then_inc(B["h_hi"], 1)

            def b_tanh(g):
                act.wait_ge(B["lz"], g.n + 1)
                nc.scalar.activation(LT, LZ, ACT.Tanh, scale=0.5).then_inc(B["tanh"], 1)

            def c_x_hi(g):
                act.wait_ge(C["xT"], g.n + 1)
                reached(act, C["h"], g.n)
                nc.scalar.activation(C_XH, PS[:, 4, :], ACT.Copy).then_inc(C["xT_hi"], 1)

            def c_h_hi(g):
                act.wait_ge(C["h"], g.n + 1)
                act.wait_ge(C["disS"], g.n + 1)
                reached(act, C["y"], g.n)
                for t in range(PER):
                    nc.scalar.activation(C_HH[:, t], PS[:, 7, t * D:(t + 1) * D], ACT.Copy, scale=C_DS[:, t:t + 1]).then_inc(C["h_hi"], 1)

            def e_x_hi(g):
                act.wait_ge(E["xn"], g.n + 1)
                nc.scalar.activation(XN3[:, bass.ds(g.n * PER, PER), :], E_XN, ACT.Copy).then_inc(E["kept"], 1)
                act.wait_ge(E["xT"], g.n + 1)
                nc.scalar.activation(ADJH[:, bass.ds(g.n * PER, PER), :], PS[:, 7, :].rearrange("p (a b) -> p a b", b=P), ACT.Copy).then_inc(E["xT_hi"], 1)

            def bc_body(g):
                up, dn, dd = g.plus(1), g.plus(-1), g.plus(-2)
                if dn.live() and upto != "B":
                    pass
                if g.live():
                    b_tanh(g)
                if dd.live() and upto != "B":
                    c_h_hi(dd)
                if up.live():
                    b_x_hi(up)
                    b_gelu(up, 0)
                    b_gelu(up, 1)
                    b_gelu(up, 2)
                    b_gelu(up, 3)
                if dn.live() and upto != "B":
                    c_x_hi(dn)
                if dd.live() and upto not in "BC":
                    e_x_hi(dd)

            b_x_hi(Group(0, 0))
            for c in range(CH):
                b_gelu(Group(0, 0), c)
            over_groups(act, bc_body, 3, 2)
            if upto != "D":
                return

            for n, (dst, src) in enumerate(((R_E, R_Z), (R_E2, R_Z2), (R_1[5], R_1[4]))):
                act.wait_ge(R["z"], n + 1)
                nc.scalar.activation(dst, src, ACT.Exp).then_inc(R["exp"], 1)

            act.wait_ge(R["go"], 1)

            def d_body(g):
                for t in range(PER):
                    if g.live():
                        n = g.tile(t)
                        act.wait_ge(DD["h"], n + 1)
                        reached(act, DD["lo"], n - 1)
                        nc.scalar.activation(D_G[t % 2], PS[:, t % 2, :], ACT.Gelu, scale=UNSCALE).then_inc(DD["gelu"], 1)
                        act.wait_ge(DD["gelu"], n + 1)
                        reached(act, DD["y"], n - 3)
                        nc.scalar.activation(D_GH[t].rearrange("p a b c -> p (a b c)"), D_G[t % 2], ACT.Copy).then_inc(DD["hi"], 1)

            over_groups(act, d_body, 1, 0)

        @block.vector
        def _(dve):
            dve.wait_ge(w_small, 12 * 16)
            dve.wait_ge(const_done, 1)
            dve.wait_ge(prep_hi, 1)
            k = 0
            nc.vector.scalar_tensor_tensor(R_LO, S_ROW, SCALE, R_HI, ALU.mult, ALU.subtract).then_inc(R["dve"], 1)
            nc.vector.tensor_scalar(EPSI, IDENT[:], EPSC[:, 0:1], None, ALU.mult).then_inc(R["dve"], 1)
            nc.vector.tensor_scalar(RMSW[:], RMSW[:], UNSCALE, None, ALU.mult).then_inc(R["dve"], 1)
            dve.wait_ge(R["dve"], 2)
            nc.vector.tensor_scalar(R_HI, R_HI, IDENT[0:2, 0:1], None, ALU.mult).then_inc(R["dve"], 1)
            nc.vector.tensor_copy(EPSH[:], EPSI).then_inc(R["dve"], 1)
            dve.wait_ge(R["dve"], 5)
            nc.vector.scalar_tensor_tensor(BROW[0:2, :], R_LO, IDENT[0:2, 1:2], R_HI, ALU.mult, ALU.add)
            nc.vector.tensor_tensor(EPSL[:], EPSI, EPSH[:], ALU.subtract).then_inc(R["dve"], 1)
            for n, (dst, src) in enumerate(((GW1, S_GW1), (GW2, S_GW2), (FW1, S_FW1), (WG, S_WG))):
                dve.wait_ge(prep_hi, n + 2)
                nc.vector.scalar_tensor_tensor(dst[1][:], src, SCALE, dst[0][:], ALU.mult, ALU.subtract).then_inc(R["dve"], 1)
            dve.wait_ge(R["pe"], 1)
            nc.vector.tensor_copy(FB1[:], PS[:, 6, 0:CH])
            nc.vector.tensor_scalar(NWT[0][:], PS[:, 7, 0:D], SCALE, None, ALU.mult).then_inc(R["dve"], 1)
            dve.wait_ge(R["dve"], 11)
            nc.vector.scalar_tensor_tensor(NWT[1][:], PS[:, 7, 0:D], SCALE, NWT[0][:], ALU.mult, ALU.subtract).then_inc(prep_done, 1)
            dve.wait_ge(prep_hi, 6)
            nc.vector.scalar_tensor_tensor(EBIAS[LO_ROW:LO_ROW + EXPERTS, :], S_EB[LO_ROW:LO_ROW + EXPERTS, :], SCALE, EBIAS[LO_ROW:LO_ROW + EXPERTS, :],
                                           ALU.mult, ALU.subtract)
            dve.wait_ge(prep_hi, 7)
            for c in range(CH):
                nc.vector.scalar_tensor_tensor(WD[1][:, c].rearrange("p (e d) -> p e d", d=D), S_WD[:, c], SCALE,
                                               WD[0][:, c].rearrange("p (e d) -> p e d", d=D), ALU.mult, ALU.subtract)
            for n, (at, src) in enumerate(((W1_AT, S_EW1), (W2_AT, S_EW2))):
                dve.wait_ge(prep_hi, n + 8)
                last = nc.vector.scalar_tensor_tensor(EXPERT[:, :, at[1]:at[1] + FF], src, SCALE, EXPERT[:, :, at[0]:at[0] + FF], ALU.mult, ALU.subtract)
            last.then_inc(prep_done, 1)

            def statistics(tiles, st, mv, ve, s_stats, s_mv, s_ve, at):
                for t in range(PER):
                    last = nc.vector.bn_stats(st[:, t], tiles(t))
                last.then_inc(s_stats, 1)
                dve.drain()
                for t in range(PER):
                    last = nc.vector.bn_aggr(mv[:, t], st[:, t])
                last.then_inc(s_mv, 1)
                dve.wait_ge(s_mv, at)
                nc.vector.tensor_scalar(ve, mv[:, :, 1], LN_EPS, None, ALU.add).then_inc(s_ve, 1)

            def normalise(dst, tiles, mv, rs, s_out):
                for t in range(PER):
                    last = nc.vector.tensor_scalar(dst(t), tiles(t), mv[:, t, 0:1], rs[:, t:t + 1], ALU.subtract, ALU.mult)
                last.then_inc(s_out, 1)

            def x_tile(g):
                return lambda t: X[:, bass.ds(g.n * PER + t, 1), :].rearrange("p a b -> p (a b)")

            def a_stats(g):
                dve.wait_ge(load[g.parity], g.half * 48 + 48)
                statistics(x_tile(g), A_ST[g.parity], A_MV[g.parity], A_VE[g.parity], A["stats"], A["mv"], A["veps"], g.n + 1)

            def a_xn(g):
                j = g.parity
                dve.wait_ge(A["rstd"], g.n + 1)
                reached(dve, A["xn_hi"], g.n - 1)
                normalise(lambda t: A_XN[j][:, t], x_tile(g), A_MV[j], A_RL[j], A["xn"])

            def a_xlo(g):
                j = g.parity
                dve.wait_ge(A["xn_hi"], g.n + 1)
                dve.wait_ge(A["xn"], g.n + 1)
                reached(dve, A["agg"], g.n - 1)
                nc.vector.tensor_tensor(A_XL[j], A_XN[j], A_XH[j], ALU.subtract).then_inc(A["xn_lo"], 1)

            def a_deg(g):
                dve.wait_ge(A["offd"], g.n + 1)
                nc.vector.tensor_reduce(DEG[:, bass.ds(g.n * PER, PER)], A_OFF, AX.X, ALU.add).then_inc(A["deg"], 1)

            def a_adjlo(g):
                dve.wait_ge(A["adj_hi"], g.n + 1)
                s = bass.ds(g.n * PER, PER)
                nc.vector.tensor_tensor(ADJL[:, s, :], PS[:, 0, :].rearrange("p (a b) -> p a b", b=P), ADJH[:, s, :], ALU.subtract).then_inc(A["adj_lo"], 1)

            def a_agglo(g):
                dve.wait_ge(A["agg_hi"], g.n + 1)
                reached(dve, A["h"], g.tile(-4))
                nc.vector.tensor_tensor(A_GL[g.parity], PS[:, 1, :], A_GH[g.parity], ALU.subtract).then_inc(A["agg_lo"], 1)

            def a_body(g):
                up = g.plus(1)
                for t in range(PER):
                    g1, t1 = behind(g, t, 1)
                    g2, t2 = behind(g, t, 2)
                    if t == 0 and up.live():
                        a_stats(up)
                    if g1.live():
                        n = g1.tile(t1)
                        dve.wait_ge(A["rs"], n + 1)
                        reached(dve, A["hT"], n - 3)
                        nc.vector.scalar_tensor_tensor(A_H[t1], PS[:, 2 + t1 % 2, :], A_RS[t1 % 2][:, 0:1], RMSW[:],
                                                       ALU.mult, ALU.mult).then_inc(A["norm"], 1)
                    if t == 1 and up.live():
                        a_xn(up)
                        a_adjlo(up)
                    if g2.live():
                        n = g2.tile(t2)
                        dve.wait_ge(A["hT_hi"], n + 1)
                        reached(dve, A["y"], n - 1)
                        nc.vector.tensor_tensor(A_HL[t2 % 2], PS[:, 4 + t2 % 2, :].rearrange("p (a b) -> p a b", b=P), A_HH[t2 % 2], ALU.subtract).then_inc(A["hT_lo"], 1)
                    if t == 1 and up.live():
                        a_xlo(up)
                        a_deg(up)
                    if t == 3 and up.live():
                        a_agglo(up)
                    if t == 3 and g.plus(-1).live():
                        a_out(g.plus(-1))
                    if g.live():
                        dve.wait_ge(A["sq"], g.tile(t) + 1)
                        nc.vector.tensor_scalar(A_SE[t % 2], A_SS[t % 2], RMS_EPS, None, ALU.add).then_inc(A["seps"], 1)

            def a_out(g):
                dve.wait_ge(A["y"], g.tile(PER))
                s = bass.ds(g.n * PER, PER)
                nc.vector.scalar_tensor_tensor(X[:, s, :], PS[:, 6 + g.parity, :].rearrange("p (a b) -> p a b", b=D), UNSCALE, X[:, s, :],
                                               ALU.mult, ALU.add).then_inc(A["x1"], 1)

            g0 = Group(0, 0)
            a_stats(g0)
            a_adjlo(g0)
            a_deg(g0)
            a_xn(g0)
            a_xlo(g0)
            a_agglo(g0)
            over_groups(dve, a_body, 2, 1)
            if upto == "A":
                return

            def ln_stats(g, k, sems):
                statistics(x_tile(g), SM[k]["st"], SM[k]["mv"], SM[k]["ve"], sems["stats"], sems["mv"], sems["veps"], g.n + 1)

            def b_xn(g):
                dve.wait_ge(B["rstd"], g.n + 1)
                reached(dve, B["xT"], g.n)
                normalise(lambda t: B_XN[:, t], x_tile(g), SM["B"]["mv"], SM["B"]["rs"], B["xn"])

            def b_xlo(g):
                dve.wait_ge(B["xT_hi"], g.n + 1)
                reached(dve, B["h"], g.n * CH)
                nc.vector.tensor_tensor(B_XL, PS[:, 4, :], B_XH, ALU.subtract).then_inc(B["xT_lo"], 1)

            def b_hlo(g, c):
                dve.wait_ge(B["h_hi"], g.n * CH + c + 1)
                nc.vector.tensor_tensor(B_HL[g.parity][:, c], B_H[:, c], B_HH[g.parity][:, c], ALU.subtract).then_inc(B["h_lo"], 1)

            def b_gate(g):
                step = [0]
                STEPS = 9

                def done(ins):
                    step[0] += 1
                    ins.then_inc(B["step"], 1)
                    dve.wait_ge(B["step"], g.n * STEPS + step[0])

                wide = [P, PER, EXPERTS]
                dve.wait_ge(B["logits"], g.n + 1)
                nc.vector.scalar_tensor_tensor(LG, PS[:, 4, 0:PER * EXPERTS].rearrange("p (a b) -> p a b", b=EXPERTS), UNSCALE,
                                               BGB[:, :].unsqueeze(1).broadcast_to(wide), ALU.mult, ALU.add).then_inc(B["lg"], 1)
                dve.wait_ge(B["lg"], g.n + 1)
                done(nc.vector.tensor_reduce(LM[:, :, 0], LG, AX.X, ALU.max))
                nc.vector.tensor_tensor(LZ, LG, LM.broadcast_to(wide), ALU.subtract).then_inc(B["lz"], 1)
                dve.wait_ge(B["lz"], g.n + 1)
                done(nc.vector.scalar_tensor_tensor(LC, LZ, 0.0, RIOTA[:, :].unsqueeze(1).broadcast_to(wide), ALU.is_ge, ALU.mult))
                done(nc.vector.tensor_reduce(LX[:, :, 0], LC, AX.X, ALU.max))
                done(nc.vector.tensor_tensor(LC, LC, LX.broadcast_to(wide), ALU.is_equal))
                dve.wait_ge(B["tanh"], g.n + 1)
                nc.vector.tensor_scalar(LN_, LT, 1.0, None, ALU.add)
                done(nc.vector.tensor_scalar(LD, LT, -1.0, 1.0, ALU.mult, ALU.add))
                done(nc.vector.reciprocal(LR, LD))
                done(nc.vector.tensor_tensor(LR, LR, LN_, ALU.mult))
                done(nc.vector.tensor_reduce(LS[:, :, 0], LR, AX.X, ALU.add))
                done(nc.vector.reciprocal(LP, LS))
                nc.vector.scalar_tensor_tensor(GATE[g.parity], LC, UNSCALE, LP.broadcast_to(wide), ALU.mult, ALU.mult).then_inc(B["gate"], 1)
                assert step[0] == STEPS

            def b_combine(g, t):
                n = g.tile(t)
                dve.wait_ge(B["y"], n + 1)
                dve.wait_ge(B["gate"], g.n + 1)
                prev = x_tile(g)(t)
                for e in range(EXPERTS):
                    dst = x_tile(g)(t) if e == EXPERTS - 1 else ACC[t % 2][:, e % 2]
                    ins = nc.vector.scalar_tensor_tensor(dst, PS[:, 2 * (t % 2) + e // 4, (e % 4) * D:(e % 4 + 1) * D],
                                                         GATE[g.parity][:, t, e:e + 1], prev, ALU.mult, ALU.add)
                    prev = dst
                    if e < EXPERTS - 1:
                        ins.then_inc(B["acc"], 1)
                        dve.wait_ge(B["acc"], n * (EXPERTS - 1) + e + 1)
                    else:
                        ins.then_inc(B["comb"], 1)

            def c_xn(g):
                dve.wait_ge(C["rstd"], g.n + 1)
                reached(dve, C["xT"], g.n)
                if upto not in "BC":
                    reached(dve, E["xT"], g.n - 1)
                normalise(lambda t: C_XN[:, t], x_tile(g), SM["C"]["mv"], SM["C"]["rs"], C["xn"])

            def c_xlo(g):
                dve.wait_ge(C["xT_hi"], g.n + 1)
                reached(dve, C["h"], g.n)
                nc.vector.tensor_tensor(C_XL, PS[:, 4, :], C_XH, ALU.subtract).then_inc(C["xT_lo"], 1)

            def c_scale(g):
                dve.wait_ge(A["dis"], GROUPS)
                reached(dve, C["h_hi"], g.n * PER)
                reached(dve, C["h_lo"], g.n)
                nc.vector.tensor_scalar(C_DS, DIS[:, bass.ds(g.n * PER, PER)], UNSCALE, None, ALU.mult).then_inc(C["disS"], 1)

            def c_hlo(g):
                dve.wait_ge(C["h_hi"], g.n * PER + PER)
                dve.wait_ge(C["disS"], g.n + 1)
                reached(dve, C["y"], g.n)
                for t in range(PER):
                    last = nc.vector.scalar_tensor_tensor(C_HL[:, t], PS[:, 7, t * D:(t + 1) * D], C_DS[:, t:t + 1], C_HH[:, t], ALU.mult, ALU.subtract)
                last.then_inc(C["h_lo"], 1)

            def c_out(g):
                dve.wait_ge(C["y"], g.n + 1)
                for t in range(PER):
                    xt = x_tile(g)(t)
                    last = nc.vector.scalar_tensor_tensor(xt, PS[:, 7, t * D:(t + 1) * D], DIS[:, bass.ds(g.n * PER + t, 1)], xt, ALU.mult, ALU.add)
                last.then_inc(C["x3"], 1)

            def e_xn(g):
                dve.wait_ge(E["rstd"], g.n + 1)
                reached(dve, E["xT"], g.n)
                reached(dve, E["kept"], g.n)
                normalise(lambda t: E_XN[:, t], x_tile(g), SM["E"]["mv"], SM["E"]["rs"], E["xn"])

            def e_xlo(g):
                dve.wait_ge(E["xT_hi"], g.n + 1)
                s = bass.ds(g.n * PER, PER)
                nc.vector.tensor_tensor(ADJL[:, s, :], PS[:, 7, :].rearrange("p (a b) -> p a b", b=P), ADJH[:, s, :], ALU.subtract)
                nc.vector.tensor_reduce(MEANT[:, bass.ds(g.n * 2 * PER, 2 * PER)], PS[:, 7, :].rearrange("p (a b) -> p a b", b=NODES), AX.X, ALU.add).then_inc(E["xT_lo"], 1)

            def bc_body(g):
                up, dn, dd = g.plus(1), g.plus(-1), g.plus(-2)
                full = upto not in "B"
                tail = upto not in "BC"
                if up.live():
                    ln_stats(up, "B", B)
                if dn.live():
                    b_combine(dn, 3)
                if g.live():
                    b_gate(g)
                if up.live():
                    b_xn(up)
                if dd.live() and full:
                    c_hlo(dd)
                if g.live():
                    b_combine(g, 0)
                if up.live():
                    b_xlo(up)
                if dn.live() and full:
                    dve.wait_ge(B["comb"], dn.tile(PER))
                    c_scale(dn)
                    ln_stats(dn, "C", C)
                if dd.live() and full:
                    c_out(dd)
                if dd.live() and tail:
                    dve.drain()
                    ln_stats(dd, "E", E)
                if g.live():
                    b_combine(g, 1)
                if dn.live() and full:
                    c_xn(dn)
                if up.live():
                    b_hlo(up, 0)
                    b_hlo(up, 1)
                if dd.live() and tail:
                    e_xn(dd)
                if g.live():
                    b_combine(g, 2)
                if up.live():
                    b_hlo(up, 2)
                    b_hlo(up, 3)
                if dn.live() and full:
                    c_xlo(dn)
                if dd.live() and tail:
                    e_xlo(dd)

            ln_stats(g0, "B", B)
            b_xn(g0)
            b_xlo(g0)
            for c in range(CH):
                b_hlo(g0, c)
            over_groups(dve, bc_body, 3, 2)
            if upto != "D":
                return

            made = [0]

            def then(ins):
                made[0] += 1
                ins.then_inc(R["step"], 1)
                dve.wait_ge(R["step"], made[0])

            def softmax(src, z, e, out, n, one):
                then(nc.vector.tensor_reduce(one[0], src, AX.X, ALU.max))
                nc.vector.tensor_scalar(z, src, one[0], None, ALU.subtract).then_inc(R["z"], 1)
                dve.wait_ge(R["exp"], n)
                then(nc.vector.tensor_reduce(one[1], e, AX.X, ALU.add))
                then(nc.vector.reciprocal(one[2], one[1]))
                then(nc.vector.tensor_scalar(out, e, one[2], None, ALU.mult))

            nc.vector.memset(R_OH, 0.0)
            dve.wait_ge(R["logits"], 1)
            then(nc.vector.scalar_tensor_tensor(R_L, PS[:, 0, 0:EXPERTS], 1.0 / NODES, BR[:], ALU.mult, ALU.add))
            softmax(R_L, R_Z, R_E, R_W, 1, (R_1[0], R_1[1], R_1[2]))
            nc.vector.tensor_copy(R_W2, R_W).then_inc(R["weights"], 1)
            dve.wait_ge(R["loads"], 1)
            then(nc.vector.tensor_scalar(R_C, PS[:, 1, 0:EXPERTS], float(TOKENS // GRAPHS), None, ALU.mult))
            then(nc.vector.reciprocal(R_S, R_C))
            then(nc.vector.tensor_scalar(R_S, R_S, CAPACITY, 1.0, ALU.mult, ALU.min))
            then(nc.vector.tensor_tensor(R_W2, R_W, R_S, ALU.mult))
            softmax(R_W2, R_Z2, R_E2, R_V, 2, (R_1[0], R_1[1], R_1[2]))
            then(nc.vector.max(R_M8, R_V))
            then(nc.vector.max_index(R_I8, R_M8, R_V))
            nc.vector.tensor_tensor(R_1[4], R_M8[:, 1:2], R_M8[:, 0:1], ALU.subtract).then_inc(R["z"], 1)
            dve.wait_ge(R["exp"], 3)
            then(nc.vector.tensor_scalar(R_1[3], R_1[5], 1.0, None, ALU.add))
            then(nc.vector.reciprocal(R_1[6], R_1[3]))
            then(nc.vector.tensor_tensor(R_1[7], R_1[5], R_1[6], ALU.mult))
            nc.vector.tensor_copy(R_Q[:, 0:2], R_I8[:, 0:2])
            nc.vector.tensor_scalar(R_Q[:, 2:3], R_1[6], UNSCALE, None, ALU.mult)
            then(nc.vector.tensor_scalar(R_Q[:, 3:4], R_1[7], UNSCALE, None, ALU.mult))
            for q in range(TOPK):
                for at in (0, LO_ROW):
                    nc.vector.tensor_scalar(R_OH[:, q, at:at + EXPERTS], RIOTA[:], R_Q[:, q:q + 1], float(EXPERTS), ALU.add, ALU.is_equal)
            for q in range(4):
                last = nc.vector.tensor_scalar(R_D[:, q], IDENT[:], R_Q[:, q:q + 1], None, ALU.mult)
            last.then_inc(R["diagonal"], 1)
            dve.wait_ge(R["rows"], 1)
            rows = PS[:, 2, :].rearrange("p (q t b) -> p t b q", q=4, b=2)
            nc.vector.tensor_scalar(IDX[:].rearrange("p t (b q) -> p t b q", q=TOPK), rows[:, :, :, 0:TOPK], 0.0, float(EXPERTS - 1), ALU.max, ALU.min)
            nc.vector.tensor_copy(CHOSEN[:].rearrange("p t (b q) -> p t b q", q=TOPK),
                                  PS[:, 3, 0:TOPK * P].rearrange("p (q t b) -> p t b q", q=TOPK, b=2))
            nc.vector.tensor_copy(WTOP[:].rearrange("p t (b q) -> p t b q", q=TOPK), rows[:, :, :, TOPK:]).then_inc(R["go"], 1)

            dve.wait_ge(R["go"], 1)

            def d_out(g):
                j = g.parity
                dve.wait_ge(DD["yT"], g.tile(PER))
                reached(dve, DD["norm"], g.n)
                s = bass.ds(g.n * PER, PER)
                nc.vector.tensor_tensor(D_R, PS[:, 4 + j, :].rearrange("p (a b) -> p a b", b=D), XN3[:, s, :], ALU.add).then_inc(DD["r"], 1)
                dve.wait_ge(DD["r"], g.n + 1)
                statistics(lambda t: D_R[:, t], SM["D"]["st"], SM["D"]["mv"], SM["D"]["ve"], DD["stats"], DD["mv"], DD["veps"], g.n + 1)

            def d_norm(g):
                j = g.parity
                dve.wait_ge(DD["rstd"], g.n + 1)
                reached(dve, DD["out"], g.n - 1)
                normalise(lambda t: D_N[j][:, t], lambda t: D_R[:, t], SM["D"]["mv"], SM["D"]["rs"], DD["norm"])

            def d_body(g):
                for t in range(PER):
                    g1, t1 = behind(g, t, 1)
                    g3, t3 = behind(g, t, 3)
                    if g1.live():
                        n = g1.tile(t1)
                        dve.wait_ge(DD["hi"], n + 1)
                        reached(dve, DD["y"], n - 3)
                        nc.vector.tensor_tensor(D_GL[t1].rearrange("p a b c -> p (a b c)"), D_G[t1 % 2], D_GH[t1].rearrange("p a b c -> p (a b c)"), ALU.subtract).then_inc(DD["lo"], 1)
                    if g3.live():
                        n = g3.tile(t3)
                        dve.wait_ge(DD["y"], n + 1)
                        w = WTOP[:, bass.ds(n, 1), :].rearrange("p a b -> p (a b)").unsqueeze(2).broadcast_to([P, 2 * TOPK, NODES])
                        nc.vector.tensor_tensor(D_YW[t3 % 2].rearrange("p b e n -> p (b e) n"), PS[:, 2 + t3 % 2, 0:2 * TOPK * NODES].rearrange("p (a n) -> p a n", n=NODES), w, ALU.mult).then_inc(DD["yw"], 1)
                        dve.wait_ge(DD["yw"], n + 1)
                        reached(dve, DD["yT"], n - 1)
                        nc.vector.tensor_tensor(D_YS[t3 % 2], D_YW[t3 % 2][:, :, 0], D_YW[t3 % 2][:, :, 1], ALU.add).then_inc(DD["ys"], 1)
                    if t == 1 and g.plus(-2).live():
                        d_out(g.plus(-2))
                    if t == 3 and g.plus(-2).live():
                        d_norm(g.plus(-2))

            over_groups(dve, d_body, 4, 2)

        @block.tensor
        def _(pe):
            pe.wait_ge(const_done, 1)
            pe.wait_ge(w_near, 5 * 16)
            pe.wait_ge(w_small, 12 * 16)
            nc.tensor.transpose(PS[:, 7, 0:D], S_NW, IDENT[:])
            nc.tensor.transpose(PS[:, 6, 0:CH], FB1R[:], IDENT[0:CH, 0:CH]).then_inc(R["pe"], 1)

            def product(dst, lhs, rhs, start=True, stop=True):
                nc.tensor.matmul(dst, lhs[0], rhs[0], start=start, stop=False)
                nc.tensor.matmul(dst, lhs[0], rhs[1], start=False, stop=False)
                return nc.tensor.matmul(dst, lhs[1], rhs[0], start=False, stop=stop)

            def a_transpose(g):
                pe.wait_ge(load[g.parity], g.half * 48 + 48)
                reached(pe, A["adj_lo"], g.n)
                for t in range(PER):
                    last = nc.tensor.transpose(PS[:, 0, t * P:(t + 1) * P], A_ADJ[g.parity][:, t], IDENT[:])
                last.then_inc(A["adjT"], 1)

            def a_aggregate(g):
                j = g.parity
                pe.wait_ge(A["adj_lo"], g.n + 1)
                pe.wait_ge(A["xn_lo"], g.n + 1)
                reached(pe, A["agg_lo"], g.n)
                for t in range(PER):
                    dst = PS[:, 1, t * P:(t + 1) * P]
                    lhs = (A_XH[j][:, t], A_XL[j][:, t])
                    at = bass.ds(g.n * PER + t, 1)
                    adj = (ADJH[:, at, :].rearrange("p a b -> p (a b)"), ADJL[:, at, :].rearrange("p a b -> p (a b)"))
                    product(dst, lhs, adj, stop=False)
                    last = product(dst, lhs, (EPSH[:], EPSL[:]), start=False)
                last.then_inc(A["agg"], 1)

            def a_body(g):
                up = g.plus(1)
                for t in range(PER):
                    g2, t2 = behind(g, t, 2)
                    g3, t3 = behind(g, t, 3)
                    if g.live():
                        n = g.tile(t)
                        if t == 0:
                            pe.wait_ge(A["agg_lo"], g.n + 1)
                        reached(pe, A["norm"], n - 1)
                        dst = PS[:, 2 + t % 2, :]
                        s = slice(t * P, (t + 1) * P)
                        nc.tensor.matmul(dst, ONE2[:], brow("gb1", 0, HID), start=True, stop=False)
                        product(dst, (A_GH[g.parity][:, s], A_GL[g.parity][:, s]), (GW1[0][:], GW1[1][:]), start=False).then_inc(A["h"], 1)
                    if t == 0 and up.live():
                        a_transpose(up)
                    if g2.live():
                        n = g2.tile(t2)
                        pe.wait_ge(A["silu"], n + 1)
                        reached(pe, A["hT_lo"], n - 1)
                        for c in range(CH):
                            last = nc.tensor.transpose(PS[:, 4 + t2 % 2, c * P:(c + 1) * P], A_H[t2][:, c * P:(c + 1) * P], IDENT[:])
                        last.then_inc(A["hT"], 1)
                    if g3.live():
                        n = g3.tile(t3)
                        pe.wait_ge(A["hT_lo"], n + 1)
                        if t3 == 0:
                            reached(pe, A["x1"], g3.n - 1)
                        dst = PS[:, 6 + g3.parity, t3 * D:(t3 + 1) * D]
                        nc.tensor.matmul(dst, ONE2[:], brow("gb2", 0, D), start=True, stop=False)
                        for c in range(CH):
                            last = product(dst, (A_HH[t3 % 2][:, c], A_HL[t3 % 2][:, c]), (GW2[0][:, c], GW2[1][:, c]), start=False, stop=(c == CH - 1))
                        last.then_inc(A["y"], 1)
                    if t == 2 and up.live():
                        a_aggregate(up)

            g0 = Group(0, 0)
            pe.wait_ge(prep_done, 2)
            a_transpose(g0)
            a_aggregate(g0)
            over_groups(pe, a_body, 2, 1)
            if upto == "A":
                return

            pe.wait_ge(A["x1"], GROUPS)

            def four_transposes(src, ready, at, out_sem):
                pe.wait_ge(ready, at)
                for t in range(PER):
                    last = nc.tensor.transpose(PS[:, 4, t * P:(t + 1) * P], src[:, t], IDENT[:])
                last.then_inc(out_sem, 1)

            def b_hidden(g, c):
                pe.wait_ge(B["xT_lo"], g.n + 1)
                reached(pe, B["gelu"], g.n * CH + c - 1)
                s = slice(c * P, (c + 1) * P)
                product(PS[:, 5 + c % 2, :], (FW1[0][:, s], FW1[1][:, s]), (B_XH, B_XL)).then_inc(B["h"], 1)

            def b_logits(g):
                pe.wait_ge(B["h_lo"], g.n * CH + CH)
                hh, hl = B_HH[g.parity], B_HL[g.parity]
                for t in range(PER):
                    s = slice(t * P, (t + 1) * P)
                    for c in range(CH):
                        last = product(PS[:, 4, t * EXPERTS:(t + 1) * EXPERTS], (hh[:, c, s], hl[:, c, s]), (WG[0][:, c], WG[1][:, c]),
                                       start=(c == 0), stop=(c == CH - 1))
                last.then_inc(B["logits"], 1)

            def b_experts(g, t):
                n = g.tile(t)
                reached(pe, B["comb"], n - 1)
                hh, hl = B_HH[g.parity], B_HL[g.parity]
                s = slice(t * P, (t + 1) * P)
                y = [PS[:, 2 * (t % 2) + k, :] for k in range(2)]
                for k in range(2):
                    nc.tensor.matmul(y[k], ONE2[:], brow("bd", k * 512, 512), start=True, stop=False)
                for c in range(CH):
                    for lhs, w in ((hh, 0), (hh, 1), (hl, 0)):
                        for k in range(2):
                            last = nc.tensor.matmul(y[k], lhs[:, c, s], WD[w][:, c, k * 512:(k + 1) * 512], start=False,
                                                    stop=(c == CH - 1 and lhs is hl))
                last.then_inc(B["y"], 1)

            def c_hidden(g):
                pe.wait_ge(C["xT_lo"], g.n + 1)
                reached(pe, C["x3"], g.n)
                for t in range(PER):
                    s = slice(t * P, (t + 1) * P)
                    dst = PS[:, 7, t * D:(t + 1) * D]
                    nc.tensor.matmul(dst, ONE2[:], brow("nb", 0, D), start=True, stop=False)
                    last = product(dst, (C_XH[:, s], C_XL[:, s]), (NWT[0][:], NWT[1][:]), start=False)
                last.then_inc(C["h"], 1)

            def c_neighbours(g):
                pe.wait_ge(C["h_lo"], g.n + 1)
                for t in range(PER):
                    at = bass.ds(g.n * PER + t, 1)
                    adj = (ADJH[:, at, :].rearrange("p a b -> p (a b)"), ADJL[:, at, :].rearrange("p a b -> p (a b)"))
                    last = product(PS[:, 7, t * D:(t + 1) * D], adj, (C_HH[:, t], C_HL[:, t]))
                last.then_inc(C["y"], 1)

            def bc_body(g):
                up, dn, dd = g.plus(1), g.plus(-1), g.plus(-2)
                full = upto not in "B"
                tail = upto not in "BC"
                if g.live():
                    b_experts(g, 0)
                if dd.live() and full:
                    c_neighbours(dd)
                if up.live():
                    if g.live():
                        pe.wait_ge(B["lg"], g.n + 1)
                    four_transposes(B_XN, B["xn"], up.n + 1, B["xT"])
                if g.live():
                    b_experts(g, 1)
                if up.live():
                    b_hidden(up, 0)
                    b_hidden(up, 1)
                if g.live():
                    b_experts(g, 2)
                if up.live():
                    b_hidden(up, 2)
                    b_hidden(up, 3)
                if g.live() and not up.live():
                    pe.wait_ge(B["lg"], g.n + 1)
                if dn.live() and full:
                    four_transposes(C_XN, C["xn"], dn.n + 1, C["xT"])
                if dd.live() and tail:
                    pe.wait_ge(E["xn"], dd.n + 1)
                    for t in range(PER):
                        last = nc.tensor.transpose(PS[:, 7, t * P:(t + 1) * P], E_XN[:, t], IDENT[:])
                    last.then_inc(E["xT"], 1)
                if g.live():
                    b_experts(g, 3)
                if dn.live() and full:
                    if dd.live() and tail:
                        pe.wait_ge(E["xT_lo"], dd.n + 1)
                    c_hidden(dn)
                if up.live():
                    if dn.live() and full:
                        pe.wait_ge(C["xT_lo"], dn.n + 1)
                    b_logits(up)

            four_transposes(B_XN, B["xn"], 1, B["xT"])
            for c in range(CH):
                b_hidden(g0, c)
            b_logits(g0)
            over_groups(pe, bc_body, 3, 2)
            if upto != "D":
                return

            pe.wait_ge(E["xT_lo"], GROUPS)
            nc.tensor.matmul(PS[:, 0, 0:EXPERTS], MEANT[:], WR[:], start=True, stop=True).then_inc(R["logits"], 1)
            pe.wait_ge(R["weights"], 1)
            nc.tensor.matmul(PS[:, 1, 0:EXPERTS], ONES[:], R_W, start=True, stop=True).then_inc(R["loads"], 1)
            pe.wait_ge(R["diagonal"], 1)
            for q in range(TOPK):
                nc.tensor.transpose(PS[:, 3, q * P:(q + 1) * P], R_OH[:, q], IDENT[:])
            nc.tensor.matmul(PS[:, 2, :], ONES[:], R_D.rearrange("p a b -> p (a b)"), start=True, stop=True).then_inc(R["rows"], 1)

            pe.wait_ge(R["go"], 1)

            def biases(dst, n, at, start=True):
                pick = CHOSEN[:, bass.ds(n, 1), :].rearrange("p a b -> p (a b)").unsqueeze(2).broadcast_to([P, 2 * TOPK, NODES])
                nc.tensor.matmul(dst, EBIAS[:, at:at + P], pick, start=start, stop=False)

            def d_hidden(g, t):
                n = g.tile(t)
                reached(pe, DD["gelu"], n - 1)
                pe.wait_ge(fetched[t], (g.n + 1) * 2 * TOPK * 16)
                at = bass.ds(n, 1)
                for c in range(FCH):
                    biases(PS[:, t % 2, c * 2 * P:(c + 1) * 2 * P], n, c * P, start=(c == 0))
                for k in range(2 * TOPK):
                    graph = slice(k // TOPK * NODES, (k // TOPK + 1) * NODES)
                    x = (ADJH[:, at, graph].rearrange("p a b -> p (a b)"), ADJL[:, at, graph].rearrange("p a b -> p (a b)"))
                    for c in range(FCH):
                        w = [SLOT[t][:, k, i + c * P:i + (c + 1) * P] for i in W1_AT]
                        last = product(PS[:, t % 2, (c * 2 * TOPK + k) * NODES:(c * 2 * TOPK + k + 1) * NODES], w, x, start=False, stop=(k == 2 * TOPK - 1 and c == FCH - 1))
                last.then_inc(DD["h"], 1)

            def d_out_product(g, t):
                n = g.tile(t)
                pe.wait_ge(DD["lo"], n + 1)
                reached(pe, DD["yw"], n - 1)
                biases(PS[:, 2 + t % 2, 0:2 * P], n, FF)
                for k in range(2 * TOPK):
                    for c in range(FCH):
                        w = [SLOT[t][:, k, i + c * D:i + (c + 1) * D] for i in W2_AT]
                        last = product(PS[:, 2 + t % 2, k * NODES:(k + 1) * NODES], w, (D_GH[t][:, c, k], D_GL[t][:, c, k]), start=False, stop=(k == 2 * TOPK - 1 and c == FCH - 1))
                last.then_inc(DD["y"], 1)

            def d_body(g):
                for t in range(PER):
                    g2, t2 = behind(g, t, 2)
                    g4, t4 = behind(g, t, 4)
                    if g.live():
                        d_hidden(g, t)
                    if g2.live():
                        d_out_product(g2, t2)
                    if g4.live():
                        n = g4.tile(t4)
                        pe.wait_ge(DD["ys"], n + 1)
                        if t4 == 0:
                            reached(pe, DD["r"], g4.n - 1)
                        nc.tensor.transpose(PS[:, 4 + g4.parity, t4 * D:(t4 + 1) * D], D_YS[t4 % 2].rearrange("p a b -> p (a b)"), IDENT[:]).then_inc(DD["yT"], 1)

            over_groups(pe, d_body, 4, 2)


NAMES = ["x", "adj", "L0_gnn_epsilon", "L0_gnn_W1", "L0_gnn_b1", "L0_gnn_rms_weight", "L0_gnn_W2", "L0_gnn_b2",
         "L0_ffn_W1", "L0_ffn_b1", "L0_ffn_Wg", "L0_ffn_bg", "L0_ffn_Wd", "L0_ffn_bd", "L1_gnn_W", "L1_gnn_b",
         "L1_ffn_Wr", "L1_ffn_br", "L1_ffn_W1", "L1_ffn_b1", "L1_ffn_W2", "L1_ffn_b2", "L1_ffn_gamma", "L1_ffn_beta"]


def kernel(**inputs):
    import numpy as np
    import concourse.bacc as bacc
    from concourse.bass_utils import run_bass_kernel_spmd

    nc = bacc.Bacc("TRN2", target_bir_lowering=False, num_devices=1)
    arrays, args = {}, []
    for name in NAMES:
        a = np.ascontiguousarray(inputs[name])
        arrays[name] = a
        args.append(nc.dram_tensor(name, a.shape, mybir.dt.from_np(a.dtype), kind="ExternalInput").ap())
    out = nc.dram_tensor("out", (GRAPHS, NODES, D), F32, kind="ExternalOutput").ap()
    build(nc, *args, out)
    r = run_bass_kernel_spmd(nc, [arrays], core_ids=[0])
    return r.results[0]["out"]
```

```python
from contextlib import ExitStack

import concourse.bass as bass
from concourse import mybir

F32 = mybir.dt.float32
F16 = mybir.dt.float16
I32 = mybir.dt.int32
U32 = mybir.dt.uint32
ALU = mybir.AluOpType
ACT = mybir.ActivationFunctionType
AX = mybir.AxisListType

P = 128
GRAPHS, NODES, D = 128, 64, 128
HID = 512
EXPERTS = 8
FF = 256
TOKENS = GRAPHS * NODES
TILES = TOKENS // P
PER = 4
GROUPS = TILES // PER
WIDE = PER * P
CH = HID // P
FCH = FF // P
TOPK = 2
LO_ROW = 32
SCALE = 64.0
UNSCALE = 1.0 / SCALE
LN_EPS = 1e-5
RMS_EPS = 1e-6
CAPACITY = float(-(-TOKENS * 5 // (4 * EXPERTS)))


class Group:

    def __init__(self, i, off):
        self.i, self.off = i, off
        self.parity = off % 2
        self.half = i + off // 2
        self.n = i * 2 + off

    def plus(self, k):
        return Group(self.i, self.off + k)

    def live(self):
        return not isinstance(self.n, int) or 0 <= self.n < GROUPS

    def tile(self, t):
        return self.n * PER + t


def behind(g, t, k):
    return g.plus((t - k) // PER), (t - k) % PER


def reached(eng, sem, count):
    if not isinstance(count, int) or count > 0:
        eng.wait_ge(sem, count)


def over_groups(eng, body, lead, tail):
    pairs = (GROUPS - lead - 1) // 2
    for n in range(lead):
        body(Group(0, n))
    with eng.Fori(0, pairs) as i:
        body(Group(i, lead))
        body(Group(i, lead + 1))
    for n in range(lead + 2 * pairs, GROUPS + tail):
        body(Group(0, n))


def build(nc, x_in, adj_in, eps_in, gw1_in, gb1_in, rms_in, gw2_in, gb2_in, fw1_in, fb1_in, wg_in,
          bg_in, wd_in, bd_in, nw_in, nb_in, wr_in, br_in, ew1_in, eb1_in, ew2_in, eb2_in,
          gamma_in, beta_in, out, upto="D"):
    ctx = ExitStack()

    def sb(name, shape, dt=F32):
        return ctx.enter_context(nc.sbuf_tensor(name, shape, dt))

    def sem(name):
        return ctx.enter_context(nc.semaphore(name))

    class Carve:

        def __init__(self, tensor):
            self.tensor, self.at = tensor, 0

        def take(self, *shape, dt=F32):
            n = 1
            for s in shape:
                n *= s
            words = n if dt == F32 else n // 2
            v = self.tensor[:, self.at:self.at + words]
            self.at += words
            if dt == F16:
                v = v.bitcast(F16)
            if len(shape) == 2:
                v = v.rearrange("p (a b) -> p a b", b=shape[1])
            if len(shape) == 3:
                v = v.rearrange("p (a b c) -> p a b c", b=shape[1], c=shape[2])
            return v

    with ctx:
        X = sb("X", [P, TILES, D])
        XN3 = sb("XN3", [P, TILES, D])
        ADJH = sb("ADJH", [P, TILES, P], F16)
        ADJL = sb("ADJL", [P, TILES, P], F16)
        GW1 = [sb(f"GW1{s}", [P, HID], F16) for s in "HL"]
        GW2 = [sb(f"GW2{s}", [P, CH, D], F16) for s in "HL"]
        FW1 = [sb(f"FW1{s}", [P, HID], F16) for s in "HL"]
        WG = [sb(f"WG{s}", [P, CH, EXPERTS], F16) for s in "HL"]
        NWT = [sb(f"NWT{s}", [P, D], F16) for s in "HL"]
        PIECES = GROUPS
        WEXP = sb("WEXP", [P, PIECES, 2 * 512], F16)
        L1_PIECE = CH * EXPERTS * D // 512
        W1_AT, W2_AT = (0, 512), (FF, 512 + FF)
        EBIAS = sb("EBIAS", [P, FF + D], F16)
        CHOSEN = sb("CHOSEN", [P, TILES, 2 * TOPK], F16)
        ROWS = dict(gb1=HID, gb2=D, nb=D, bd=EXPERTS * D)
        row_at, n_rows = {}, 0
        for k, n in ROWS.items():
            row_at[k] = n_rows
            n_rows += n
        BROW = sb("BROW", [2, n_rows], F16)

        def brow(k, a, n):
            return BROW[0:2, row_at[k] + a:row_at[k] + a + n]

        IDENT = sb("IDENT", [P, P])
        NOTI = sb("NOTI", [P, P])
        ONES = sb("ONES", [P, P])
        ONE2 = sb("ONE2", [2, P], F16)
        SLOT3 = sb("SLOT3", [P, 2 * TOPK * 2 * FF])
        IDX = sb("IDX", [P, TILES, 2 * TOPK], I32)
        WTOP = sb("WTOP", [P, TILES, 2 * TOPK])
        EPSH = sb("EPSH", [P, P], F16)
        EPSL = sb("EPSL", [P, P], F16)
        EPSC = sb("EPSC", [P, 1])
        NEGH = sb("NEGH", [P, P])
        RMSW = sb("RMSW", [P, HID])
        FB1 = sb("FB1", [P, CH])
        FB1R = sb("FB1R", [CH, P])
        BGB = sb("BGB", [P, EXPERTS])
        RIOTA = sb("RIOTA", [P, EXPERTS])
        DEG = sb("DEG", [P, TILES])
        DIS = sb("DIS", [P, TILES])
        MEANT = sb("MEANT", [P, GRAPHS])
        WR = sb("WR", [P, EXPERTS])
        BR = sb("BR", [P, EXPERTS])
        GAMMA = sb("GAMMA", [P, D])
        BETA = sb("BETA", [P, D])
        WORK = sb("WORK", [P, 11648])
        PS = ctx.enter_context(nc.psum_tensor("PS", [P, 8, 512], F32))

        S_EXP = XN3[:, :, :].rearrange("p a b -> p (a b)").rearrange("p (j w) -> p j w", w=512)
        near = Carve(X[:, :, :].rearrange("p a b -> p (a b)")[:, 3 * WIDE:])
        S_GW1 = near.take(HID)
        S_GW2 = near.take(CH, D)
        late = Carve(SLOT3[:])
        S_FW1 = late.take(HID)
        S_WG = late.take(CH, EXPERTS)
        S_NW = late.take(D)
        S_EB = late.take(FF + D)
        S_ROW = Carve(WORK[:, :]).take(n_rows)[0:2, :]
        rowp = Carve(WORK[:, n_rows:])
        R_HI = rowp.take(n_rows, dt=F16)[0:2, :]
        R_LO = rowp.take(n_rows, dt=F16)[0:2, :]
        EPSI = rowp.take(P)

        a = Carve(WORK[:, 9860:])
        A_ADJ = [a.take(PER, P) for _ in range(2)]
        A_OFF = a.take(PER, P)
        a2 = Carve(WORK[:, 0:9700])
        A_XN = [a2.take(PER, D) for _ in range(2)]
        A_XH = [a2.take(PER, D, dt=F16) for _ in range(2)]
        A_XL = [a2.take(PER, D, dt=F16) for _ in range(2)]
        A_GH = [a2.take(WIDE, dt=F16) for _ in range(2)]
        A_GL = [a2.take(WIDE, dt=F16) for _ in range(2)]
        A_H = [a2.take(HID) for _ in range(4)]
        A_HH = [a2.take(CH, P, dt=F16) for _ in range(2)]
        A_HL = [a2.take(CH, P, dt=F16) for _ in range(2)]
        A_JUNK = [a2.take(HID, dt=F16) for _ in range(2)]
        A_SS = [a2.take(1) for _ in range(2)]
        A_SE = [a2.take(1) for _ in range(2)]
        A_RS = [a2.take(1) for _ in range(2)]
        A_ST = [a2.take(PER, 6) for _ in range(2)]
        A_MV = [a2.take(PER, 2) for _ in range(2)]
        A_VE = [a2.take(PER) for _ in range(2)]
        A_RL = [a2.take(PER) for _ in range(2)]

        b = Carve(WORK[:, :])
        B_H = b.take(CH, WIDE)
        B_HH = [b.take(CH, WIDE, dt=F16) for _ in range(2)]
        B_HL = [b.take(CH, WIDE, dt=F16) for _ in range(2)]
        B_XN = b.take(PER, D)
        B_XH = b.take(WIDE, dt=F16)
        B_XL = b.take(WIDE, dt=F16)
        C_XN = b.take(PER, D)
        C_XH = b.take(WIDE, dt=F16)
        C_XL = b.take(WIDE, dt=F16)
        C_HH = b.take(PER, D, dt=F16)
        C_HL = b.take(PER, D, dt=F16)
        ACC = [b.take(2, D) for _ in range(2)]
        SM = {}
        for k in ("B", "C", "E"):
            SM[k] = dict(st=b.take(PER, 6), mv=b.take(PER, 2), ve=b.take(PER), rs=b.take(PER))
        C_DS = b.take(PER)
        E_XN = b.take(PER, D)
        LG = b.take(PER, EXPERTS)
        LZ = b.take(PER, EXPERTS)
        LT = b.take(PER, EXPERTS)
        LC = b.take(PER, EXPERTS)
        LN_ = b.take(PER, EXPERTS)
        LD = b.take(PER, EXPERTS)
        LR = b.take(PER, EXPERTS)
        LM = b.take(PER, 1)
        LX = b.take(PER, 1)
        LS = b.take(PER, 1)
        LP = b.take(PER, 1)
        GATE = [b.take(PER, EXPERTS) for _ in range(2)]

        r = Carve(WORK[:, :])
        R_L = r.take(EXPERTS); R_Z = r.take(EXPERTS); R_E = r.take(EXPERTS); R_W = r.take(EXPERTS)
        R_C = r.take(EXPERTS); R_S = r.take(EXPERTS); R_W2 = r.take(EXPERTS); R_Z2 = r.take(EXPERTS)
        R_E2 = r.take(EXPERTS); R_V = r.take(EXPERTS); R_M8 = r.take(EXPERTS); R_I8 = r.take(EXPERTS).bitcast(U32)
        R_1 = [r.take(1) for _ in range(8)]
        R_Q = r.take(4)
        R_D = r.take(4, P)
        R_OH = r.take(TOPK, P)

        SLOT = [v.rearrange("p (k w) -> p k w", k=2 * TOPK)
                for v in (WEXP[:, 0:4].rearrange("p a b -> p (a b)"), WEXP[:, 4:8].rearrange("p a b -> p (a b)"), WORK[:, 0:2048].bitcast(F16), SLOT3[:].bitcast(F16))]
        d = Carve(WORK[:, 2048:])
        D_G = [d.take(WIDE) for _ in range(2)]
        D_GH = [d.take(FCH, 2 * TOPK, NODES, dt=F16) for _ in range(4)]
        D_GL = [d.take(FCH, 2 * TOPK, NODES, dt=F16) for _ in range(4)]
        D_YW = [d.take(2, TOPK, NODES) for _ in range(2)]
        D_YS = [d.take(2, NODES) for _ in range(2)]
        D_R = d.take(PER, D)
        D_N = [d.take(PER, D) for _ in range(2)]
        D_XB = [d.take(PER, D) for _ in range(2)]
        D_O = [d.take(PER, D) for _ in range(2)]
        SM["D"] = dict(st=d.take(PER, 6), mv=d.take(PER, 2), ve=d.take(PER), rs=d.take(PER))

        w_near = sem("w_near"); w_late = sem("w_late"); w_experts = sem("w_experts")
        piece_scaled = sem("piece_scaled"); piece_lo = sem("piece_lo")
        prep_hi = sem("prep_hi"); prep_done = sem("prep_done"); const_done = sem("const_done")
        pool_step = sem("pool_step"); adj_clear = sem("adj_clear")
        load = [sem("load_even"), sem("load_odd")]
        A = {k: sem("A_" + k) for k in (
            "stats", "mv", "veps", "rstd", "xn", "xn_hi", "xn_lo", "offd", "deg", "dis",
            "adjT", "adj_hi", "adj_lo", "agg", "agg_hi", "agg_lo",
            "h", "sq", "seps", "rs", "norm", "silu", "hT", "hT_hi", "hT_lo", "y", "x1")}
        B = {k: sem("B_" + k) for k in (
            "stats", "mv", "veps", "rstd", "xn", "xT", "xT_hi", "xT_lo", "h", "gelu", "h_hi", "h_lo",
            "logits", "lg", "lmax", "lz", "tanh", "step", "gate", "y", "acc", "comb")}
        C = {k: sem("C_" + k) for k in (
            "stats", "mv", "veps", "rstd", "xn", "xT", "xT_hi", "xT_lo", "h", "disS", "h_hi", "h_lo",
            "y", "x3")}
        E = {k: sem("E_" + k) for k in (
            "stats", "mv", "veps", "rstd", "xn", "xT", "xT_hi", "xT_lo", "kept")}
        R = {k: sem("R_" + k) for k in ("pe", "dve", "z", "exp", "step", "logits", "weights", "loads", "diagonal", "rows", "go")}
        stored = sem("stored")
        fetched = [sem(f"experts_fetched_{t}") for t in range(PER)]
        DD = {k: sem("D_" + k) for k in (
            "h", "gelu", "hi", "lo", "y", "yw", "ys", "yT", "r", "stats", "mv", "veps", "rstd", "norm",
            "xb", "gam", "out", "copied")}
        store = [sem("store_even"), sem("store_odd")]

        x_view = x_in.rearrange("(t two) n d -> (two n) t d", two=2)
        adj_view = adj_in.rearrange("(t two) n m -> two n t m", two=2)
        out_view = out.rearrange("(t two) n d -> (two n) t d", two=2)

        FETCHED = 3

        def experts_of(n, kind):
            return nc.values_load_multi_w_load_instructions(
                IDX[0:1, bass.ds(n, 1), :].rearrange("p a b -> p (a b)"), engines=[kind],
                min_val=0, max_val=EXPERTS - 1, skip_runtime_bounds_check_because="stage R clamps them")[1]

        def expert_weights(e):
            return WEXP[:, bass.ds(e + L1_PIECE, 1), :].rearrange("p a b -> p (a b)")

        def fetch_experts(eng, kind, g, t, pairs):
            n = g.tile(t)
            experts = experts_of(n, kind)
            reached(eng, DD["y"], n - 3)
            for k in pairs:
                eng.dma_start(SLOT[t][:, k], expert_weights(experts[k])).then_inc(fetched[t], 16)

        NEAR, LATE, ALL_EXPERTS = 8 * 16, 13 * 16, (CH + 1 + FCH) * 16

        block = ctx.enter_context(nc.Block())

        @block.sync
        def _(sp):
            sp.wait_ge(adj_clear, 2)

            def a_load(g):
                reached(sp, load[g.parity], g.half * 48)
                reached(sp, A["adjT"], g.n - 1)
                reached(sp, A["offd"], g.n - 1)
                if isinstance(g.n, int) and g.n >= 2 and g.n < 5:
                    sp.wait_ge(prep_done, 1)
                if not isinstance(g.n, int):
                    pass
                sp.dma_start(X[:, bass.ds(g.n * PER, PER), :], x_view[:, bass.ds(g.n * PER, PER), :]).then_inc(load[g.parity], 16)
                for half in range(2):
                    s = slice(half * NODES, (half + 1) * NODES)
                    sp.dma_start(A_ADJ[g.parity][s, :, s], adj_view[half, :, bass.ds(g.n * PER, PER), :]).then_inc(load[g.parity], 16)

                if isinstance(g.n, int) and g.n == 2:
                    late_weights()

            def late_weights():
                sp.wait_ge(adj_clear, 3)
                for dst, src in ((S_FW1, fw1_in), (S_WG, wg_in.rearrange("(c p) e -> p c e", p=P)), (S_NW, nw_in),
                                 (FB1R[:], fb1_in.rearrange("(c p) -> c p", p=P)), (BGB[:], bg_in.partition_broadcast(P)),
                                 (BR[:], br_in.partition_broadcast(P)), (GAMMA[:], gamma_in.partition_broadcast(P)),
                                 (BETA[:], beta_in.partition_broadcast(P)), (WR[:], wr_in),
                                 (S_EB[0:EXPERTS, 0:FF], eb1_in), (S_EB[0:EXPERTS, FF:FF + D], eb2_in),
                                 (S_EB[LO_ROW:LO_ROW + EXPERTS, 0:FF], eb1_in), (S_EB[LO_ROW:LO_ROW + EXPERTS, FF:FF + D], eb2_in)):
                    sp.dma_start(dst, src).then_inc(w_late, 16)
                for c in range(CH):
                    sp.dma_start(S_EXP[:, 2 * c:2 * c + 2, :].rearrange("p k (e d) -> p (k e) d", d=D),
                                 wd_in.rearrange("e (c p) d -> c p e d", p=P)[c]).then_inc(w_experts, 16)
                sp.dma_start(S_EXP[:, L1_PIECE:, 0:FF], ew1_in.rearrange("e d f -> d e f")).then_inc(w_experts, 16)
                for c in range(FCH):
                    sp.dma_start(S_EXP[:, L1_PIECE:, FF + c * D:FF + (c + 1) * D],
                                 ew2_in.rearrange("e (c p) d -> c p e d", p=P)[c]).then_inc(w_experts, 16)

            over_groups(sp, a_load, 3, 0)

            if upto != "D":
                last = dict(A=(A["x1"], GROUPS), B=(B["comb"], TILES), C=(C["x3"], GROUPS), E=(E["xT_lo"], GROUPS))[upto]
                sp.wait_ge(*last)
                sp.dma_start(out_view, X[:, :, :] if upto != "E" else XN3[:, :, :]).then_inc(stored, 16)
                sp.wait_ge(stored, 16)
                return

            sp.wait_ge(R["go"], 1)

            def d_body(g):
                for t in range(PER):
                    if g.live():
                        fetch_experts(sp, mybir.EngineType.SP, g, t, (0, 1))
                dn = g.plus(-3)
                if dn.live():
                    sp.wait_ge(DD["out"], dn.n + 1)
                    sp.dma_start(out_view[:, bass.ds(dn.n * PER, PER), :], D_O[dn.parity]).then_inc(store[dn.parity], 16)

            over_groups(sp, d_body, 4, 3)
            for j in range(2):
                sp.wait_ge(store[j], GROUPS // 2 * 16)

        @block.gpsimd
        def _(pool):
            for j in range(2):
                nc.gpsimd.memset(A_ADJ[j], 0.0).then_inc(adj_clear, 1)
            nc.gpsimd.memset(S_EB, 0.0).then_inc(adj_clear, 1)
            nc.gpsimd.memset(IDENT[:], 0.0).then_inc(pool_step, 1)
            nc.gpsimd.memset(NOTI[:], 1.0).then_inc(pool_step, 1)
            nc.gpsimd.memset(ONES[:], 1.0)
            nc.gpsimd.memset(ONE2[:], 1.0)
            nc.gpsimd.memset(NEGH[:], -0.5)
            pool.wait_ge(pool_step, 2)
            nc.gpsimd.affine_select(out=IDENT[:], in_=IDENT[:], compare_op=ALU.not_equal, fill=1.0, base=0,
                                    pattern=[[-1, P]], channel_multiplier=1)
            nc.gpsimd.affine_select(out=NOTI[:], in_=NOTI[:], compare_op=ALU.not_equal, fill=0.0, base=0,
                                    pattern=[[-1, P]], channel_multiplier=1)
            nc.gpsimd.iota(RIOTA[:], pattern=[[-1, EXPERTS]], base=EXPERTS, channel_multiplier=0,
                           allow_small_or_imprecise_dtypes=True).then_inc(const_done, 1)
            pool.wait_ge(const_done, 1)

            def power(dst, src, ready, at, s_out, k):
                pool.wait_ge(ready, at)
                nc.gpsimd.tensor_tensor(dst, src, NEGH[:, 0:k], ALU.pow).then_inc(s_out, 1)

            def a_rstd(g):
                power(A_RL[g.parity], A_VE[g.parity], A["veps"], g.n + 1, A["rstd"], PER)

            def a_offd(g):
                pool.wait_ge(load[g.parity], g.half * 48 + 48)
                reached(pool, A["deg"], g.n)
                nc.gpsimd.tensor_tensor(A_OFF, A_ADJ[g.parity], NOTI[:, :].unsqueeze(1).broadcast_to([P, PER, P]), ALU.mult).then_inc(A["offd"], 1)

            def a_xlo(g):
                j = g.parity
                pool.wait_ge(A["xn_hi"], g.n + 1)
                pool.wait_ge(A["xn"], g.n + 1)
                reached(pool, A["agg"], g.n - 1)
                nc.gpsimd.tensor_tensor(A_XL[j], A_XN[j], A_XH[j], ALU.subtract).then_inc(A["xn_lo"], 1)

            def a_deg(g):
                pool.wait_ge(A["deg"], g.n + 1)
                nc.gpsimd.tensor_tensor(DIS[:, bass.ds(g.n * PER, PER)], DEG[:, bass.ds(g.n * PER, PER)], NEGH[:, 0:PER], ALU.pow).then_inc(A["dis"], 1)

            def a_body(g):
                for t in range(PER):
                    if g.live():
                        n = g.tile(t)
                        power(A_RS[t % 2], A_SE[t % 2], A["seps"], n + 1, A["rs"], 1)
                    if t == 0 and g.plus(1).live():
                        a_xlo(g.plus(1))
                        a_offd(g.plus(1))
                    if t == 2 and g.plus(2).live():
                        a_rstd(g.plus(2))
                    if t == 3 and g.plus(1).live():
                        a_deg(g.plus(1))
                    if t == 1 and g.plus(-1).live():
                        piece_lo_part(g.plus(-1))

            def piece_lo_part(g):
                pool.wait_ge(piece_scaled, g.n + 1)
                nc.gpsimd.tensor_tensor(WEXP[:, bass.ds(g.n, 1), 512:1024], S_EXP[:, bass.ds(g.n, 1), :], WEXP[:, bass.ds(g.n, 1), 0:512],
                                        ALU.subtract).then_inc(piece_lo, 1)

            a_offd(Group(0, 0))
            a_rstd(Group(0, 0))
            a_rstd(Group(0, 1))
            a_xlo(Group(0, 0))
            a_deg(Group(0, 0))
            over_groups(pool, a_body, 2, 1)
            if upto == "A":
                return

            def ln_power(g, k, sems, j=0):
                power(SM[k]["rs"], SM[k]["ve"], sems["veps"], g.n + 1, sems["rstd"], PER)

            def bc_body(g):
                if g.plus(1).live():
                    ln_power(g.plus(1), "B", B)
                if g.plus(-1).live() and upto != "B":
                    ln_power(g.plus(-1), "C", C)
                if g.plus(-2).live() and upto not in "BC":
                    ln_power(g.plus(-2), "E", E)

            ln_power(Group(0, 0), "B", B)
            over_groups(pool, bc_body, 3, 2)
            if upto != "D":
                return

            pool.wait_ge(R["go"], 1)

            def d_lo(g, t):
                n = g.tile(t)
                pool.wait_ge(DD["hi"], n + 1)
                reached(pool, DD["y"], n - 3)
                nc.gpsimd.tensor_tensor(D_GL[t].rearrange("p a b c -> p (a b c)"), D_G[t % 2], D_GH[t].rearrange("p a b c -> p (a b c)"), ALU.subtract).then_inc(DD["lo"], 1)

            def d_beta(g):
                reached(pool, DD["out"], g.n - 1)
                nc.gpsimd.tensor_tensor(D_XB[g.parity], X[:, bass.ds(g.n * PER, PER), :],
                                        BETA[:, :].unsqueeze(1).broadcast_to([P, PER, D]), ALU.add).then_inc(DD["xb"], 1)

            def d_gamma(g):
                j = g.parity
                pool.wait_ge(DD["norm"], g.n + 1)
                nc.gpsimd.tensor_tensor(D_N[j], D_N[j], GAMMA[:, :].unsqueeze(1).broadcast_to([P, PER, D]), ALU.mult).then_inc(DD["gam"], 1)

            def d_sum(g):
                j = g.parity
                pool.wait_ge(DD["gam"], g.n + 1)
                pool.wait_ge(DD["xb"], g.n + 1)
                reached(pool, store[j], g.half * 16)
                nc.gpsimd.tensor_tensor(D_O[j], D_N[j], D_XB[j], ALU.add).then_inc(DD["out"], 1)

            def d_body(g):
                for t in range(PER):
                    g1, t1 = behind(g, t, 1)
                    if g1.live():
                        d_lo(g1, t1)
                    if t == 0 and g.plus(-3).live():
                        d_gamma(g.plus(-3))
                    if t == 1 and g.plus(-3).live():
                        d_sum(g.plus(-3))
                    if t == 2 and g.plus(-2).live():
                        ln_power(g.plus(-2), "D", DD)
                    if t == 3 and g.plus(-2).live():
                        d_beta(g.plus(-2))

            over_groups(pool, d_body, 4, 3)

        @block.scalar
        def _(act):
            act.dma_start(S_GW1, gw1_in).then_inc(w_near, 16)
            act.dma_start(S_GW2, gw2_in.rearrange("(c p) d -> p c d", p=P)).then_inc(w_near, 16)
            for name, src in (("gb1", gb1_in), ("gb2", gb2_in), ("nb", nb_in), ("bd", bd_in.rearrange("e d -> (e d)"))):
                act.dma_start(S_ROW[:, row_at[name]:row_at[name] + ROWS[name]], src.partition_broadcast(2)).then_inc(w_near, 16)
            act.dma_start(EPSC[:], eps_in.partition_broadcast(P)).then_inc(w_near, 16)
            act.dma_start(RMSW[:], rms_in.partition_broadcast(P)).then_inc(w_near, 16)
            act.wait_ge(w_near, NEAR)
            for dst, src in ((R_HI, S_ROW), (GW1[0][:], S_GW1), (GW2[0][:], S_GW2)):
                nc.scalar.activation(dst, src, ACT.Copy, scale=SCALE).then_inc(prep_hi, 1)

            def late_hi():
                act.wait_ge(w_late, LATE)
                for dst, src in ((FW1[0][:], S_FW1), (WG[0][:], S_WG), (EBIAS[:], S_EB)):
                    nc.scalar.activation(dst, src, ACT.Copy, scale=SCALE).then_inc(prep_hi, 1)

            def piece(g):
                act.wait_ge(w_experts, ALL_EXPERTS)
                nc.scalar.activation(WEXP[:, bass.ds(g.n, 1), 0:512], S_EXP[:, bass.ds(g.n, 1), :], ACT.Copy, scale=SCALE)
                nc.scalar.activation(S_EXP[:, bass.ds(g.n, 1), :], S_EXP[:, bass.ds(g.n, 1), :], ACT.Copy, scale=SCALE).then_inc(piece_scaled, 1)

            act.wait_ge(prep_done, 1)

            def adj_hi(g):
                act.wait_ge(A["adjT"], g.n + 1)
                nc.scalar.activation(ADJH[:, bass.ds(g.n * PER, PER), :], PS[:, 0, :].rearrange("p (a b) -> p a b", b=P), ACT.Copy).then_inc(A["adj_hi"], 1)

            def xn_hi(g):
                act.wait_ge(A["xn"], g.n + 1)
                reached(act, A["agg"], g.n - 1)
                nc.scalar.activation(A_XH[g.parity], A_XN[g.parity], ACT.Copy).then_inc(A["xn_hi"], 1)

            def agg_hi(g):
                act.wait_ge(A["agg"], g.n + 1)
                reached(act, A["h"], g.tile(-4))
                nc.scalar.activation(A_GH[g.parity], PS[:, 1, :], ACT.Copy).then_inc(A["agg_hi"], 1)

            def a_body(g):
                for t in range(PER):
                    if g.live():
                        n = g.tile(t)
                        act.wait_ge(A["h"], n + 1)
                        reached(act, A["rs"], n - 1)
                        reached(act, A["sq"], n - 1)
                        nc.scalar.activation(A_JUNK[t % 2], PS[:, 2 + t % 2, :], ACT.Square, scale=UNSCALE * HID ** -0.5,
                                             accum_out=A_SS[t % 2]).then_inc(A["sq"], 1)
                    if t == 0 and g.plus(1).live():
                        adj_hi(g.plus(1))
                    g1, t1 = behind(g, t, 1)
                    g2, t2 = behind(g, t, 2)
                    if g2.live():
                        n = g2.tile(t2)
                        act.wait_ge(A["hT"], n + 1)
                        reached(act, A["y"], n - 1)
                        nc.scalar.activation(A_HH[t2 % 2], PS[:, 4 + t2 % 2, :].rearrange("p (a b) -> p a b", b=P), ACT.Copy).then_inc(A["hT_hi"], 1)
                    if t == 0 and g.plus(1).live():
                        xn_hi(g.plus(1))
                    if g1.live():
                        n = g1.tile(t1)
                        act.wait_ge(A["norm"], n + 1)
                        nc.scalar.activation(A_H[t1], A_H[t1], ACT.Silu).then_inc(A["silu"], 1)
                    if t == 2 and g.plus(1).live():
                        agg_hi(g.plus(1))
                    if t == 1 and g.plus(-1).live():
                        piece(g.plus(-1))
                if isinstance(g.n, int) and g.n == 1:
                    late_hi()

            adj_hi(Group(0, 0))
            xn_hi(Group(0, 0))
            agg_hi(Group(0, 0))
            over_groups(act, a_body, 2, 1)
            if upto == "A":
                return

            act.wait_ge(A["x1"], GROUPS)

            def b_x_hi(g):
                act.wait_ge(B["xT"], g.n + 1)
                reached(act, B["h"], g.n * CH)
                nc.scalar.activation(B_XH, PS[:, 4, :], ACT.Copy).then_inc(B["xT_hi"], 1)

            def b_gelu(g, c):
                act.wait_ge(B["h"], g.n * CH + c + 1)
                reached(act, B["h_lo"], g.n * CH - CH + c + 1)
                nc.scalar.activation(B_H[:, c], PS[:, 5 + c % 2, :], ACT.Gelu, bias=FB1[:, c:c + 1], scale=UNSCALE).then_inc(B["gelu"], 1)
                act.wait_ge(B["gelu"], g.n * CH + c + 1)
                reached(act, B["y"], g.tile(-PER))
                nc.scalar.activation(B_HH[g.parity][:, c], B_H[:, c], ACT.Copy).then_inc(B["h_hi"], 1)

            def b_tanh(g):
                act.wait_ge(B["lz"], g.n + 1)
                nc.scalar.activation(LT, LZ, ACT.Tanh, scale=0.5).then_inc(B["tanh"], 1)

            def c_x_hi(g):
                act.wait_ge(C["xT"], g.n + 1)
                reached(act, C["h"], g.n)
                nc.scalar.activation(C_XH, PS[:, 4, :], ACT.Copy).then_inc(C["xT_hi"], 1)

            def c_h_hi(g):
                act.wait_ge(C["h"], g.n + 1)
                act.wait_ge(C["disS"], g.n + 1)
                reached(act, C["y"], g.n)
                for t in range(PER):
                    nc.scalar.activation(C_HH[:, t], PS[:, 7, t * D:(t + 1) * D], ACT.Copy, scale=C_DS[:, t:t + 1]).then_inc(C["h_hi"], 1)

            def e_x_hi(g):
                act.wait_ge(E["xn"], g.n + 1)
                nc.scalar.activation(XN3[:, bass.ds(g.n * PER, PER), :], E_XN, ACT.Copy).then_inc(E["kept"], 1)
                act.wait_ge(E["xT"], g.n + 1)
                nc.scalar.activation(ADJH[:, bass.ds(g.n * PER, PER), :], PS[:, 7, :].rearrange("p (a b) -> p a b", b=P), ACT.Copy).then_inc(E["xT_hi"], 1)

            def bc_body(g):
                up, dn, dd = g.plus(1), g.plus(-1), g.plus(-2)
                if dn.live() and upto != "B":
                    pass
                if g.live():
                    b_tanh(g)
                if dd.live() and upto != "B":
                    c_h_hi(dd)
                if up.live():
                    b_x_hi(up)
                    b_gelu(up, 0)
                    b_gelu(up, 1)
                    b_gelu(up, 2)
                    b_gelu(up, 3)
                if dn.live() and upto != "B":
                    c_x_hi(dn)
                if dd.live() and upto not in "BC":
                    e_x_hi(dd)

            b_x_hi(Group(0, 0))
            for c in range(CH):
                b_gelu(Group(0, 0), c)
            over_groups(act, bc_body, 3, 2)
            if upto != "D":
                return

            for n, (dst, src) in enumerate(((R_E, R_Z), (R_E2, R_Z2), (R_1[5], R_1[4]))):
                act.wait_ge(R["z"], n + 1)
                nc.scalar.activation(dst, src, ACT.Exp).then_inc(R["exp"], 1)

            act.wait_ge(R["go"], 1)
            for t in range(2):
                fetch_experts(act, mybir.EngineType.Activation, Group(0, 0), t, (2,))

            def d_body(g):
                for t in range(PER):
                    if g.live():
                        g2, t2 = behind(g, t, -2)
                        if g2.live():
                            fetch_experts(act, mybir.EngineType.Activation, g2, t2, (2,))
                        n = g.tile(t)
                        act.wait_ge(DD["h"], n + 1)
                        reached(act, DD["lo"], n - 1)
                        nc.scalar.activation(D_G[t % 2], PS[:, t % 2, :], ACT.Gelu, scale=UNSCALE).then_inc(DD["gelu"], 1)
                        act.wait_ge(DD["gelu"], n + 1)
                        reached(act, DD["y"], n - 3)
                        nc.scalar.activation(D_GH[t].rearrange("p a b c -> p (a b c)"), D_G[t % 2], ACT.Copy).then_inc(DD["hi"], 1)

            over_groups(act, d_body, 1, 0)

        @block.vector
        def _(dve):
            dve.wait_ge(w_near, NEAR)
            dve.wait_ge(const_done, 1)
            dve.wait_ge(prep_hi, 1)
            nc.vector.scalar_tensor_tensor(R_LO, S_ROW, SCALE, R_HI, ALU.mult, ALU.subtract).then_inc(R["dve"], 1)
            nc.vector.tensor_scalar(EPSI, IDENT[:], EPSC[:, 0:1], None, ALU.mult).then_inc(R["dve"], 1)
            nc.vector.tensor_scalar(RMSW[:], RMSW[:], UNSCALE, None, ALU.mult).then_inc(R["dve"], 1)
            dve.wait_ge(R["dve"], 2)
            nc.vector.tensor_scalar(R_HI, R_HI, IDENT[0:2, 0:1], None, ALU.mult).then_inc(R["dve"], 1)
            nc.vector.tensor_copy(EPSH[:], EPSI).then_inc(R["dve"], 1)
            dve.wait_ge(R["dve"], 5)
            nc.vector.scalar_tensor_tensor(BROW[0:2, :], R_LO, IDENT[0:2, 1:2], R_HI, ALU.mult, ALU.add)
            nc.vector.tensor_tensor(EPSL[:], EPSI, EPSH[:], ALU.subtract)
            for n, (dst, src) in enumerate(((GW1, S_GW1), (GW2, S_GW2))):
                dve.wait_ge(prep_hi, n + 2)
                last = nc.vector.scalar_tensor_tensor(dst[1][:], src, SCALE, dst[0][:], ALU.mult, ALU.subtract)
            last.then_inc(prep_done, 1)

            def late_lo():
                for n, (dst, src) in enumerate(((FW1, S_FW1), (WG, S_WG))):
                    dve.wait_ge(prep_hi, n + 4)
                    nc.vector.scalar_tensor_tensor(dst[1][:], src, SCALE, dst[0][:], ALU.mult, ALU.subtract)
                dve.wait_ge(prep_hi, 6)
                rows = slice(LO_ROW, LO_ROW + EXPERTS)
                nc.vector.scalar_tensor_tensor(EBIAS[rows, :], S_EB[rows, :], SCALE, EBIAS[rows, :], ALU.mult, ALU.subtract)
                dve.wait_ge(R["pe"], 1)
                nc.vector.tensor_copy(FB1[:], PS[:, 7, D:D + CH])
                nc.vector.tensor_scalar(NWT[0][:], PS[:, 7, 0:D], SCALE, None, ALU.mult).then_inc(R["dve"], 1)
                dve.wait_ge(R["dve"], 6)
                nc.vector.scalar_tensor_tensor(NWT[1][:], PS[:, 7, 0:D], SCALE, NWT[0][:], ALU.mult, ALU.subtract).then_inc(prep_done, 1)

            def statistics(tiles, st, mv, ve, s_stats, s_mv, s_ve, at):
                for t in range(PER):
                    last = nc.vector.bn_stats(st[:, t], tiles(t))
                last.then_inc(s_stats, 1)
                dve.drain()
                for t in range(PER):
                    last = nc.vector.bn_aggr(mv[:, t], st[:, t])
                last.then_inc(s_mv, 1)
                dve.wait_ge(s_mv, at)
                nc.vector.tensor_scalar(ve, mv[:, :, 1], LN_EPS, None, ALU.add).then_inc(s_ve, 1)

            def normalise(dst, tiles, mv, rs, s_out):
                for t in range(PER):
                    last = nc.vector.tensor_scalar(dst(t), tiles(t), mv[:, t, 0:1], rs[:, t:t + 1], ALU.subtract, ALU.mult)
                last.then_inc(s_out, 1)

            def x_tile(g):
                return lambda t: X[:, bass.ds(g.n * PER + t, 1), :].rearrange("p a b -> p (a b)")

            def a_stats(g):
                dve.wait_ge(load[g.parity], g.half * 48 + 48)
                statistics(x_tile(g), A_ST[g.parity], A_MV[g.parity], A_VE[g.parity], A["stats"], A["mv"], A["veps"], g.n + 1)

            def a_xn(g):
                j = g.parity
                dve.wait_ge(A["rstd"], g.n + 1)
                reached(dve, A["xn_hi"], g.n - 1)
                reached(dve, A["xn_lo"], g.n - 1)
                normalise(lambda t: A_XN[j][:, t], x_tile(g), A_MV[j], A_RL[j], A["xn"])

            def a_deg(g):
                dve.wait_ge(A["offd"], g.n + 1)
                nc.vector.tensor_reduce(DEG[:, bass.ds(g.n * PER, PER)], A_OFF, AX.X, ALU.add).then_inc(A["deg"], 1)

            def a_adjlo(g):
                dve.wait_ge(A["adj_hi"], g.n + 1)
                s = bass.ds(g.n * PER, PER)
                nc.vector.tensor_tensor(ADJL[:, s, :], PS[:, 0, :].rearrange("p (a b) -> p a b", b=P), ADJH[:, s, :], ALU.subtract).then_inc(A["adj_lo"], 1)

            def a_agglo(g):
                dve.wait_ge(A["agg_hi"], g.n + 1)
                reached(dve, A["h"], g.tile(-4))
                nc.vector.tensor_tensor(A_GL[g.parity], PS[:, 1, :], A_GH[g.parity], ALU.subtract).then_inc(A["agg_lo"], 1)

            def a_body(g):
                up = g.plus(1)
                for t in range(PER):
                    g1, t1 = behind(g, t, 1)
                    g2, t2 = behind(g, t, 2)
                    if t == 2 and g.plus(2).live():
                        a_stats(g.plus(2))
                    if g1.live():
                        n = g1.tile(t1)
                        dve.wait_ge(A["rs"], n + 1)
                        reached(dve, A["hT"], n - 3)
                        nc.vector.scalar_tensor_tensor(A_H[t1], PS[:, 2 + t1 % 2, :], A_RS[t1 % 2][:, 0:1], RMSW[:],
                                                       ALU.mult, ALU.mult).then_inc(A["norm"], 1)
                    if g.live():
                        dve.wait_ge(A["sq"], g.tile(t) + 1)
                        nc.vector.tensor_scalar(A_SE[t % 2], A_SS[t % 2], RMS_EPS, None, ALU.add).then_inc(A["seps"], 1)
                    if t == 3 and up.live():
                        a_agglo(up)
                    if t == 0 and up.live():
                        a_xn(up)
                    if t == 1 and up.live():
                        a_adjlo(up)
                    if g2.live():
                        n = g2.tile(t2)
                        dve.wait_ge(A["hT_hi"], n + 1)
                        reached(dve, A["y"], n - 1)
                        nc.vector.tensor_tensor(A_HL[t2 % 2], PS[:, 4 + t2 % 2, :].rearrange("p (a b) -> p a b", b=P), A_HH[t2 % 2], ALU.subtract).then_inc(A["hT_lo"], 1)
                    if t == 1 and up.live():
                        a_deg(up)
                    if t == 3 and g.plus(-1).live():
                        a_out(g.plus(-1))
                if isinstance(g.n, int) and g.n == 1:
                    late_lo()

            def a_out(g):
                dve.wait_ge(A["y"], g.tile(PER))
                s = bass.ds(g.n * PER, PER)
                nc.vector.scalar_tensor_tensor(X[:, s, :], PS[:, 6 + g.parity, :].rearrange("p (a b) -> p a b", b=D), UNSCALE, X[:, s, :],
                                               ALU.mult, ALU.add).then_inc(A["x1"], 1)

            g0 = Group(0, 0)
            a_stats(g0)
            a_stats(g0.plus(1))
            a_adjlo(g0)
            a_deg(g0)
            a_xn(g0)
            a_agglo(g0)
            over_groups(dve, a_body, 2, 1)
            if upto == "A":
                return

            def ln_stats(g, k, sems):
                statistics(x_tile(g), SM[k]["st"], SM[k]["mv"], SM[k]["ve"], sems["stats"], sems["mv"], sems["veps"], g.n + 1)

            def b_xn(g):
                dve.wait_ge(B["rstd"], g.n + 1)
                reached(dve, B["xT"], g.n)
                normalise(lambda t: B_XN[:, t], x_tile(g), SM["B"]["mv"], SM["B"]["rs"], B["xn"])

            def b_xlo(g):
                dve.wait_ge(B["xT_hi"], g.n + 1)
                reached(dve, B["h"], g.n * CH)
                nc.vector.tensor_tensor(B_XL, PS[:, 4, :], B_XH, ALU.subtract).then_inc(B["xT_lo"], 1)

            def b_hlo(g, c):
                dve.wait_ge(B["h_hi"], g.n * CH + c + 1)
                nc.vector.tensor_tensor(B_HL[g.parity][:, c], B_H[:, c], B_HH[g.parity][:, c], ALU.subtract).then_inc(B["h_lo"], 1)

            def b_gate(g):
                step = [0]
                STEPS = 9

                def done(ins):
                    step[0] += 1
                    ins.then_inc(B["step"], 1)
                    dve.wait_ge(B["step"], g.n * STEPS + step[0])

                wide = [P, PER, EXPERTS]
                dve.wait_ge(B["logits"], g.n + 1)
                nc.vector.scalar_tensor_tensor(LG, PS[:, 4, 0:PER * EXPERTS].rearrange("p (a b) -> p a b", b=EXPERTS), UNSCALE,
                                               BGB[:, :].unsqueeze(1).broadcast_to(wide), ALU.mult, ALU.add).then_inc(B["lg"], 1)
                dve.wait_ge(B["lg"], g.n + 1)
                done(nc.vector.tensor_reduce(LM[:, :, 0], LG, AX.X, ALU.max))
                nc.vector.tensor_tensor(LZ, LG, LM.broadcast_to(wide), ALU.subtract).then_inc(B["lz"], 1)
                dve.wait_ge(B["lz"], g.n + 1)
                done(nc.vector.scalar_tensor_tensor(LC, LZ, 0.0, RIOTA[:, :].unsqueeze(1).broadcast_to(wide), ALU.is_ge, ALU.mult))
                done(nc.vector.tensor_reduce(LX[:, :, 0], LC, AX.X, ALU.max))
                done(nc.vector.tensor_tensor(LC, LC, LX.broadcast_to(wide), ALU.is_equal))
                dve.wait_ge(B["tanh"], g.n + 1)
                nc.vector.tensor_scalar(LN_, LT, 1.0, None, ALU.add)
                done(nc.vector.tensor_scalar(LD, LT, -1.0, 1.0, ALU.mult, ALU.add))
                done(nc.vector.reciprocal(LR, LD))
                done(nc.vector.tensor_tensor(LR, LR, LN_, ALU.mult))
                done(nc.vector.tensor_reduce(LS[:, :, 0], LR, AX.X, ALU.add))
                done(nc.vector.reciprocal(LP, LS))
                nc.vector.scalar_tensor_tensor(GATE[g.parity], LC, UNSCALE, LP.broadcast_to(wide), ALU.mult, ALU.mult).then_inc(B["gate"], 1)
                assert step[0] == STEPS

            def b_combine(g, t):
                n = g.tile(t)
                dve.wait_ge(B["y"], n + 1)
                dve.wait_ge(B["gate"], g.n + 1)
                prev = x_tile(g)(t)
                for e in range(EXPERTS):
                    dst = x_tile(g)(t) if e == EXPERTS - 1 else ACC[t % 2][:, e % 2]
                    ins = nc.vector.scalar_tensor_tensor(dst, PS[:, 2 * (t % 2) + e // 4, (e % 4) * D:(e % 4 + 1) * D],
                                                         GATE[g.parity][:, t, e:e + 1], prev, ALU.mult, ALU.add)
                    prev = dst
                    if e < EXPERTS - 1:
                        ins.then_inc(B["acc"], 1)
                        dve.wait_ge(B["acc"], n * (EXPERTS - 1) + e + 1)
                    else:
                        ins.then_inc(B["comb"], 1)

            def c_xn(g):
                dve.wait_ge(C["rstd"], g.n + 1)
                reached(dve, C["xT"], g.n)
                if upto not in "BC":
                    reached(dve, E["xT"], g.n - 1)
                normalise(lambda t: C_XN[:, t], x_tile(g), SM["C"]["mv"], SM["C"]["rs"], C["xn"])

            def c_xlo(g):
                dve.wait_ge(C["xT_hi"], g.n + 1)
                reached(dve, C["h"], g.n)
                nc.vector.tensor_tensor(C_XL, PS[:, 4, :], C_XH, ALU.subtract).then_inc(C["xT_lo"], 1)

            def c_scale(g):
                dve.wait_ge(A["dis"], GROUPS)
                reached(dve, C["h_hi"], g.n * PER)
                reached(dve, C["h_lo"], g.n)
                nc.vector.tensor_scalar(C_DS, DIS[:, bass.ds(g.n * PER, PER)], UNSCALE, None, ALU.mult).then_inc(C["disS"], 1)

            def c_hlo(g):
                dve.wait_ge(C["h_hi"], g.n * PER + PER)
                dve.wait_ge(C["disS"], g.n + 1)
                reached(dve, C["y"], g.n)
                for t in range(PER):
                    last = nc.vector.scalar_tensor_tensor(C_HL[:, t], PS[:, 7, t * D:(t + 1) * D], C_DS[:, t:t + 1], C_HH[:, t], ALU.mult, ALU.subtract)
                last.then_inc(C["h_lo"], 1)

            def c_out(g):
                dve.wait_ge(C["y"], g.n + 1)
                for t in range(PER):
                    xt = x_tile(g)(t)
                    last = nc.vector.scalar_tensor_tensor(xt, PS[:, 7, t * D:(t + 1) * D], DIS[:, bass.ds(g.n * PER + t, 1)], xt, ALU.mult, ALU.add)
                last.then_inc(C["x3"], 1)

            def e_xn(g):
                dve.wait_ge(E["rstd"], g.n + 1)
                reached(dve, E["xT"], g.n)
                reached(dve, E["kept"], g.n)
                normalise(lambda t: E_XN[:, t], x_tile(g), SM["E"]["mv"], SM["E"]["rs"], E["xn"])

            def e_xlo(g):
                dve.wait_ge(E["xT_hi"], g.n + 1)
                s = bass.ds(g.n * PER, PER)
                nc.vector.tensor_tensor(ADJL[:, s, :], PS[:, 7, :].rearrange("p (a b) -> p a b", b=P), ADJH[:, s, :], ALU.subtract)
                nc.vector.tensor_reduce(MEANT[:, bass.ds(g.n * 2 * PER, 2 * PER)], PS[:, 7, :].rearrange("p (a b) -> p a b", b=NODES), AX.X, ALU.add).then_inc(E["xT_lo"], 1)

            def bc_body(g):
                up, dn, dd = g.plus(1), g.plus(-1), g.plus(-2)
                full = upto not in "B"
                tail = upto not in "BC"
                if up.live():
                    ln_stats(up, "B", B)
                if dn.live():
                    b_combine(dn, 3)
                if g.live():
                    b_gate(g)
                if up.live():
                    b_xn(up)
                if dd.live() and full:
                    c_hlo(dd)
                if g.live():
                    b_combine(g, 0)
                if up.live():
                    b_xlo(up)
                if dn.live() and full:
                    dve.wait_ge(B["comb"], dn.tile(PER))
                    c_scale(dn)
                    ln_stats(dn, "C", C)
                if dd.live() and full:
                    c_out(dd)
                if dd.live() and tail:
                    dve.drain()
                    ln_stats(dd, "E", E)
                if g.live():
                    b_combine(g, 1)
                if dn.live() and full:
                    c_xn(dn)
                if up.live():
                    b_hlo(up, 0)
                    b_hlo(up, 1)
                if dd.live() and tail:
                    e_xn(dd)
                if g.live():
                    b_combine(g, 2)
                if up.live():
                    b_hlo(up, 2)
                    b_hlo(up, 3)
                if dn.live() and full:
                    c_xlo(dn)
                if dd.live() and tail:
                    e_xlo(dd)

            ln_stats(g0, "B", B)
            b_xn(g0)
            b_xlo(g0)
            for c in range(CH):
                b_hlo(g0, c)
            over_groups(dve, bc_body, 3, 2)
            if upto != "D":
                return

            made = [0]

            def then(ins):
                made[0] += 1
                ins.then_inc(R["step"], 1)
                dve.wait_ge(R["step"], made[0])

            def softmax(src, z, e, out, n, one):
                then(nc.vector.tensor_reduce(one[0], src, AX.X, ALU.max))
                nc.vector.tensor_scalar(z, src, one[0], None, ALU.subtract).then_inc(R["z"], 1)
                dve.wait_ge(R["exp"], n)
                then(nc.vector.tensor_reduce(one[1], e, AX.X, ALU.add))
                then(nc.vector.reciprocal(one[2], one[1]))
                then(nc.vector.tensor_scalar(out, e, one[2], None, ALU.mult))

            nc.vector.memset(R_OH, 0.0)
            dve.wait_ge(R["logits"], 1)
            then(nc.vector.scalar_tensor_tensor(R_L, PS[:, 0, 0:EXPERTS], 1.0 / NODES, BR[:], ALU.mult, ALU.add))
            softmax(R_L, R_Z, R_E, R_W, 1, (R_1[0], R_1[1], R_1[2]))
            nc.vector.tensor_copy(R_W2, R_W).then_inc(R["weights"], 1)
            dve.wait_ge(R["loads"], 1)
            then(nc.vector.tensor_scalar(R_C, PS[:, 1, 0:EXPERTS], float(TOKENS // GRAPHS), None, ALU.mult))
            then(nc.vector.reciprocal(R_S, R_C))
            then(nc.vector.tensor_scalar(R_S, R_S, CAPACITY, 1.0, ALU.mult, ALU.min))
            then(nc.vector.tensor_tensor(R_W2, R_W, R_S, ALU.mult))
            softmax(R_W2, R_Z2, R_E2, R_V, 2, (R_1[0], R_1[1], R_1[2]))
            then(nc.vector.max(R_M8, R_V))
            then(nc.vector.max_index(R_I8, R_M8, R_V))
            nc.vector.tensor_tensor(R_1[4], R_M8[:, 1:2], R_M8[:, 0:1], ALU.subtract).then_inc(R["z"], 1)
            dve.wait_ge(R["exp"], 3)
            then(nc.vector.tensor_scalar(R_1[3], R_1[5], 1.0, None, ALU.add))
            then(nc.vector.reciprocal(R_1[6], R_1[3]))
            then(nc.vector.tensor_tensor(R_1[7], R_1[5], R_1[6], ALU.mult))
            nc.vector.tensor_copy(R_Q[:, 0:2], R_I8[:, 0:2])
            nc.vector.tensor_scalar(R_Q[:, 2:3], R_1[6], UNSCALE, None, ALU.mult)
            then(nc.vector.tensor_scalar(R_Q[:, 3:4], R_1[7], UNSCALE, None, ALU.mult))
            for q in range(TOPK):
                for at in (0, LO_ROW):
                    nc.vector.tensor_scalar(R_OH[:, q, at:at + EXPERTS], RIOTA[:], R_Q[:, q:q + 1], float(EXPERTS), ALU.add, ALU.is_equal)
            for q in range(4):
                last = nc.vector.tensor_scalar(R_D[:, q], IDENT[:], R_Q[:, q:q + 1], None, ALU.mult)
            last.then_inc(R["diagonal"], 1)
            dve.wait_ge(R["rows"], 1)
            rows = PS[:, 2, :].rearrange("p (q t b) -> p t b q", q=4, b=2)
            nc.vector.tensor_scalar(IDX[:].rearrange("p t (b q) -> p t b q", q=TOPK), rows[:, :, :, 0:TOPK], 0.0, float(EXPERTS - 1), ALU.max, ALU.min)
            nc.vector.tensor_copy(CHOSEN[:].rearrange("p t (b q) -> p t b q", q=TOPK),
                                  PS[:, 3, 0:TOPK * P].rearrange("p (q t b) -> p t b q", q=TOPK, b=2))
            nc.vector.tensor_copy(WTOP[:].rearrange("p t (b q) -> p t b q", q=TOPK), rows[:, :, :, TOPK:]).then_inc(R["go"], 1)

            dve.wait_ge(R["go"], 1)

            def d_out(g):
                j = g.parity
                dve.wait_ge(DD["yT"], g.tile(PER))
                reached(dve, DD["norm"], g.n)
                s = bass.ds(g.n * PER, PER)
                nc.vector.tensor_tensor(D_R, PS[:, 4 + j, :].rearrange("p (a b) -> p a b", b=D), XN3[:, s, :], ALU.add).then_inc(DD["r"], 1)
                dve.wait_ge(DD["r"], g.n + 1)
                statistics(lambda t: D_R[:, t], SM["D"]["st"], SM["D"]["mv"], SM["D"]["ve"], DD["stats"], DD["mv"], DD["veps"], g.n + 1)

            def d_norm(g):
                j = g.parity
                dve.wait_ge(DD["rstd"], g.n + 1)
                reached(dve, DD["out"], g.n - 1)
                normalise(lambda t: D_N[j][:, t], lambda t: D_R[:, t], SM["D"]["mv"], SM["D"]["rs"], DD["norm"])

            def copy_expert(g, t):
                n = g.tile(t)
                e = experts_of(n, mybir.EngineType.DVE)[3]
                reached(dve, DD["y"], n - 3)
                nc.vector.tensor_copy(SLOT[t][:, 3], expert_weights(e)).then_inc(DD["copied"], 1)

            copy_expert(Group(0, 0), 0)

            def d_body(g):
                for t in range(PER):
                    g3, t3 = behind(g, t, 3)
                    g_up, t_up = behind(g, t, -1)
                    if g_up.live():
                        copy_expert(g_up, t_up)
                    if g3.live():
                        n = g3.tile(t3)
                        dve.wait_ge(DD["y"], n + 1)
                        w = WTOP[:, bass.ds(n, 1), :].rearrange("p a b -> p (a b)").unsqueeze(2).broadcast_to([P, 2 * TOPK, NODES])
                        nc.vector.tensor_tensor(D_YW[t3 % 2].rearrange("p b e n -> p (b e) n"), PS[:, 2 + t3 % 2, 0:2 * TOPK * NODES].rearrange("p (a n) -> p a n", n=NODES), w, ALU.mult).then_inc(DD["yw"], 1)
                        dve.wait_ge(DD["yw"], n + 1)
                        reached(dve, DD["yT"], n - 1)
                        nc.vector.tensor_tensor(D_YS[t3 % 2], D_YW[t3 % 2][:, :, 0], D_YW[t3 % 2][:, :, 1], ALU.add).then_inc(DD["ys"], 1)
                    if t == 1 and g.plus(-2).live():
                        d_out(g.plus(-2))
                    if t == 3 and g.plus(-2).live():
                        d_norm(g.plus(-2))

            over_groups(dve, d_body, 4, 2)

        @block.tensor
        def _(pe):
            pe.wait_ge(const_done, 1)
            def product(dst, lhs, rhs, start=True, stop=True):
                nc.tensor.matmul(dst, lhs[0], rhs[0], start=start, stop=False)
                nc.tensor.matmul(dst, lhs[0], rhs[1], start=False, stop=False)
                return nc.tensor.matmul(dst, lhs[1], rhs[0], start=False, stop=stop)

            def a_transpose(g):
                pe.wait_ge(load[g.parity], g.half * 48 + 48)
                reached(pe, A["adj_lo"], g.n)
                for t in range(PER):
                    last = nc.tensor.transpose(PS[:, 0, t * P:(t + 1) * P], A_ADJ[g.parity][:, t], IDENT[:])
                last.then_inc(A["adjT"], 1)

            def a_aggregate(g):
                j = g.parity
                pe.wait_ge(A["adj_lo"], g.n + 1)
                pe.wait_ge(A["xn_lo"], g.n + 1)
                reached(pe, A["agg_lo"], g.n)
                for t in range(PER):
                    dst = PS[:, 1, t * P:(t + 1) * P]
                    lhs = (A_XH[j][:, t], A_XL[j][:, t])
                    at = bass.ds(g.n * PER + t, 1)
                    adj = (ADJH[:, at, :].rearrange("p a b -> p (a b)"), ADJL[:, at, :].rearrange("p a b -> p (a b)"))
                    product(dst, lhs, adj, stop=False)
                    last = product(dst, lhs, (EPSH[:], EPSL[:]), start=False)
                last.then_inc(A["agg"], 1)

            def a_body(g):
                up = g.plus(1)
                for t in range(PER):
                    g2, t2 = behind(g, t, 2)
                    g3, t3 = behind(g, t, 3)
                    if t == 2 and up.live():
                        a_aggregate(up)
                    if t == 3 and isinstance(g.n, int) and g.n == 1:
                        pe.wait_ge(w_late, LATE)
                        nc.tensor.transpose(PS[:, 7, 0:D], S_NW, IDENT[:])
                        nc.tensor.transpose(PS[:, 7, D:D + CH], FB1R[:], IDENT[0:CH, 0:CH]).then_inc(R["pe"], 1)
                    if g.live():
                        n = g.tile(t)
                        if t == 0:
                            pe.wait_ge(A["agg_lo"], g.n + 1)
                        reached(pe, A["norm"], n - 1)
                        dst = PS[:, 2 + t % 2, :]
                        s = slice(t * P, (t + 1) * P)
                        nc.tensor.matmul(dst, ONE2[:], brow("gb1", 0, HID), start=True, stop=False)
                        product(dst, (A_GH[g.parity][:, s], A_GL[g.parity][:, s]), (GW1[0][:], GW1[1][:]), start=False).then_inc(A["h"], 1)
                    if t == 0 and up.live():
                        a_transpose(up)
                    if g2.live():
                        n = g2.tile(t2)
                        pe.wait_ge(A["silu"], n + 1)
                        reached(pe, A["hT_lo"], n - 1)
                        for c in range(CH):
                            last = nc.tensor.transpose(PS[:, 4 + t2 % 2, c * P:(c + 1) * P], A_H[t2][:, c * P:(c + 1) * P], IDENT[:])
                        last.then_inc(A["hT"], 1)
                    if g3.live():
                        n = g3.tile(t3)
                        pe.wait_ge(A["hT_lo"], n + 1)
                        if t3 == 0:
                            reached(pe, A["x1"], g3.n - 1)
                            if isinstance(g3.n, int) and g3.n == 1:
                                pe.wait_ge(prep_done, 2)
                        dst = PS[:, 6 + g3.parity, t3 * D:(t3 + 1) * D]
                        nc.tensor.matmul(dst, ONE2[:], brow("gb2", 0, D), start=True, stop=False)
                        for c in range(CH):
                            last = product(dst, (A_HH[t3 % 2][:, c], A_HL[t3 % 2][:, c]), (GW2[0][:, c], GW2[1][:, c]), start=False, stop=(c == CH - 1))
                        last.then_inc(A["y"], 1)

            g0 = Group(0, 0)
            pe.wait_ge(prep_done, 1)
            a_transpose(g0)
            a_aggregate(g0)
            over_groups(pe, a_body, 2, 1)
            if upto == "A":
                return

            pe.wait_ge(A["x1"], GROUPS)
            pe.wait_ge(piece_lo, PIECES)

            def four_transposes(src, ready, at, out_sem):
                pe.wait_ge(ready, at)
                for t in range(PER):
                    last = nc.tensor.transpose(PS[:, 4, t * P:(t + 1) * P], src[:, t], IDENT[:])
                last.then_inc(out_sem, 1)

            def b_hidden(g, c):
                pe.wait_ge(B["xT_lo"], g.n + 1)
                reached(pe, B["gelu"], g.n * CH + c - 1)
                s = slice(c * P, (c + 1) * P)
                product(PS[:, 5 + c % 2, :], (FW1[0][:, s], FW1[1][:, s]), (B_XH, B_XL)).then_inc(B["h"], 1)

            def b_logits(g):
                pe.wait_ge(B["h_lo"], g.n * CH + CH)
                hh, hl = B_HH[g.parity], B_HL[g.parity]
                for t in range(PER):
                    s = slice(t * P, (t + 1) * P)
                    for c in range(CH):
                        last = product(PS[:, 4, t * EXPERTS:(t + 1) * EXPERTS], (hh[:, c, s], hl[:, c, s]), (WG[0][:, c], WG[1][:, c]),
                                       start=(c == 0), stop=(c == CH - 1))
                last.then_inc(B["logits"], 1)

            def b_experts(g, t):
                n = g.tile(t)
                reached(pe, B["comb"], n - 1)
                hh, hl = B_HH[g.parity], B_HL[g.parity]
                s = slice(t * P, (t + 1) * P)
                y = [PS[:, 2 * (t % 2) + k, :] for k in range(2)]
                for k in range(2):
                    nc.tensor.matmul(y[k], ONE2[:], brow("bd", k * 512, 512), start=True, stop=False)
                for c in range(CH):
                    for lhs, w in ((hh, 0), (hh, 1), (hl, 0)):
                        for k in range(2):
                            last = nc.tensor.matmul(y[k], lhs[:, c, s], WEXP[:, 2 * c + k, w * 512:(w + 1) * 512], start=False,
                                                    stop=(c == CH - 1 and lhs is hl))
                last.then_inc(B["y"], 1)

            def c_hidden(g):
                pe.wait_ge(C["xT_lo"], g.n + 1)
                reached(pe, C["x3"], g.n)
                for t in range(PER):
                    s = slice(t * P, (t + 1) * P)
                    dst = PS[:, 7, t * D:(t + 1) * D]
                    nc.tensor.matmul(dst, ONE2[:], brow("nb", 0, D), start=True, stop=False)
                    last = product(dst, (C_XH[:, s], C_XL[:, s]), (NWT[0][:], NWT[1][:]), start=False)
                last.then_inc(C["h"], 1)

            def c_neighbours(g):
                pe.wait_ge(C["h_lo"], g.n + 1)
                for t in range(PER):
                    at = bass.ds(g.n * PER + t, 1)
                    adj = (ADJH[:, at, :].rearrange("p a b -> p (a b)"), ADJL[:, at, :].rearrange("p a b -> p (a b)"))
                    last = product(PS[:, 7, t * D:(t + 1) * D], adj, (C_HH[:, t], C_HL[:, t]))
                last.then_inc(C["y"], 1)

            def bc_body(g):
                up, dn, dd = g.plus(1), g.plus(-1), g.plus(-2)
                full = upto not in "B"
                tail = upto not in "BC"
                if g.live():
                    b_experts(g, 0)
                if dd.live() and full:
                    c_neighbours(dd)
                if up.live():
                    if g.live():
                        pe.wait_ge(B["lg"], g.n + 1)
                    four_transposes(B_XN, B["xn"], up.n + 1, B["xT"])
                if g.live():
                    b_experts(g, 1)
                if up.live():
                    b_hidden(up, 0)
                    b_hidden(up, 1)
                if g.live():
                    b_experts(g, 2)
                if up.live():
                    b_hidden(up, 2)
                    b_hidden(up, 3)
                if g.live() and not up.live():
                    pe.wait_ge(B["lg"], g.n + 1)
                if dn.live() and full:
                    four_transposes(C_XN, C["xn"], dn.n + 1, C["xT"])
                if dd.live() and tail:
                    pe.wait_ge(E["xn"], dd.n + 1)
                    for t in range(PER):
                        last = nc.tensor.transpose(PS[:, 7, t * P:(t + 1) * P], E_XN[:, t], IDENT[:])
                    last.then_inc(E["xT"], 1)
                if g.live():
                    b_experts(g, 3)
                if dn.live() and full:
                    if dd.live() and tail:
                        pe.wait_ge(E["xT_lo"], dd.n + 1)
                    c_hidden(dn)
                if up.live():
                    if dn.live() and full:
                        pe.wait_ge(C["xT_lo"], dn.n + 1)
                    b_logits(up)

            four_transposes(B_XN, B["xn"], 1, B["xT"])
            for c in range(CH):
                b_hidden(g0, c)
            b_logits(g0)
            over_groups(pe, bc_body, 3, 2)
            if upto != "D":
                return

            pe.wait_ge(E["xT_lo"], GROUPS)
            nc.tensor.matmul(PS[:, 0, 0:EXPERTS], MEANT[:], WR[:], start=True, stop=True).then_inc(R["logits"], 1)
            pe.wait_ge(R["weights"], 1)
            nc.tensor.matmul(PS[:, 1, 0:EXPERTS], ONES[:], R_W, start=True, stop=True).then_inc(R["loads"], 1)
            pe.wait_ge(R["diagonal"], 1)
            for q in range(TOPK):
                nc.tensor.transpose(PS[:, 3, q * P:(q + 1) * P], R_OH[:, q], IDENT[:])
            nc.tensor.matmul(PS[:, 2, :], ONES[:], R_D.rearrange("p a b -> p (a b)"), start=True, stop=True).then_inc(R["rows"], 1)

            pe.wait_ge(R["go"], 1)

            def biases(dst, n, at, start=True):
                pick = CHOSEN[:, bass.ds(n, 1), :].rearrange("p a b -> p (a b)").unsqueeze(2).broadcast_to([P, 2 * TOPK, NODES])
                nc.tensor.matmul(dst, EBIAS[:, at:at + P], pick, start=start, stop=False)

            def d_hidden(g, t):
                n = g.tile(t)
                reached(pe, DD["gelu"], n - 1)
                pe.wait_ge(fetched[t], (g.n + 1) * FETCHED * 16)
                pe.wait_ge(DD["copied"], n + 1)
                at = bass.ds(n, 1)
                for c in range(FCH):
                    biases(PS[:, t % 2, c * 2 * P:(c + 1) * 2 * P], n, c * P, start=(c == 0))
                for k in range(2 * TOPK):
                    graph = slice(k // TOPK * NODES, (k // TOPK + 1) * NODES)
                    x = (ADJH[:, at, graph].rearrange("p a b -> p (a b)"), ADJL[:, at, graph].rearrange("p a b -> p (a b)"))
                    for c in range(FCH):
                        w = [SLOT[t][:, k, i + c * P:i + (c + 1) * P] for i in W1_AT]
                        last = product(PS[:, t % 2, (c * 2 * TOPK + k) * NODES:(c * 2 * TOPK + k + 1) * NODES], w, x, start=False, stop=(k == 2 * TOPK - 1 and c == FCH - 1))
                last.then_inc(DD["h"], 1)

            def d_out_product(g, t):
                n = g.tile(t)
                pe.wait_ge(DD["lo"], n + 1)
                reached(pe, DD["yw"], n - 1)
                biases(PS[:, 2 + t % 2, 0:2 * P], n, FF)
                for k in range(2 * TOPK):
                    for c in range(FCH):
                        w = [SLOT[t][:, k, i + c * D:i + (c + 1) * D] for i in W2_AT]
                        last = product(PS[:, 2 + t % 2, k * NODES:(k + 1) * NODES], w, (D_GH[t][:, c, k], D_GL[t][:, c, k]), start=False, stop=(k == 2 * TOPK - 1 and c == FCH - 1))
                last.then_inc(DD["y"], 1)

            def d_body(g):
                for t in range(PER):
                    g2, t2 = behind(g, t, 2)
                    g4, t4 = behind(g, t, 4)
                    if g2.live():
                        d_out_product(g2, t2)
                    if g.live():
                        d_hidden(g, t)
                    if g4.live():
                        n = g4.tile(t4)
                        pe.wait_ge(DD["ys"], n + 1)
                        if t4 == 0:
                            reached(pe, DD["r"], g4.n - 1)
                        nc.tensor.transpose(PS[:, 4 + g4.parity, t4 * D:(t4 + 1) * D], D_YS[t4 % 2].rearrange("p a b -> p (a b)"), IDENT[:]).then_inc(DD["yT"], 1)

            over_groups(pe, d_body, 4, 2)


NAMES = ["x", "adj", "L0_gnn_epsilon", "L0_gnn_W1", "L0_gnn_b1", "L0_gnn_rms_weight", "L0_gnn_W2", "L0_gnn_b2",
         "L0_ffn_W1", "L0_ffn_b1", "L0_ffn_Wg", "L0_ffn_bg", "L0_ffn_Wd", "L0_ffn_bd", "L1_gnn_W", "L1_gnn_b",
         "L1_ffn_Wr", "L1_ffn_br", "L1_ffn_W1", "L1_ffn_b1", "L1_ffn_W2", "L1_ffn_b2", "L1_ffn_gamma", "L1_ffn_beta"]


def kernel(**inputs):
    import numpy as np
    import concourse.bacc as bacc
    from concourse.bass_utils import run_bass_kernel_spmd

    nc = bacc.Bacc("TRN2", target_bir_lowering=False, num_devices=1)
    arrays, args = {}, []
    for name in NAMES:
        a = np.ascontiguousarray(inputs[name])
        arrays[name] = a
        args.append(nc.dram_tensor(name, a.shape, mybir.dt.from_np(a.dtype), kind="ExternalInput").ap())
    out = nc.dram_tensor("out", (GRAPHS, NODES, D), F32, kind="ExternalOutput").ap()
    build(nc, *args, out)
    r = run_bass_kernel_spmd(nc, [arrays], core_ids=[0])
    return r.results[0]["out"]
```

```python
from contextlib import ExitStack

import concourse.bass as bass
from concourse import mybir

F32 = mybir.dt.float32
F16 = mybir.dt.float16
I32 = mybir.dt.int32
U32 = mybir.dt.uint32
ALU = mybir.AluOpType
ACT = mybir.ActivationFunctionType
AX = mybir.AxisListType

P = 128
GRAPHS, NODES, D = 128, 64, 128
HID = 512
EXPERTS = 8
FF = 256
TOKENS = GRAPHS * NODES
TILES = TOKENS // P
PER = 4
GROUPS = TILES // PER
WIDE = PER * P
CH = HID // P
FCH = FF // P
TOPK = 2
LO_ROW = 32
WORK_WORDS = 11648
SCALE = 64.0
UNSCALE = 1.0 / SCALE
LN_EPS = 1e-5
RMS_EPS = 1e-6
CAPACITY = float(-(-TOKENS * 5 // (4 * EXPERTS)))


class Group:

    def __init__(self, i, off):
        self.i, self.off = i, off
        self.parity = off % 2
        self.half = i + off // 2
        self.n = i * 2 + off

    def plus(self, k):
        return Group(self.i, self.off + k)

    def live(self):
        return not isinstance(self.n, int) or 0 <= self.n < GROUPS

    def tile(self, t):
        return self.n * PER + t


def behind(g, t, k):
    return g.plus((t - k) // PER), (t - k) % PER


def reached(eng, sem, count):
    if not isinstance(count, int) or count > 0:
        eng.wait_ge(sem, count)


def over_groups(eng, body, lead, tail):
    pairs = (GROUPS - lead - 1) // 2
    for n in range(lead):
        body(Group(0, n))
    with eng.Fori(0, pairs) as i:
        body(Group(i, lead))
        body(Group(i, lead + 1))
    for n in range(lead + 2 * pairs, GROUPS + tail):
        body(Group(0, n))


def build(nc, x_in, adj_in, eps_in, gw1_in, gb1_in, rms_in, gw2_in, gb2_in, fw1_in, fb1_in, wg_in,
          bg_in, wd_in, bd_in, nw_in, nb_in, wr_in, br_in, ew1_in, eb1_in, ew2_in, eb2_in,
          gamma_in, beta_in, out):
    ctx = ExitStack()

    def sb(name, shape, dt=F32):
        return ctx.enter_context(nc.sbuf_tensor(name, shape, dt))

    def sem(name):
        return ctx.enter_context(nc.semaphore(name))

    class Carve:

        def __init__(self, tensor):
            self.tensor, self.at = tensor, 0

        def take(self, *shape, dt=F32):
            n = 1
            for s in shape:
                n *= s
            words = n if dt == F32 else n // 2
            v = self.tensor[:, self.at:self.at + words]
            self.at += words
            if dt == F16:
                v = v.bitcast(F16)
            if len(shape) == 2:
                v = v.rearrange("p (a b) -> p a b", b=shape[1])
            if len(shape) == 3:
                v = v.rearrange("p (a b c) -> p a b c", b=shape[1], c=shape[2])
            return v

    with ctx:
        X = sb("X", [P, TILES, D])
        XN3 = sb("XN3", [P, TILES, D])
        ADJH = sb("ADJH", [P, TILES, P], F16)
        ADJL = sb("ADJL", [P, TILES, P], F16)
        GW1 = [sb(f"GW1{s}", [P, HID], F16) for s in "HL"]
        GW2 = [sb(f"GW2{s}", [P, CH, D], F16) for s in "HL"]
        FW1 = [sb(f"FW1{s}", [P, HID], F16) for s in "HL"]
        WG2 = sb("WG2", [P, CH, 2, EXPERTS], F16)
        WG = [WG2[:, :, i] for i in range(2)]
        NWT = [sb(f"NWT{s}", [P, D], F16) for s in "HL"]
        PIECE = 512
        L1_PIECE = CH * EXPERTS * D // PIECE
        PIECES = L1_PIECE + EXPERTS
        WEXP = sb("WEXP", [P, PIECES, 2 * PIECE], F16)
        W1_AT, W2_AT = (0, PIECE), (FF, PIECE + FF)
        assert PIECES == GROUPS and PIECE == 2 * FF == WIDE
        EBIAS = sb("EBIAS", [P, FF + D], F16)
        CHOSEN = sb("CHOSEN", [P, TILES, 2 * TOPK], F16)
        ROWS = dict(gb1=HID, gb2=D, nb=D, bd=EXPERTS * D)
        row_at, n_rows = {}, 0
        for k, n in ROWS.items():
            row_at[k] = n_rows
            n_rows += n
        BROW = sb("BROW", [2, n_rows], F16)
        ROWS_A = row_at["nb"]
        ROWSCALE = sb("ROWSCALE", [2, 1])

        def brow(k, a, n):
            return BROW[0:2, row_at[k] + a:row_at[k] + a + n]

        IDENT = sb("IDENT", [P, P])
        NOTI = sb("NOTI", [P, P])
        ONES = sb("ONES", [P, P])
        ONE2 = sb("ONE2", [2, P], F16)
        NEGH = sb("NEGH", [P, EXPERTS])
        RIOTA = sb("RIOTA", [P, EXPERTS])
        EPSH = sb("EPSH", [P, P], F16)
        EPSL = sb("EPSL", [P, P], F16)
        EPSC = sb("EPSC", [P, 1])
        RMSW = sb("RMSW", [P, HID])
        FB1 = sb("FB1", [P, CH])
        FB1R = sb("FB1R", [CH, P])
        BGB = sb("BGB", [P, EXPERTS])
        WR = sb("WR", [P, EXPERTS])
        BR = sb("BR", [P, EXPERTS])
        GAMMA = sb("GAMMA", [P, D])
        BETA = sb("BETA", [P, D])
        DEG = sb("DEG", [P, TILES])
        DIS = sb("DIS", [P, TILES])
        MEANT = sb("MEANT", [P, GRAPHS])
        IDX = sb("IDX", [P, 2 * TOPK, TILES], I32)
        WTOP = sb("WTOP", [P, TILES, 2 * TOPK])
        SLOT3 = sb("SLOT3", [P, 2 * TOPK * PIECE])
        WORK = sb("WORK", [P, WORK_WORDS])
        PS = ctx.enter_context(nc.psum_tensor("PS", [P, 8, 512], F32))

        S_EXP = XN3[:, :, :].rearrange("p a b -> p (a b)").rearrange("p (j w) -> p j w", w=PIECE)
        near = Carve(X[:, :, :].rearrange("p a b -> p (a b)")[:, 3 * WIDE:])
        S_GW1 = near.take(HID)
        S_GW2 = near.take(CH, D)
        late = Carve(SLOT3[:])
        S_FW1 = late.take(HID)
        S_WG = late.take(CH, EXPERTS)
        S_NW = late.take(D)
        S_EB = late.take(FF + D)
        WORK_A = WORK_WORDS - 3 * WIDE
        a = Carve(WORK[:, WORK_A:])
        A_ADJ = [a.take(PER, P) for _ in range(2)]
        A_OFF = a.take(PER, P)
        a2 = Carve(WORK[:, 0:WORK_A])
        A_XN = [a2.take(PER, D) for _ in range(2)]
        A_XH = [a2.take(PER, D, dt=F16) for _ in range(2)]
        A_XL = [a2.take(PER, D, dt=F16) for _ in range(2)]
        A_GH = [a2.take(WIDE, dt=F16) for _ in range(2)]
        A_GL = [a2.take(WIDE, dt=F16) for _ in range(2)]
        A_SS = [a2.take(1) for _ in range(2)]
        A_SE = [a2.take(1) for _ in range(2)]
        A_RS = [a2.take(1) for _ in range(2)]
        A_STATS = [a2.take(PER, 6) for _ in range(2)]
        A_MV = [a2.take(PER, 2) for _ in range(2)]
        A_VE = [a2.take(PER) for _ in range(2)]
        A_RSTD = [a2.take(PER) for _ in range(2)]
        hidden_at = a2.at
        A_H = [a2.take(HID) for _ in range(4)]
        A_HH = [a2.take(CH, P, dt=F16) for _ in range(2)]
        A_HL = [a2.take(CH, P, dt=F16) for _ in range(2)]
        A_JUNK = [a2.take(HID, dt=F16) for _ in range(2)]
        rows = Carve(WORK[:, hidden_at:])
        S_ROWA = rows.take(ROWS_A)[0:2, :]
        M_ROWA = rows.take(ROWS_A, dt=F16)[0:2, :]
        EPSI = rows.take(P)
        S_ROWB = a2.take(n_rows - ROWS_A)[0:2, :]
        M_ROWB = a2.take(n_rows - ROWS_A, dt=F16)[0:2, :]
        assert a2.at <= WORK_A

        b = Carve(WORK[:, :])
        B_XN = b.take(PER, D)
        B_XH = b.take(WIDE, dt=F16)
        B_XL = b.take(WIDE, dt=F16)
        NORM = {"B": dict(st=b.take(PER, 6), mv=b.take(PER, 2), ve=b.take(PER), rs=b.take(PER))}
        B_H = b.take(CH, WIDE)
        B_HH = [b.take(CH, WIDE, dt=F16) for _ in range(2)]
        B_HL = [b.take(CH, WIDE, dt=F16) for _ in range(2)]
        C_XN = b.take(PER, D)
        C_XH = b.take(WIDE, dt=F16)
        C_XL = b.take(WIDE, dt=F16)
        C_HH = b.take(PER, D, dt=F16)
        C_HL = b.take(PER, D, dt=F16)
        ACC = [b.take(2, D) for _ in range(2)]
        for k in ("C", "E"):
            NORM[k] = dict(st=b.take(PER, 6), mv=b.take(PER, 2), ve=b.take(PER), rs=b.take(PER))
        C_SCALE = b.take(PER)
        E_XN = b.take(PER, D)
        LOGIT = b.take(PER, EXPERTS)
        LOGIT_Z = b.take(PER, EXPERTS)
        TANH_Z = b.take(PER, EXPERTS)
        ONEHOT = b.take(PER, EXPERTS)
        EXP_TOP = b.take(PER, EXPERTS)
        EXP_BOTTOM = b.take(PER, EXPERTS)
        EXP_Z = b.take(PER, EXPERTS)
        LOGIT_MAX = b.take(PER, 1)
        FIRST = b.take(PER, 1)
        EXP_SUM = b.take(PER, 1)
        PROB = b.take(PER, 1)
        GATE = [b.take(PER, EXPERTS) for _ in range(2)]

        SLOT = [v.rearrange("p (k w) -> p k w", k=2 * TOPK)
                for v in (WEXP[:, 0:4].rearrange("p a b -> p (a b)"), WEXP[:, 4:8].rearrange("p a b -> p (a b)"),
                          WORK[:, 0:2048].bitcast(F16), SLOT3[:].bitcast(F16))]
        d = Carve(WORK[:, 2048:])
        D_G = [d.take(WIDE) for _ in range(2)]
        D_GH = [d.take(FCH, 2 * TOPK, NODES, dt=F16) for _ in range(4)]
        D_GL = [d.take(FCH, 2 * TOPK, NODES, dt=F16) for _ in range(4)]
        D_WEIGHTED = [d.take(2, TOPK, NODES) for _ in range(2)]
        D_SUM = [d.take(2, NODES) for _ in range(2)]
        D_RES = d.take(PER, D)
        D_NORM = [d.take(PER, D) for _ in range(2)]
        D_XB = [d.take(PER, D) for _ in range(2)]
        D_O = [d.take(PER, D) for _ in range(2)]
        NORM["D"] = dict(st=d.take(PER, 6), mv=d.take(PER, 2), ve=d.take(PER), rs=d.take(PER))

        r = Carve(WORK[:, 2048 + d.at:])
        R_LOGIT, R_Z, R_E, R_WEIGHT = (r.take(EXPERTS) for _ in range(4))
        R_LOAD, R_FACTOR, R_SCALED = (r.take(EXPERTS) for _ in range(3))
        R_Z2, R_E2, R_FINAL = (r.take(EXPERTS) for _ in range(3))
        R_TOP, R_TOPI = r.take(EXPERTS), r.take(EXPERTS).bitcast(U32)
        R_MAX, R_SUM, R_INV, R_DEN = (r.take(1) for _ in range(4))
        R_GAP, R_EGAP = r.take(1), r.take(1)
        R_FIRST, R_SECOND = r.take(1), r.take(1)
        R_NUMBERS = r.take(4)
        R_DIAG = r.take(4, P)
        R_ONEHOT = r.take(TOPK, P)
        assert 2048 + d.at + r.at <= WORK_WORDS

        w_near, w_late = sem("weights_near"), sem("weights_late")
        w_experts_l0, w_experts_l1 = sem("weights_experts_l0"), sem("weights_experts_l1")
        const_done, pool_step, row_scale = sem("constants_done"), sem("pool_step"), sem("row_scale_ready")
        buffers_clear = sem("buffers_clear")
        prep_hi, prep_done, transposed = sem("weights_hi_ready"), sem("weights_ready"), sem("weights_transposed")
        piece_scaled, piece_lo = sem("piece_scaled"), sem("piece_lo_ready")
        load = [sem("load_even"), sem("load_odd")]
        store = [sem("store_even"), sem("store_odd")]
        A = {k: sem("A_" + k) for k in (
            "mv", "veps", "rstd", "xn", "xn_hi", "xn_lo",
            "offd", "deg", "dis",
            "adjT", "adj_hi", "adj_lo",
            "agg", "agg_hi", "agg_lo",
            "h", "sq", "seps", "rs", "norm",
            "silu", "hT", "hT_hi", "hT_lo",
            "y", "x1")}
        B = {k: sem("B_" + k) for k in (
            "mv", "veps", "rstd", "xn", "xT", "xT_hi", "xT_lo",
            "h", "gelu", "h_hi", "h_lo",
            "logits", "lg", "lz",
            "tanh", "step", "gate",
            "y", "acc", "comb")}
        C = {k: sem("C_" + k) for k in (
            "mv", "veps", "rstd", "xn", "xT", "xT_hi", "xT_lo",
            "h", "scale", "h_hi", "h_lo",
            "y", "x3")}
        E = {k: sem("E_" + k) for k in (
            "mv", "veps", "rstd", "xn", "xT", "xT_hi", "xT_lo", "kept")}
        R = {k: sem("R_" + k) for k in (
            "logits", "z", "exp", "step", "weights", "loads",
            "diagonal", "rows", "go")}
        fetched = [sem(f"D_fetched_{t}") for t in range(PER)]
        DD = {k: sem("D_" + k) for k in (
            "copied", "h", "hi", "lo_pool", "lo_dve",
            "y", "yw", "ys", "yT",
            "r", "mv", "veps", "rstd", "norm",
            "gam", "xb", "out")}

        x_view = x_in.rearrange("(t two) n d -> (two n) t d", two=2)
        adj_view = adj_in.rearrange("(t two) n m -> two n t m", two=2)
        out_view = out.rearrange("(t two) n d -> (two n) t d", two=2)

        LO_DVE = 256
        FETCHED = 3

        def experts_of(g, k, kind):
            return nc.values_load_multi_w_load_instructions(
                IDX[0:1, k, bass.ds(g.n * PER, PER)], engines=[kind],
                min_val=0, max_val=EXPERTS - 1, skip_runtime_bounds_check_because="stage R clamps them")[1]

        def expert_weights(e):
            return WEXP[:, bass.ds(e + L1_PIECE, 1), :].rearrange("p a b -> p (a b)")

        def fetch_expert(eng, g, t, k, e):
            reached(eng, DD["y"], g.tile(t) - 3)
            eng.dma_start(SLOT[t][:, k], expert_weights(e)).then_inc(fetched[t], 16)

        NEAR, LATE = 6 * 16, 15 * 16

        block = ctx.enter_context(nc.Block())

        @block.sync
        def _(sp):
            sp.wait_ge(buffers_clear, 2)

            def a_load(g):
                reached(sp, load[g.parity], g.half * 48)
                reached(sp, A["adjT"], g.n - 1)
                reached(sp, A["offd"], g.n - 1)
                if isinstance(g.n, int) and g.n == 2:
                    sp.wait_ge(prep_done, 3)
                sp.dma_start(X[:, bass.ds(g.n * PER, PER), :], x_view[:, bass.ds(g.n * PER, PER), :]).then_inc(load[g.parity], 16)
                for half in range(2):
                    s = slice(half * NODES, (half + 1) * NODES)
                    sp.dma_start(A_ADJ[g.parity][s, :, s], adj_view[half, :, bass.ds(g.n * PER, PER), :]).then_inc(load[g.parity], 16)

                if isinstance(g.n, int) and g.n == 2:
                    late_weights()
                if isinstance(g.n, int) and g.n == 3:
                    l1_expert_weights()

            def late_weights():
                sp.wait_ge(buffers_clear, 3)
                for dst, src in ((S_FW1, fw1_in), (S_WG, wg_in.rearrange("(c p) e -> p c e", p=P)), (S_NW, nw_in),
                                 (FB1R[:], fb1_in.rearrange("(c p) -> c p", p=P)), (BGB[:], bg_in.partition_broadcast(P)),
                                 (BR[:], br_in.partition_broadcast(P)), (GAMMA[:], gamma_in.partition_broadcast(P)),
                                 (BETA[:], beta_in.partition_broadcast(P)), (WR[:], wr_in),
                                 (S_EB[0:EXPERTS, 0:FF], eb1_in), (S_EB[0:EXPERTS, FF:FF + D], eb2_in),
                                 (S_EB[LO_ROW:LO_ROW + EXPERTS, 0:FF], eb1_in), (S_EB[LO_ROW:LO_ROW + EXPERTS, FF:FF + D], eb2_in)):
                    sp.dma_start(dst, src).then_inc(w_late, 16)
                for name, src in (("nb", nb_in), ("bd", bd_in.rearrange("e d -> (e d)"))):
                    at = row_at[name] - ROWS_A
                    sp.dma_start(S_ROWB[:, at:at + ROWS[name]], src.partition_broadcast(2)).then_inc(w_late, 16)
                for c in range(CH):
                    sp.dma_start(S_EXP[:, 2 * c:2 * c + 2, :].rearrange("p k (e d) -> p (k e) d", d=D),
                                 wd_in.rearrange("e (c p) d -> c p e d", p=P)[c]).then_inc(w_experts_l0, 16)

            def l1_expert_weights():
                sp.dma_start(S_EXP[:, L1_PIECE:, 0:FF], ew1_in.rearrange("e d f -> d e f")).then_inc(w_experts_l1, 16)
                for c in range(FCH):
                    sp.dma_start(S_EXP[:, L1_PIECE:, FF + c * D:FF + (c + 1) * D],
                                 ew2_in.rearrange("e (c p) d -> c p e d", p=P)[c]).then_inc(w_experts_l1, 16)

            over_groups(sp, a_load, 4, 0)

            sp.wait_ge(R["go"], 1)

            def d_body(g):
                if g.live():
                    experts = [experts_of(g, k, mybir.EngineType.SP) for k in range(2)]
                    for t in range(PER):
                        for k in range(2):
                            fetch_expert(sp, g, t, k, experts[k][t])
                dn = g.plus(-3)
                if dn.live():
                    sp.wait_ge(DD["out"], dn.n + 1)
                    sp.dma_start(out_view[:, bass.ds(dn.n * PER, PER), :], D_O[dn.parity]).then_inc(store[dn.parity], 16)

            over_groups(sp, d_body, 4, 3)
            for j in range(2):
                sp.wait_ge(store[j], GROUPS // 2 * 16)

        @block.gpsimd
        def _(pool):
            for j in range(2):
                nc.gpsimd.memset(A_ADJ[j], 0.0).then_inc(buffers_clear, 1)
            nc.gpsimd.memset(S_EB, 0.0).then_inc(buffers_clear, 1)
            nc.gpsimd.memset(IDENT[:], 0.0).then_inc(pool_step, 1)
            nc.gpsimd.memset(NOTI[:], 1.0).then_inc(pool_step, 1)
            nc.gpsimd.memset(ONES[:], 1.0)
            nc.gpsimd.memset(ONE2[:], 1.0)
            nc.gpsimd.memset(NEGH[:], -0.5)
            pool.wait_ge(pool_step, 2)
            nc.gpsimd.affine_select(out=IDENT[:], in_=IDENT[:], compare_op=ALU.not_equal, fill=1.0, base=0,
                                    pattern=[[-1, P]], channel_multiplier=1)
            nc.gpsimd.affine_select(out=NOTI[:], in_=NOTI[:], compare_op=ALU.not_equal, fill=0.0, base=0,
                                    pattern=[[-1, P]], channel_multiplier=1)
            nc.gpsimd.iota(RIOTA[:], pattern=[[-1, EXPERTS]], base=EXPERTS, channel_multiplier=0,
                           allow_small_or_imprecise_dtypes=True).then_inc(const_done, 1)
            pool.wait_ge(const_done, 1)

            def power(dst, src, ready, at, s_out, k):
                pool.wait_ge(ready, at)
                nc.gpsimd.tensor_tensor(dst, src, NEGH[:, 0:k], ALU.pow).then_inc(s_out, 1)

            def ln_power(g, k, sems):
                power(NORM[k]["rs"], NORM[k]["ve"], sems["veps"], g.n + 1, sems["rstd"], PER)

            def a_rstd(g):
                power(A_RSTD[g.parity], A_VE[g.parity], A["veps"], g.n + 1, A["rstd"], PER)

            def a_offd(g):
                pool.wait_ge(load[g.parity], g.half * 48 + 48)
                reached(pool, A["deg"], g.n)
                nc.gpsimd.tensor_tensor(A_OFF, A_ADJ[g.parity], NOTI[:, :].unsqueeze(1).broadcast_to([P, PER, P]), ALU.mult).then_inc(A["offd"], 1)

            def a_xlo(g):
                j = g.parity
                pool.wait_ge(A["xn_hi"], g.n + 1)
                pool.wait_ge(A["xn"], g.n + 1)
                reached(pool, A["agg"], g.n - 1)
                nc.gpsimd.tensor_tensor(A_XL[j], A_XN[j], A_XH[j], ALU.subtract).then_inc(A["xn_lo"], 1)

            def a_deg(g):
                pool.wait_ge(A["deg"], g.n + 1)
                nc.gpsimd.tensor_tensor(DIS[:, bass.ds(g.n * PER, PER)], DEG[:, bass.ds(g.n * PER, PER)], NEGH[:, 0:PER], ALU.pow).then_inc(A["dis"], 1)

            def a_body(g):
                for t in range(PER):
                    if g.live():
                        n = g.tile(t)
                        power(A_RS[t % 2], A_SE[t % 2], A["seps"], n + 1, A["rs"], 1)
                    if t == 0 and g.plus(1).live():
                        a_xlo(g.plus(1))
                        a_offd(g.plus(1))
                    if t == 2 and g.plus(2).live():
                        a_rstd(g.plus(2))
                    if t == 3 and g.plus(1).live():
                        a_deg(g.plus(1))
                    if isinstance(g.n, int) and g.n == GROUPS and t == 0:
                        ln_power(Group(0, 0), "B", B)
                    if t == 1 and g.plus(-1).live():
                        piece_lo_part(g.plus(-1))

            def piece_lo_part(g):
                pool.wait_ge(piece_scaled, g.n + 1)
                nc.gpsimd.tensor_tensor(WEXP[:, bass.ds(g.n, 1), PIECE:], S_EXP[:, bass.ds(g.n, 1), :], WEXP[:, bass.ds(g.n, 1), 0:PIECE],
                                        ALU.subtract).then_inc(piece_lo, 1)

            a_offd(Group(0, 0))
            a_rstd(Group(0, 0))
            a_xlo(Group(0, 0))
            a_deg(Group(0, 0))
            a_rstd(Group(0, 1))
            over_groups(pool, a_body, 2, 1)

            def bc_body(g):
                if g.plus(1).live():
                    ln_power(g.plus(1), "B", B)
                if g.plus(-1).live():
                    ln_power(g.plus(-1), "C", C)
                if g.plus(-2).live():
                    ln_power(g.plus(-2), "E", E)

            over_groups(pool, bc_body, 3, 2)

            pool.wait_ge(R["go"], 1)

            def d_lo(g, t):
                n = g.tile(t)
                pool.wait_ge(DD["hi"], n + 1)
                reached(pool, DD["y"], n - 3)
                nc.gpsimd.tensor_tensor(D_GL[t].rearrange("p a b c -> p (a b c)")[:, LO_DVE:], D_G[t % 2][:, LO_DVE:],
                                        D_GH[t].rearrange("p a b c -> p (a b c)")[:, LO_DVE:], ALU.subtract).then_inc(DD["lo_pool"], 1)

            def d_beta(g):
                reached(pool, DD["out"], g.n - 1)
                nc.gpsimd.tensor_tensor(D_XB[g.parity], X[:, bass.ds(g.n * PER, PER), :],
                                        BETA[:, :].unsqueeze(1).broadcast_to([P, PER, D]), ALU.add).then_inc(DD["xb"], 1)

            def d_gamma(g):
                j = g.parity
                pool.wait_ge(DD["norm"], g.n + 1)
                nc.gpsimd.tensor_tensor(D_NORM[j], D_NORM[j], GAMMA[:, :].unsqueeze(1).broadcast_to([P, PER, D]), ALU.mult).then_inc(DD["gam"], 1)

            def d_sum(g):
                j = g.parity
                pool.wait_ge(DD["gam"], g.n + 1)
                pool.wait_ge(DD["xb"], g.n + 1)
                reached(pool, store[j], g.half * 16)
                nc.gpsimd.tensor_tensor(D_O[j], D_NORM[j], D_XB[j], ALU.add).then_inc(DD["out"], 1)

            def d_body(g):
                for t in range(PER):
                    g1, t1 = behind(g, t, 1)
                    if g1.live():
                        d_lo(g1, t1)
                    if t == 0 and g.plus(-3).live():
                        d_gamma(g.plus(-3))
                    if t == 1 and g.plus(-3).live():
                        d_sum(g.plus(-3))
                    if t == 2 and g.plus(-2).live():
                        ln_power(g.plus(-2), "D", DD)
                    if t == 3 and g.plus(-2).live():
                        d_beta(g.plus(-2))

            over_groups(pool, d_body, 5, 3)

        @block.scalar
        def _(act):
            act.dma_start(EPSC[:], eps_in.partition_broadcast(P)).then_inc(w_near, 16)
            act.dma_start(RMSW[:], rms_in.partition_broadcast(P)).then_inc(w_near, 16)
            for name, src in (("gb1", gb1_in), ("gb2", gb2_in)):
                act.dma_start(S_ROWA[:, row_at[name]:row_at[name] + ROWS[name]], src.partition_broadcast(2)).then_inc(w_near, 16)
            act.dma_start(S_GW1, gw1_in).then_inc(w_near, 16)
            act.dma_start(S_GW2, gw2_in.rearrange("(c p) d -> p c d", p=P)).then_inc(w_near, 16)

            def near_hi():
                act.wait_ge(w_near, NEAR)
                act.wait_ge(row_scale, 1)
                nc.scalar.activation(M_ROWA, S_ROWA, ACT.Copy, scale=ROWSCALE[:, 0:1]).then_inc(prep_hi, 1)
                for dst, src in ((GW1[0][:], S_GW1), (GW2[0][:], S_GW2)):
                    nc.scalar.activation(dst, src, ACT.Copy, scale=SCALE).then_inc(prep_hi, 1)

            def late_hi():
                act.wait_ge(w_late, LATE)
                for dst, src in ((FW1[0][:], S_FW1), (WG[0], S_WG)):
                    nc.scalar.activation(dst, src, ACT.Copy, scale=SCALE).then_inc(prep_hi, 1)

            def late_rows_hi():
                nc.scalar.activation(M_ROWB, S_ROWB, ACT.Copy, scale=ROWSCALE[:, 0:1]).then_inc(prep_hi, 1)
                nc.scalar.activation(EBIAS[:], S_EB, ACT.Copy, scale=SCALE).then_inc(prep_hi, 1)

            def piece(g):
                act.wait_ge(w_experts_l0, CH * 16)
                if not isinstance(g.n, int) or g.n >= L1_PIECE:
                    act.wait_ge(w_experts_l1, (1 + FCH) * 16)
                nc.scalar.activation(WEXP[:, bass.ds(g.n, 1), 0:PIECE], S_EXP[:, bass.ds(g.n, 1), :], ACT.Copy, scale=SCALE)
                nc.scalar.activation(S_EXP[:, bass.ds(g.n, 1), :], S_EXP[:, bass.ds(g.n, 1), :], ACT.Copy, scale=SCALE).then_inc(piece_scaled, 1)

            def adj_hi(g):
                act.wait_ge(A["adjT"], g.n + 1)
                nc.scalar.activation(ADJH[:, bass.ds(g.n * PER, PER), :], PS[:, 0, :].rearrange("p (a b) -> p a b", b=P), ACT.Copy).then_inc(A["adj_hi"], 1)

            def xn_hi(g):
                act.wait_ge(A["xn"], g.n + 1)
                reached(act, A["agg"], g.n - 1)
                nc.scalar.activation(A_XH[g.parity], A_XN[g.parity], ACT.Copy).then_inc(A["xn_hi"], 1)

            def agg_hi(g):
                act.wait_ge(A["agg"], g.n + 1)
                reached(act, A["h"], g.tile(-4))
                nc.scalar.activation(A_GH[g.parity], PS[:, 1, :], ACT.Copy).then_inc(A["agg_hi"], 1)

            def a_body(g):
                for t in range(PER):
                    if g.live():
                        n = g.tile(t)
                        act.wait_ge(A["h"], n + 1)
                        reached(act, A["rs"], n - 1)
                        reached(act, A["sq"], n - 1)
                        nc.scalar.activation(A_JUNK[t % 2], PS[:, 2 + t % 2, :], ACT.Square, scale=UNSCALE * HID ** -0.5,
                                             accum_out=A_SS[t % 2]).then_inc(A["sq"], 1)
                    if t == 0 and g.plus(1).live():
                        adj_hi(g.plus(1))
                    g1, t1 = behind(g, t, 1)
                    g2, t2 = behind(g, t, 2)
                    if g2.live():
                        n = g2.tile(t2)
                        act.wait_ge(A["hT"], n + 1)
                        reached(act, A["y"], n - 1)
                        nc.scalar.activation(A_HH[t2 % 2], PS[:, 4 + t2 % 2, :].rearrange("p (a b) -> p a b", b=P), ACT.Copy).then_inc(A["hT_hi"], 1)
                    if t == 0 and g.plus(1).live():
                        xn_hi(g.plus(1))
                    if t == 1 and g.plus(-1).live():
                        piece(g.plus(-1))
                    if g1.live():
                        n = g1.tile(t1)
                        act.wait_ge(A["norm"], n + 1)
                        nc.scalar.activation(A_H[t1], A_H[t1], ACT.Silu).then_inc(A["silu"], 1)
                    if t == 2 and g.plus(1).live():
                        agg_hi(g.plus(1))
                if isinstance(g.n, int) and g.n == GROUPS - 1:
                    late_hi()

            adj_hi(Group(0, 0))
            xn_hi(Group(0, 0))
            near_hi()
            agg_hi(Group(0, 0))
            over_groups(act, a_body, 2, 1)

            def b_x_hi(g):
                act.wait_ge(B["xT"], g.n + 1)
                reached(act, B["h"], g.n * CH)
                nc.scalar.activation(B_XH, PS[:, 4, :], ACT.Copy).then_inc(B["xT_hi"], 1)

            def b_gelu(g, c):
                act.wait_ge(B["h"], g.n * CH + c + 1)
                reached(act, B["h_lo"], g.n * CH - CH + c + 1)
                nc.scalar.activation(B_H[:, c], PS[:, 5 + c % 2, :], ACT.Gelu, bias=FB1[:, c:c + 1], scale=UNSCALE).then_inc(B["gelu"], 1)
                act.wait_ge(B["gelu"], g.n * CH + c + 1)
                reached(act, B["y"], g.tile(-PER))
                nc.scalar.activation(B_HH[g.parity][:, c], B_H[:, c], ACT.Copy).then_inc(B["h_hi"], 1)

            def b_tanh(g):
                act.wait_ge(B["lz"], g.n + 1)
                nc.scalar.activation(TANH_Z, LOGIT_Z, ACT.Tanh, scale=0.5).then_inc(B["tanh"], 1)

            def c_x_hi(g):
                act.wait_ge(C["xT"], g.n + 1)
                reached(act, C["h"], g.n)
                nc.scalar.activation(C_XH, PS[:, 4, :], ACT.Copy).then_inc(C["xT_hi"], 1)

            def c_h_hi(g):
                act.wait_ge(C["h"], g.n + 1)
                act.wait_ge(C["scale"], g.n + 1)
                reached(act, C["y"], g.n)
                for t in range(PER):
                    nc.scalar.activation(C_HH[:, t], PS[:, 7, t * D:(t + 1) * D], ACT.Copy, scale=C_SCALE[:, t:t + 1]).then_inc(C["h_hi"], 1)

            def e_x_hi(g):
                act.wait_ge(E["xn"], g.n + 1)
                nc.scalar.activation(XN3[:, bass.ds(g.n * PER, PER), :], E_XN, ACT.Copy).then_inc(E["kept"], 1)
                act.wait_ge(E["xT"], g.n + 1)
                nc.scalar.activation(ADJH[:, bass.ds(g.n * PER, PER), :], PS[:, 7, :].rearrange("p (a b) -> p a b", b=P), ACT.Copy).then_inc(E["xT_hi"], 1)

            def bc_body(g):
                up, dn, dd = g.plus(1), g.plus(-1), g.plus(-2)
                if dd.live():
                    c_h_hi(dd)
                if g.live():
                    b_tanh(g)
                if up.live():
                    b_x_hi(up)
                    b_gelu(up, 0)
                    b_gelu(up, 1)
                    b_gelu(up, 2)
                    b_gelu(up, 3)
                if dn.live():
                    c_x_hi(dn)
                if dd.live():
                    e_x_hi(dd)

            b_x_hi(Group(0, 0))
            late_rows_hi()
            act.wait_ge(A["x1"], GROUPS)
            act.wait_ge(prep_done, 4)
            for c in range(CH):
                b_gelu(Group(0, 0), c)
            over_groups(act, bc_body, 3, 2)

            for n, (dst, src) in enumerate(((R_E, R_Z), (R_E2, R_Z2), (R_EGAP, R_GAP))):
                act.wait_ge(R["z"], n + 1)
                nc.scalar.activation(dst, src, ACT.Exp).then_inc(R["exp"], 1)

            act.wait_ge(R["go"], 1)

            def d_body(g):
                if g.live():
                    experts = experts_of(g, 2, mybir.EngineType.Activation)
                for t in range(PER):
                    if g.live():
                        fetch_expert(act, g, t, 2, experts[t])
                    g2, t2 = behind(g, t, 2)
                    if g2.live():
                        n = g2.tile(t2)
                        act.wait_ge(DD["h"], n + 1)
                        reached(act, DD["lo_pool"], n - 1)
                        reached(act, DD["lo_dve"], n - 1)
                        nc.scalar.activation(D_G[t2 % 2], PS[:, t2 % 2, :], ACT.Gelu, scale=UNSCALE)
                        reached(act, DD["y"], n - 3)
                        nc.scalar.activation(D_GH[t2].rearrange("p a b c -> p (a b c)"), PS[:, t2 % 2, :], ACT.Gelu, scale=UNSCALE).then_inc(DD["hi"], 1)

            over_groups(act, d_body, 2, 1)

        @block.vector
        def _(dve):
            def split_rows(dst, staged, masked):
                return nc.vector.scalar_tensor_tensor(dst, staged, SCALE, masked, ALU.mult, ALU.subtract)

            def near_lo():
                dve.wait_ge(w_near, NEAR)
                nc.vector.tensor_scalar(EPSI, IDENT[:], EPSC[:, 0:1], None, ALU.mult)
                nc.vector.tensor_scalar(RMSW[:], RMSW[:], UNSCALE, None, ALU.mult)
                dve.drain()
                nc.vector.tensor_copy(EPSH[:], EPSI)
                dve.drain()
                nc.vector.tensor_tensor(EPSL[:], EPSI, EPSH[:], ALU.subtract).then_inc(prep_done, 1)
                dve.wait_ge(prep_hi, 1)
                split_rows(BROW[:, 0:ROWS_A], S_ROWA, M_ROWA)
                for n, (dst, src) in enumerate(((GW1, S_GW1), (GW2, S_GW2))):
                    dve.wait_ge(prep_hi, n + 2)
                    nc.vector.scalar_tensor_tensor(dst[1][:], src, SCALE, dst[0][:], ALU.mult, ALU.subtract).then_inc(prep_done, 1)

            def late_lo():
                dve.wait_ge(prep_hi, 4)
                nc.vector.scalar_tensor_tensor(FW1[1][:], S_FW1, SCALE, FW1[0][:], ALU.mult, ALU.subtract)
                dve.wait_ge(prep_hi, 5)
                nc.vector.scalar_tensor_tensor(WG[1], S_WG, SCALE, WG[0], ALU.mult, ALU.subtract)
                dve.wait_ge(transposed, 1)
                nc.vector.tensor_copy(FB1[:], PS[:, 0, D:D + CH]).then_inc(prep_done, 1)

            def late_rows_lo():
                dve.wait_ge(prep_hi, 6)
                split_rows(BROW[:, ROWS_A:], S_ROWB, M_ROWB)
                dve.wait_ge(prep_hi, 7)
                rows = slice(LO_ROW, LO_ROW + EXPERTS)
                nc.vector.scalar_tensor_tensor(EBIAS[rows, :], S_EB[rows, :], SCALE, EBIAS[rows, :], ALU.mult, ALU.subtract)
                nc.vector.tensor_scalar(NWT[0][:], PS[:, 0, 0:D], SCALE, None, ALU.mult)
                dve.drain()
                nc.vector.scalar_tensor_tensor(NWT[1][:], PS[:, 0, 0:D], SCALE, NWT[0][:], ALU.mult, ALU.subtract).then_inc(prep_done, 1)

            def statistics(tiles, st, mv, ve, s_mv, s_ve, at):
                for t in range(PER):
                    nc.vector.bn_stats(st[:, t], tiles(t))
                dve.drain()
                for t in range(PER):
                    last = nc.vector.bn_aggr(mv[:, t], st[:, t])
                last.then_inc(s_mv, 1)
                dve.wait_ge(s_mv, at)
                nc.vector.tensor_scalar(ve, mv[:, :, 1], LN_EPS, None, ALU.add).then_inc(s_ve, 1)

            def normalise(dst, tiles, mv, rs, s_out):
                for t in range(PER):
                    last = nc.vector.tensor_scalar(dst(t), tiles(t), mv[:, t, 0:1], rs[:, t:t + 1], ALU.subtract, ALU.mult)
                last.then_inc(s_out, 1)

            def x_tile(g):
                return lambda t: X[:, bass.ds(g.n * PER + t, 1), :].rearrange("p a b -> p (a b)")

            def ln_stats(g, k, sems):
                statistics(x_tile(g), NORM[k]["st"], NORM[k]["mv"], NORM[k]["ve"], sems["mv"], sems["veps"], g.n + 1)

            def b_xn(g):
                dve.wait_ge(B["rstd"], g.n + 1)
                reached(dve, B["xT"], g.n)
                normalise(lambda t: B_XN[:, t], x_tile(g), NORM["B"]["mv"], NORM["B"]["rs"], B["xn"])

            def a_stats(g):
                dve.wait_ge(load[g.parity], g.half * 48 + 48)
                statistics(x_tile(g), A_STATS[g.parity], A_MV[g.parity], A_VE[g.parity], A["mv"], A["veps"], g.n + 1)

            def a_xn(g):
                j = g.parity
                dve.wait_ge(A["rstd"], g.n + 1)
                reached(dve, A["xn_hi"], g.n - 1)
                reached(dve, A["xn_lo"], g.n - 1)
                normalise(lambda t: A_XN[j][:, t], x_tile(g), A_MV[j], A_RSTD[j], A["xn"])

            def a_deg(g):
                dve.wait_ge(A["offd"], g.n + 1)
                nc.vector.tensor_reduce(DEG[:, bass.ds(g.n * PER, PER)], A_OFF, AX.X, ALU.add).then_inc(A["deg"], 1)

            def a_adjlo(g):
                dve.wait_ge(A["adj_hi"], g.n + 1)
                s = bass.ds(g.n * PER, PER)
                nc.vector.tensor_tensor(ADJL[:, s, :], PS[:, 0, :].rearrange("p (a b) -> p a b", b=P), ADJH[:, s, :], ALU.subtract).then_inc(A["adj_lo"], 1)

            def a_agglo(g):
                dve.wait_ge(A["agg_hi"], g.n + 1)
                reached(dve, A["h"], g.tile(-4))
                nc.vector.tensor_tensor(A_GL[g.parity], PS[:, 1, :], A_GH[g.parity], ALU.subtract).then_inc(A["agg_lo"], 1)

            def a_body(g):
                up = g.plus(1)
                for t in range(PER):
                    g1, t1 = behind(g, t, 1)
                    g2, t2 = behind(g, t, 2)
                    if t == 0 and up.live():
                        a_xn(up)
                    if g1.live():
                        n = g1.tile(t1)
                        dve.wait_ge(A["rs"], n + 1)
                        reached(dve, A["hT"], n - 3)
                        nc.vector.scalar_tensor_tensor(A_H[t1], PS[:, 2 + t1 % 2, :], A_RS[t1 % 2][:, 0:1], RMSW[:],
                                                       ALU.mult, ALU.mult).then_inc(A["norm"], 1)
                    if t == 2 and g.plus(2).live():
                        a_stats(g.plus(2))
                    if g.live():
                        dve.wait_ge(A["sq"], g.tile(t) + 1)
                        nc.vector.tensor_scalar(A_SE[t % 2], A_SS[t % 2], RMS_EPS, None, ALU.add).then_inc(A["seps"], 1)
                    if t == 3 and up.live():
                        a_agglo(up)
                    if t == 1 and up.live():
                        a_adjlo(up)
                    if g2.live():
                        n = g2.tile(t2)
                        dve.wait_ge(A["hT_hi"], n + 1)
                        reached(dve, A["y"], n - 1)
                        nc.vector.tensor_tensor(A_HL[t2 % 2], PS[:, 4 + t2 % 2, :].rearrange("p (a b) -> p a b", b=P), A_HH[t2 % 2], ALU.subtract).then_inc(A["hT_lo"], 1)
                    if t == 1 and up.live():
                        a_deg(up)
                    if t == 3 and g.plus(-1).live():
                        a_out(g.plus(-1))
                    if isinstance(g.n, int) and g.n == GROUPS and t == 0:
                        dve.wait_ge(A["agg"], GROUPS)
                        dve.wait_ge(A["x1"], 1)
                        ln_stats(g0, "B", B)
                    if isinstance(g.n, int) and g.n == GROUPS and t == 2:
                        b_xn(g0)
                if isinstance(g.n, int) and g.n == GROUPS - 1:
                    late_lo()

            def a_out(g):
                dve.wait_ge(A["y"], g.tile(PER))
                s = bass.ds(g.n * PER, PER)
                nc.vector.scalar_tensor_tensor(X[:, s, :], PS[:, 6 + g.parity, :].rearrange("p (a b) -> p a b", b=D), UNSCALE, X[:, s, :],
                                               ALU.mult, ALU.add).then_inc(A["x1"], 1)

            g0 = Group(0, 0)
            a_stats(g0)
            dve.wait_ge(const_done, 1)
            nc.vector.tensor_scalar(ROWSCALE[:], IDENT[0:2, 1:2], SCALE, None, ALU.mult).then_inc(row_scale, 1)
            a_adjlo(g0)
            a_xn(g0)
            a_deg(g0)
            near_lo()
            a_stats(g0.plus(1))
            a_agglo(g0)
            over_groups(dve, a_body, 2, 1)

            def b_xlo(g):
                dve.wait_ge(B["xT_hi"], g.n + 1)
                reached(dve, B["h"], g.n * CH)
                nc.vector.tensor_tensor(B_XL, PS[:, 4, :], B_XH, ALU.subtract).then_inc(B["xT_lo"], 1)

            def b_hlo(g, c):
                dve.wait_ge(B["h_hi"], g.n * CH + c + 1)
                nc.vector.tensor_tensor(B_HL[g.parity][:, c], B_H[:, c], B_HH[g.parity][:, c], ALU.subtract).then_inc(B["h_lo"], 1)

            def b_gate(g):
                step = [0]
                STEPS = 10

                def done(ins):
                    step[0] += 1
                    ins.then_inc(B["step"], 1)
                    dve.wait_ge(B["step"], g.n * STEPS + step[0])

                wide = [P, PER, EXPERTS]
                dve.wait_ge(B["logits"], g.n + 1)
                parts = PS[:, 4, 0:PER * 2 * EXPERTS].rearrange("p (a i b) -> p a i b", i=2, b=EXPERTS)
                done(nc.vector.scalar_tensor_tensor(LOGIT, parts[:, :, 0], UNSCALE,
                                                    BGB[:, :].unsqueeze(1).broadcast_to(wide), ALU.mult, ALU.add))
                nc.vector.scalar_tensor_tensor(LOGIT, parts[:, :, 1], UNSCALE, LOGIT, ALU.mult, ALU.add).then_inc(B["lg"], 1)
                dve.wait_ge(B["lg"], g.n + 1)
                done(nc.vector.tensor_reduce(LOGIT_MAX[:, :, 0], LOGIT, AX.X, ALU.max))
                nc.vector.tensor_tensor(LOGIT_Z, LOGIT, LOGIT_MAX.broadcast_to(wide), ALU.subtract).then_inc(B["lz"], 1)
                dve.wait_ge(B["lz"], g.n + 1)
                done(nc.vector.scalar_tensor_tensor(ONEHOT, LOGIT_Z, 0.0, RIOTA[:, :].unsqueeze(1).broadcast_to(wide), ALU.is_ge, ALU.mult))
                done(nc.vector.tensor_reduce(FIRST[:, :, 0], ONEHOT, AX.X, ALU.max))
                done(nc.vector.tensor_tensor(ONEHOT, ONEHOT, FIRST.broadcast_to(wide), ALU.is_equal))
                dve.wait_ge(B["tanh"], g.n + 1)
                nc.vector.tensor_scalar(EXP_TOP, TANH_Z, 1.0, None, ALU.add)
                done(nc.vector.tensor_scalar(EXP_BOTTOM, TANH_Z, -1.0, 1.0, ALU.mult, ALU.add))
                done(nc.vector.reciprocal(EXP_Z, EXP_BOTTOM))
                done(nc.vector.tensor_tensor(EXP_Z, EXP_Z, EXP_TOP, ALU.mult))
                done(nc.vector.tensor_reduce(EXP_SUM[:, :, 0], EXP_Z, AX.X, ALU.add))
                done(nc.vector.reciprocal(PROB, EXP_SUM))
                nc.vector.scalar_tensor_tensor(GATE[g.parity], ONEHOT, UNSCALE, PROB.broadcast_to(wide), ALU.mult, ALU.mult).then_inc(B["gate"], 1)
                assert step[0] == STEPS

            def b_combine(g, t):
                n = g.tile(t)
                dve.wait_ge(B["y"], n + 1)
                dve.wait_ge(B["gate"], g.n + 1)
                for e in range(EXPERTS):
                    y = PS[:, 2 * (t % 2) + e // 4, (e % 4) * D:(e % 4 + 1) * D]
                    gate, sum_e = GATE[g.parity][:, t, e:e + 1], ACC[t % 2][:, e % 2]
                    if e >= 2:
                        dve.wait_ge(B["acc"], n * EXPERTS + e - 1)
                    if e == 1:
                        ins = nc.vector.tensor_scalar(sum_e, y, gate, None, ALU.mult)
                    else:
                        ins = nc.vector.scalar_tensor_tensor(sum_e, y, gate, x_tile(g)(t) if e == 0 else sum_e, ALU.mult, ALU.add)
                    ins.then_inc(B["acc"], 1)
                dve.wait_ge(B["acc"], n * EXPERTS + EXPERTS)
                nc.vector.tensor_tensor(x_tile(g)(t), ACC[t % 2][:, 0], ACC[t % 2][:, 1], ALU.add).then_inc(B["comb"], 1)

            def c_xn(g):
                dve.wait_ge(C["rstd"], g.n + 1)
                reached(dve, C["xT"], g.n)
                reached(dve, E["xT"], g.n - 1)
                normalise(lambda t: C_XN[:, t], x_tile(g), NORM["C"]["mv"], NORM["C"]["rs"], C["xn"])

            def c_xlo(g):
                dve.wait_ge(C["xT_hi"], g.n + 1)
                reached(dve, C["h"], g.n)
                nc.vector.tensor_tensor(C_XL, PS[:, 4, :], C_XH, ALU.subtract).then_inc(C["xT_lo"], 1)

            def c_scale(g):
                dve.wait_ge(A["dis"], GROUPS)
                reached(dve, C["h_hi"], g.n * PER)
                reached(dve, C["h_lo"], g.n)
                nc.vector.tensor_scalar(C_SCALE, DIS[:, bass.ds(g.n * PER, PER)], UNSCALE, None, ALU.mult).then_inc(C["scale"], 1)

            def c_hlo(g):
                dve.wait_ge(C["h_hi"], g.n * PER + PER)
                dve.wait_ge(C["scale"], g.n + 1)
                reached(dve, C["y"], g.n)
                for t in range(PER):
                    last = nc.vector.scalar_tensor_tensor(C_HL[:, t], PS[:, 7, t * D:(t + 1) * D], C_SCALE[:, t:t + 1], C_HH[:, t], ALU.mult, ALU.subtract)
                last.then_inc(C["h_lo"], 1)

            def c_out(g):
                dve.wait_ge(C["y"], g.n + 1)
                for t in range(PER):
                    xt = x_tile(g)(t)
                    last = nc.vector.scalar_tensor_tensor(xt, PS[:, 7, t * D:(t + 1) * D], DIS[:, bass.ds(g.n * PER + t, 1)], xt, ALU.mult, ALU.add)
                last.then_inc(C["x3"], 1)

            def e_xn(g):
                dve.wait_ge(E["rstd"], g.n + 1)
                reached(dve, E["xT"], g.n)
                reached(dve, E["kept"], g.n)
                normalise(lambda t: E_XN[:, t], x_tile(g), NORM["E"]["mv"], NORM["E"]["rs"], E["xn"])

            def e_xlo(g):
                dve.wait_ge(E["xT_hi"], g.n + 1)
                s = bass.ds(g.n * PER, PER)
                nc.vector.tensor_tensor(ADJL[:, s, :], PS[:, 7, :].rearrange("p (a b) -> p a b", b=P), ADJH[:, s, :], ALU.subtract)
                nc.vector.tensor_reduce(MEANT[:, bass.ds(g.n * 2 * PER, 2 * PER)], PS[:, 7, :].rearrange("p (a b) -> p a b", b=NODES), AX.X, ALU.add).then_inc(E["xT_lo"], 1)

            def bc_body(g):
                up, dn, dd = g.plus(1), g.plus(-1), g.plus(-2)
                if up.live():
                    ln_stats(up, "B", B)
                if dn.live():
                    b_combine(dn, 3)
                if dd.live():
                    c_hlo(dd)
                if up.live():
                    b_xn(up)
                if g.live():
                    b_gate(g)
                if g.live():
                    b_combine(g, 0)
                if up.live():
                    b_xlo(up)
                if dn.live():
                    dve.wait_ge(B["comb"], dn.tile(PER))
                    c_scale(dn)
                    ln_stats(dn, "C", C)
                if dd.live():
                    c_out(dd)
                if dd.live():
                    dve.drain()
                    ln_stats(dd, "E", E)
                if g.live():
                    b_combine(g, 1)
                if dn.live():
                    c_xn(dn)
                if up.live():
                    b_hlo(up, 0)
                    b_hlo(up, 1)
                if dd.live():
                    e_xn(dd)
                if g.live():
                    b_combine(g, 2)
                if up.live():
                    b_hlo(up, 2)
                    b_hlo(up, 3)
                if dn.live():
                    c_xlo(dn)
                if dd.live():
                    e_xlo(dd)

            b_xlo(g0)
            late_rows_lo()
            for c in range(CH):
                b_hlo(g0, c)
            over_groups(dve, bc_body, 3, 2)

            made = [0]

            def then(ins):
                made[0] += 1
                ins.then_inc(R["step"], 1)
                dve.wait_ge(R["step"], made[0])

            def softmax(src, z, e, out, n, one):
                then(nc.vector.tensor_reduce(one[0], src, AX.X, ALU.max))
                nc.vector.tensor_scalar(z, src, one[0], None, ALU.subtract).then_inc(R["z"], 1)
                dve.wait_ge(R["exp"], n)
                then(nc.vector.tensor_reduce(one[1], e, AX.X, ALU.add))
                then(nc.vector.reciprocal(one[2], one[1]))
                then(nc.vector.tensor_scalar(out, e, one[2], None, ALU.mult))

            nc.vector.memset(R_ONEHOT, 0.0)
            dve.wait_ge(R["logits"], 1)
            then(nc.vector.scalar_tensor_tensor(R_LOGIT, PS[:, 0, 0:EXPERTS], 1.0 / NODES, BR[:], ALU.mult, ALU.add))
            softmax(R_LOGIT, R_Z, R_E, R_WEIGHT, 1, (R_MAX, R_SUM, R_INV))
            nc.vector.tensor_copy(R_SCALED, R_WEIGHT).then_inc(R["weights"], 1)
            dve.wait_ge(R["loads"], 1)
            then(nc.vector.tensor_scalar(R_LOAD, PS[:, 1, 0:EXPERTS], float(TOKENS // GRAPHS), None, ALU.mult))
            then(nc.vector.reciprocal(R_FACTOR, R_LOAD))
            then(nc.vector.tensor_scalar(R_FACTOR, R_FACTOR, CAPACITY, 1.0, ALU.mult, ALU.min))
            then(nc.vector.tensor_tensor(R_SCALED, R_WEIGHT, R_FACTOR, ALU.mult))
            softmax(R_SCALED, R_Z2, R_E2, R_FINAL, 2, (R_MAX, R_SUM, R_INV))
            then(nc.vector.max(R_TOP, R_FINAL))
            then(nc.vector.max_index(R_TOPI, R_TOP, R_FINAL))
            nc.vector.tensor_tensor(R_GAP, R_TOP[:, 1:2], R_TOP[:, 0:1], ALU.subtract).then_inc(R["z"], 1)
            then(nc.vector.tensor_copy(R_NUMBERS[:, 0:2], R_TOPI[:, 0:2]))
            for q in range(TOPK):
                nc.vector.tensor_scalar(R_DIAG[:, q], IDENT[:], R_NUMBERS[:, q:q + 1], None, ALU.mult)
                for at in (0, LO_ROW):
                    last = nc.vector.tensor_scalar(R_ONEHOT[:, q, at:at + EXPERTS], RIOTA[:], R_NUMBERS[:, q:q + 1], float(EXPERTS), ALU.add, ALU.is_equal)
            last.then_inc(R["diagonal"], 1)
            dve.wait_ge(R["exp"], 3)
            then(nc.vector.tensor_scalar(R_DEN, R_EGAP, 1.0, None, ALU.add))
            then(nc.vector.reciprocal(R_FIRST, R_DEN))
            then(nc.vector.tensor_tensor(R_SECOND, R_EGAP, R_FIRST, ALU.mult))
            nc.vector.tensor_scalar(R_NUMBERS[:, 2:3], R_FIRST, UNSCALE, None, ALU.mult)
            then(nc.vector.tensor_scalar(R_NUMBERS[:, 3:4], R_SECOND, UNSCALE, None, ALU.mult))
            for q in range(TOPK, 2 * TOPK):
                last = nc.vector.tensor_scalar(R_DIAG[:, q], IDENT[:], R_NUMBERS[:, q:q + 1], None, ALU.mult)
            last.then_inc(R["diagonal"], 1)
            dve.wait_ge(R["rows"], 1)
            nc.vector.tensor_scalar(IDX[:].rearrange("p (b q) t -> p t b q", q=TOPK), PS[:, 2, 0:TOPK * P].rearrange("p (q t b) -> p t b q", q=TOPK, b=2), 0.0, float(EXPERTS - 1), ALU.max, ALU.min)
            nc.vector.tensor_copy(CHOSEN[:].rearrange("p t (b q) -> p t b q", q=TOPK),
                                  PS[:, 3, 0:TOPK * P].rearrange("p (q t b) -> p t b q", q=TOPK, b=2)).then_inc(R["go"], 1)
            dve.wait_ge(R["rows"], 2)
            then(nc.vector.tensor_copy(WTOP[:].rearrange("p t (b q) -> p t b q", q=TOPK), PS[:, 6, 0:TOPK * P].rearrange("p (q t b) -> p t b q", q=TOPK, b=2)))

            dve.wait_ge(R["go"], 1)

            def d_out(g):
                j = g.parity
                dve.wait_ge(DD["yT"], g.tile(PER))
                reached(dve, DD["norm"], g.n)
                s = bass.ds(g.n * PER, PER)
                nc.vector.tensor_tensor(D_RES, PS[:, 4 + j, :].rearrange("p (a b) -> p a b", b=D), XN3[:, s, :], ALU.add).then_inc(DD["r"], 1)
                dve.wait_ge(DD["r"], g.n + 1)
                statistics(lambda t: D_RES[:, t], NORM["D"]["st"], NORM["D"]["mv"], NORM["D"]["ve"], DD["mv"], DD["veps"], g.n + 1)

            def d_norm(g):
                j = g.parity
                dve.wait_ge(DD["rstd"], g.n + 1)
                reached(dve, DD["out"], g.n - 1)
                normalise(lambda t: D_NORM[j][:, t], lambda t: D_RES[:, t], NORM["D"]["mv"], NORM["D"]["rs"], DD["norm"])

            def d_body(g):
                if g.live():
                    experts = experts_of(g, 3, mybir.EngineType.DVE)
                for t in range(PER):
                    g2, t2 = behind(g, t, 2)
                    g4, t4 = behind(g, t, 4)
                    if g.live():
                        n = g.tile(t)
                        reached(dve, DD["y"], n - 3)
                        nc.vector.tensor_copy(SLOT[t][:, 3], expert_weights(experts[t])).then_inc(DD["copied"], 1)
                    if g4.live():
                        n = g4.tile(t4)
                        dve.wait_ge(DD["y"], n + 1)
                        w = WTOP[:, bass.ds(n, 1), :].rearrange("p a b -> p (a b)").unsqueeze(2).broadcast_to([P, 2 * TOPK, NODES])
                        nc.vector.tensor_tensor(D_WEIGHTED[t4 % 2].rearrange("p b e n -> p (b e) n"), PS[:, 2 + t4 % 2, 0:2 * TOPK * NODES].rearrange("p (a n) -> p a n", n=NODES), w, ALU.mult).then_inc(DD["yw"], 1)
                        dve.wait_ge(DD["yw"], n + 1)
                        reached(dve, DD["yT"], n - 1)
                        nc.vector.tensor_tensor(D_SUM[t4 % 2], D_WEIGHTED[t4 % 2][:, :, 0], D_WEIGHTED[t4 % 2][:, :, 1], ALU.add).then_inc(DD["ys"], 1)
                    if g2.live():
                        n = g2.tile(t2)
                        dve.wait_ge(DD["hi"], n + 1)
                        reached(dve, DD["y"], n - 3)
                        nc.vector.tensor_tensor(D_GL[t2].rearrange("p a b c -> p (a b c)")[:, 0:LO_DVE], D_G[t2 % 2][:, 0:LO_DVE],
                                                D_GH[t2].rearrange("p a b c -> p (a b c)")[:, 0:LO_DVE], ALU.subtract).then_inc(DD["lo_dve"], 1)
                    if t == 2 and g.plus(-2).live():
                        d_out(g.plus(-2))
                    if t == 0 and g.plus(-3).live():
                        d_norm(g.plus(-3))

            over_groups(dve, d_body, 6, 3)

        @block.tensor
        def _(pe):
            pe.wait_ge(const_done, 1)

            def product(dst, lhs, rhs, start=True, stop=True):
                nc.tensor.matmul(dst, lhs[0], rhs[0], start=start, stop=False)
                nc.tensor.matmul(dst, lhs[0], rhs[1], start=False, stop=False)
                return nc.tensor.matmul(dst, lhs[1], rhs[0], start=False, stop=stop)

            def a_transpose(g):
                pe.wait_ge(load[g.parity], g.half * 48 + 48)
                reached(pe, A["adj_lo"], g.n)
                for t in range(PER):
                    last = nc.tensor.transpose(PS[:, 0, t * P:(t + 1) * P], A_ADJ[g.parity][:, t], IDENT[:])
                last.then_inc(A["adjT"], 1)

            def a_aggregate(g):
                j = g.parity
                pe.wait_ge(A["adj_lo"], g.n + 1)
                pe.wait_ge(A["xn_lo"], g.n + 1)
                reached(pe, A["agg_lo"], g.n)
                for t in range(PER):
                    dst = PS[:, 1, t * P:(t + 1) * P]
                    lhs = (A_XH[j][:, t], A_XL[j][:, t])
                    at = bass.ds(g.n * PER + t, 1)
                    adj = (ADJH[:, at, :].rearrange("p a b -> p (a b)"), ADJL[:, at, :].rearrange("p a b -> p (a b)"))
                    product(dst, lhs, adj, stop=False)
                    last = product(dst, lhs, (EPSH[:], EPSL[:]), start=False)
                last.then_inc(A["agg"], 1)

            def late_transposes():
                pe.wait_ge(w_late, LATE)
                pe.wait_ge(A["adj_lo"], GROUPS)
                nc.tensor.transpose(PS[:, 0, 0:D], S_NW, IDENT[:])
                nc.tensor.transpose(PS[:, 0, D:D + CH], FB1R[:], IDENT[0:CH, 0:CH]).then_inc(transposed, 1)

            def a_body(g):
                up = g.plus(1)
                for t in range(PER):
                    g2, t2 = behind(g, t, 2)
                    g3, t3 = behind(g, t, 3)
                    if t == 2 and up.live():
                        a_aggregate(up)
                    if g.live():
                        n = g.tile(t)
                        if t == 0:
                            pe.wait_ge(A["agg_lo"], g.n + 1)
                            if isinstance(g.n, int) and g.n == GROUPS - 1:
                                late_transposes()
                        reached(pe, A["norm"], n - 1)
                        dst = PS[:, 2 + t % 2, :]
                        s = slice(t * P, (t + 1) * P)
                        nc.tensor.matmul(dst, ONE2[:], brow("gb1", 0, HID), start=True, stop=False)
                        product(dst, (A_GH[g.parity][:, s], A_GL[g.parity][:, s]), (GW1[0][:], GW1[1][:]), start=False).then_inc(A["h"], 1)
                    if t == 0 and up.live():
                        a_transpose(up)
                    if g2.live():
                        n = g2.tile(t2)
                        pe.wait_ge(A["silu"], n + 1)
                        reached(pe, A["hT_lo"], n - 1)
                        for c in range(CH):
                            last = nc.tensor.transpose(PS[:, 4 + t2 % 2, c * P:(c + 1) * P], A_H[t2][:, c * P:(c + 1) * P], IDENT[:])
                        last.then_inc(A["hT"], 1)
                    if g3.live():
                        n = g3.tile(t3)
                        pe.wait_ge(A["hT_lo"], n + 1)
                        if t3 == 0:
                            reached(pe, A["x1"], g3.n - 1)
                        dst = PS[:, 6 + g3.parity, t3 * D:(t3 + 1) * D]
                        nc.tensor.matmul(dst, ONE2[:], brow("gb2", 0, D), start=True, stop=False)
                        for c in range(CH):
                            last = product(dst, (A_HH[t3 % 2][:, c], A_HL[t3 % 2][:, c]), (GW2[0][:, c], GW2[1][:, c]), start=False, stop=(c == CH - 1))
                        last.then_inc(A["y"], 1)

            g0 = Group(0, 0)
            a_transpose(g0)
            pe.wait_ge(prep_done, 1)
            a_aggregate(g0)
            pe.wait_ge(prep_done, 3)
            over_groups(pe, a_body, 2, 1)

            def four_transposes(src, ready, at, out_sem):
                pe.wait_ge(ready, at)
                for t in range(PER):
                    last = nc.tensor.transpose(PS[:, 4, t * P:(t + 1) * P], src[:, t], IDENT[:])
                last.then_inc(out_sem, 1)

            def b_hidden(g, c):
                pe.wait_ge(B["xT_lo"], g.n + 1)
                reached(pe, B["gelu"], g.n * CH + c - 1)
                s = slice(c * P, (c + 1) * P)
                product(PS[:, 5 + c % 2, :], (FW1[0][:, s], FW1[1][:, s]), (B_XH, B_XL)).then_inc(B["h"], 1)

            def b_logits(g):
                pe.wait_ge(B["h_lo"], g.n * CH + CH)
                hh, hl = B_HH[g.parity], B_HL[g.parity]
                for t in range(PER):
                    s = slice(t * P, (t + 1) * P)
                    for c in range(CH):
                        at = t * 2 * EXPERTS
                        nc.tensor.matmul(PS[:, 4, at:at + 2 * EXPERTS], hh[:, c, s], WG2[:, c].rearrange("p a b -> p (a b)"),
                                         start=(t == 0 and c == 0), stop=False)
                        last = nc.tensor.matmul(PS[:, 4, at:at + EXPERTS], hl[:, c, s], WG2[:, c, 0], start=False,
                                                stop=(t == PER - 1 and c == CH - 1))
                last.then_inc(B["logits"], 1)

            def b_experts(g, t):
                n = g.tile(t)
                reached(pe, B["comb"], n - 1)
                hh, hl = B_HH[g.parity], B_HL[g.parity]
                s = slice(t * P, (t + 1) * P)
                y = [PS[:, 2 * (t % 2) + k, :] for k in range(2)]
                for k in range(2):
                    nc.tensor.matmul(y[k], ONE2[:], brow("bd", k * 512, 512), start=True, stop=False)
                for c in range(CH):
                    for lhs, w in ((hh, 0), (hh, 1), (hl, 0)):
                        for k in range(2):
                            last = nc.tensor.matmul(y[k], lhs[:, c, s], WEXP[:, 2 * c + k, w * PIECE:(w + 1) * PIECE], start=False,
                                                    stop=(c == CH - 1 and lhs is hl))
                last.then_inc(B["y"], 1)

            def c_hidden(g):
                pe.wait_ge(C["xT_lo"], g.n + 1)
                reached(pe, C["x3"], g.n)
                for t in range(PER):
                    s = slice(t * P, (t + 1) * P)
                    dst = PS[:, 7, t * D:(t + 1) * D]
                    nc.tensor.matmul(dst, ONE2[:], brow("nb", 0, D), start=True, stop=False)
                    last = product(dst, (C_XH[:, s], C_XL[:, s]), (NWT[0][:], NWT[1][:]), start=False)
                last.then_inc(C["h"], 1)

            def c_neighbours(g):
                pe.wait_ge(C["h_lo"], g.n + 1)
                for t in range(PER):
                    at = bass.ds(g.n * PER + t, 1)
                    adj = (ADJH[:, at, :].rearrange("p a b -> p (a b)"), ADJL[:, at, :].rearrange("p a b -> p (a b)"))
                    last = product(PS[:, 7, t * D:(t + 1) * D], adj, (C_HH[:, t], C_HL[:, t]))
                last.then_inc(C["y"], 1)

            def bc_body(g):
                up, dn, dd = g.plus(1), g.plus(-1), g.plus(-2)
                if g.live():
                    b_experts(g, 0)
                if dd.live():
                    c_neighbours(dd)
                if up.live():
                    if g.live():
                        pe.wait_ge(B["lg"], g.n + 1)
                    four_transposes(B_XN, B["xn"], up.n + 1, B["xT"])
                if g.live():
                    b_experts(g, 1)
                if up.live():
                    b_hidden(up, 0)
                    b_hidden(up, 1)
                if g.live():
                    b_experts(g, 2)
                if up.live():
                    b_hidden(up, 2)
                    b_hidden(up, 3)
                if g.live() and not up.live():
                    pe.wait_ge(B["lg"], g.n + 1)
                if dn.live():
                    four_transposes(C_XN, C["xn"], dn.n + 1, C["xT"])
                if dd.live():
                    pe.wait_ge(E["xn"], dd.n + 1)
                    for t in range(PER):
                        last = nc.tensor.transpose(PS[:, 7, t * P:(t + 1) * P], E_XN[:, t], IDENT[:])
                    last.then_inc(E["xT"], 1)
                if g.live():
                    b_experts(g, 3)
                if dn.live():
                    if dd.live():
                        pe.wait_ge(E["xT_lo"], dd.n + 1)
                    c_hidden(dn)
                if up.live():
                    if dn.live():
                        pe.wait_ge(C["xT_lo"], dn.n + 1)
                    b_logits(up)

            pe.wait_ge(A["hT_lo"], TILES)
            four_transposes(B_XN, B["xn"], 1, B["xT"])
            pe.wait_ge(prep_done, 4)
            pe.wait_ge(A["x1"], GROUPS)
            for c in range(CH):
                b_hidden(g0, c)
            b_logits(g0)
            pe.wait_ge(prep_done, 5)
            pe.wait_ge(piece_lo, PIECES)
            over_groups(pe, bc_body, 3, 2)

            pe.wait_ge(E["xT_lo"], GROUPS)
            nc.tensor.matmul(PS[:, 0, 0:EXPERTS], MEANT[:], WR[:], start=True, stop=True).then_inc(R["logits"], 1)
            pe.wait_ge(R["weights"], 1)
            nc.tensor.matmul(PS[:, 1, 0:EXPERTS], ONES[:], R_WEIGHT, start=True, stop=True).then_inc(R["loads"], 1)
            pe.wait_ge(R["diagonal"], 1)
            for q in range(TOPK):
                nc.tensor.transpose(PS[:, 3, q * P:(q + 1) * P], R_ONEHOT[:, q], IDENT[:])
            nc.tensor.matmul(PS[:, 2, 0:TOPK * P], ONES[:], R_DIAG[:, 0:TOPK].rearrange("p a b -> p (a b)"), start=True, stop=True).then_inc(R["rows"], 1)
            pe.wait_ge(R["diagonal"], 2)
            nc.tensor.matmul(PS[:, 6, 0:TOPK * P], ONES[:], R_DIAG[:, TOPK:].rearrange("p a b -> p (a b)"), start=True, stop=True).then_inc(R["rows"], 1)

            pe.wait_ge(R["go"], 1)

            def biases(dst, n, at, start=True):
                pick = CHOSEN[:, bass.ds(n, 1), :].rearrange("p a b -> p (a b)").unsqueeze(2).broadcast_to([P, 2 * TOPK, NODES])
                nc.tensor.matmul(dst, EBIAS[:, at:at + P], pick, start=start, stop=False)

            def d_hidden(g, t):
                n = g.tile(t)
                reached(pe, DD["hi"], n - 1)
                pe.wait_ge(fetched[t], (g.n + 1) * FETCHED * 16)
                pe.wait_ge(DD["copied"], n + 1)
                at = bass.ds(n, 1)
                for c in range(FCH):
                    biases(PS[:, t % 2, c * 2 * P:(c + 1) * 2 * P], n, c * P, start=(c == 0))
                for k in range(2 * TOPK):
                    graph = slice(k // TOPK * NODES, (k // TOPK + 1) * NODES)
                    x = (ADJH[:, at, graph].rearrange("p a b -> p (a b)"), ADJL[:, at, graph].rearrange("p a b -> p (a b)"))
                    for c in range(FCH):
                        w = [SLOT[t][:, k, i + c * P:i + (c + 1) * P] for i in W1_AT]
                        last = product(PS[:, t % 2, (c * 2 * TOPK + k) * NODES:(c * 2 * TOPK + k + 1) * NODES], w, x, start=False, stop=(k == 2 * TOPK - 1 and c == FCH - 1))
                last.then_inc(DD["h"], 1)

            def d_out_product(g, t):
                n = g.tile(t)
                pe.wait_ge(DD["lo_pool"], n + 1)
                pe.wait_ge(DD["lo_dve"], n + 1)
                reached(pe, DD["yw"], n - 1)
                biases(PS[:, 2 + t % 2, 0:2 * P], n, FF)
                for k in range(2 * TOPK):
                    for c in range(FCH):
                        w = [SLOT[t][:, k, i + c * D:i + (c + 1) * D] for i in W2_AT]
                        last = product(PS[:, 2 + t % 2, k * NODES:(k + 1) * NODES], w, (D_GH[t][:, c, k], D_GL[t][:, c, k]), start=False, stop=(k == 2 * TOPK - 1 and c == FCH - 1))
                last.then_inc(DD["y"], 1)

            def d_body(g):
                for t in range(PER):
                    g2, t2 = behind(g, t, 2)
                    g4, t4 = behind(g, t, 4)
                    if g2.live():
                        d_out_product(g2, t2)
                    if g.live():
                        d_hidden(g, t)
                    if g4.live():
                        n = g4.tile(t4)
                        pe.wait_ge(DD["ys"], n + 1)
                        if t4 == 0:
                            reached(pe, DD["r"], g4.n - 1)
                        nc.tensor.transpose(PS[:, 4 + g4.parity, t4 * D:(t4 + 1) * D], D_SUM[t4 % 2].rearrange("p a b -> p (a b)"), IDENT[:]).then_inc(DD["yT"], 1)

            over_groups(pe, d_body, 4, 2)


NAMES = ["x", "adj", "L0_gnn_epsilon", "L0_gnn_W1", "L0_gnn_b1", "L0_gnn_rms_weight", "L0_gnn_W2", "L0_gnn_b2",
         "L0_ffn_W1", "L0_ffn_b1", "L0_ffn_Wg", "L0_ffn_bg", "L0_ffn_Wd", "L0_ffn_bd", "L1_gnn_W", "L1_gnn_b",
         "L1_ffn_Wr", "L1_ffn_br", "L1_ffn_W1", "L1_ffn_b1", "L1_ffn_W2", "L1_ffn_b2", "L1_ffn_gamma", "L1_ffn_beta"]


def kernel(**inputs):
    import numpy as np
    import concourse.bacc as bacc
    from concourse.bass_utils import run_bass_kernel_spmd

    nc = bacc.Bacc("TRN2", target_bir_lowering=False, num_devices=1)
    arrays, args = {}, []
    for name in NAMES:
        a = np.ascontiguousarray(inputs[name])
        arrays[name] = a
        args.append(nc.dram_tensor(name, a.shape, mybir.dt.from_np(a.dtype), kind="ExternalInput").ap())
    out = nc.dram_tensor("out", (GRAPHS, NODES, D), F32, kind="ExternalOutput").ap()
    build(nc, *args, out)
    r = run_bass_kernel_spmd(nc, [arrays], core_ids=[0])
    return r.results[0]["out"]
```
